# Optimizing a Trainium2 kernel written in Bass

```python
import numpy as np
import jax
import jax.numpy as jnp

def _softmax(x, axis=-1):
    return jax.nn.softmax(x, axis=axis)

def _gelu(x):
    return jax.nn.gelu(x, approximate=True)

def _silu(x):
    return jax.nn.silu(x)

def _sigmoid(x):
    return jax.nn.sigmoid(x)

def _layernorm(x, axis=-1, eps=1e-05):
    m = jnp.mean(x, axis=axis, keepdims=True)
    v = jnp.var(x, axis=axis, keepdims=True)
    return (x - m) / jnp.sqrt(v + eps)

def _scatter_add(tgt, idx, src, axis=0):
    return tgt.at[idx].add(src)

def _segment_sum(src, seg, n):
    return jax.ops.segment_sum(src, seg, n)
kernel_name = 'mk_gnn_resnorm_d4_gnn_r32_0a8a3d'

def setup_inputs(seed: int=0):
    np.random.seed(seed)
    _w = jnp.asarray

    def _rec_inputs():
        import jax
        import jax.numpy as jnp
        _gk = jax.random.key(seed)
        x = 7.22e-05 + 1 * jax.random.normal(jax.random.fold_in(_gk, 1), (3125, 256), jnp.float32)
        src = jax.random.randint(jax.random.fold_in(_gk, 2), (50000,), 0, 3125, jnp.int32)
        dst = jax.random.randint(jax.random.fold_in(_gk, 3), (50000,), 0, 3125, jnp.int32)
        _o = jnp.argsort(dst, stable=True)
        src = src[_o]
        dst = dst[_o]
        edge_attr_10 = jax.random.uniform(jax.random.fold_in(_gk, 12), (50000, 10), jnp.float32, 0.0, 1)
        edge_attr_4 = 0.00109026 + 0.999989 * jax.random.normal(jax.random.fold_in(_gk, 13), (50000, 4), jnp.float32)
        return (x, src, dst, edge_attr_10, edge_attr_4)
    x, src, dst, edge_attr_10, edge_attr_4 = _rec_inputs()

    def _L0_gnn_setup():
        import jax, jax.numpy as jnp
        import numpy as np
        import math
        N = 1024
        E = N * 16
        D = 256
        H = 8
        DH = 32
        TD = H * DH
        FFN = 1024
        L = 2
        EPS = 1e-05

        def _layernorm(x, g, b):
            mu = jnp.mean(x, axis=-1, keepdims=True)
            var = jnp.mean(jnp.square(x - mu), axis=-1, keepdims=True)
            return (x - mu) * jax.lax.rsqrt(var + EPS) * g + b
        key = jax.random.key(seed)
        ks = jax.random.split(key, 16)
        w = lambda k, *s: jax.random.normal(k, s, dtype=jnp.float32) * 0.02
        return {'x': jax.random.normal(ks[0], (N, D), dtype=jnp.float32), 'edge_index': jax.random.randint(ks[1], (2, E), 0, N, dtype=jnp.int64).astype(jnp.int32), 'w_in': w(ks[2], D, D), 'b_in': jnp.zeros((D,), jnp.float32), 'ln1_g': jnp.ones((L, D), jnp.float32), 'ln1_b': jnp.zeros((L, D), jnp.float32), 'ln2_g': jnp.ones((L, D), jnp.float32), 'ln2_b': jnp.zeros((L, D), jnp.float32), 'wq': w(ks[3], L, D, TD), 'bq': jnp.zeros((L, TD), jnp.float32), 'wk': w(ks[4], L, D, TD), 'bk': jnp.zeros((L, TD), jnp.float32), 'wv': w(ks[5], L, D, TD), 'bv': jnp.zeros((L, TD), jnp.float32), 'wo': w(ks[6], L, TD, D), 'bo': jnp.zeros((L, D), jnp.float32), 'w1': w(ks[7], L, D, FFN), 'b1': jnp.zeros((L, FFN), jnp.float32), 'w2': w(ks[8], L, FFN, D), 'b2': jnp.zeros((L, D), jnp.float32)}
    _L0_gnn_all = _L0_gnn_setup()
    _L0_gnn_in = {k: v for k, v in _L0_gnn_all.items() if k in ('w_in', 'b_in', 'ln1_g', 'ln1_b', 'ln2_g', 'ln2_b', 'wq', 'bq', 'wk', 'bk', 'wv', 'bv', 'wo', 'bo', 'w1', 'b1', 'w2', 'b2')}
    del _L0_gnn_all

    def _L1_gnn_setup():
        import jax, jax.numpy as jnp
        import numpy as np
        N_NODES = 50000
        N_EDGES = 50000
        IN_DIM, OUT_DIM, N_HEADS = (256, 64, 4)
        EPS = 1e-12
        key = jax.random.key(seed)
        k1, k2, k3, k4, k5 = jax.random.split(key, 5)
        h = jax.random.normal(k1, (N_NODES, IN_DIM), dtype=jnp.float32)
        edge_index = jax.random.randint(k2, (2, N_EDGES), 0, N_NODES, dtype=jnp.int32)
        W = jax.random.normal(k3, (IN_DIM, OUT_DIM), dtype=jnp.float32) * 0.05
        Wl = jax.random.normal(k4, (N_HEADS, OUT_DIM), dtype=jnp.float32) * 0.05
        Wr = jax.random.normal(k5, (N_HEADS, OUT_DIM), dtype=jnp.float32) * 0.05
        b = jnp.zeros((OUT_DIM,), dtype=jnp.float32)
        return {'h': h, 'W': W, 'Wl': Wl, 'Wr': Wr, 'b': b, 'edge_index': edge_index}
    _L1_gnn_all = _L1_gnn_setup()
    _L1_gnn_in = {k: v for k, v in _L1_gnn_all.items() if k in ('W', 'Wl', 'Wr', 'b')}
    del _L1_gnn_all

    def _L2_gnn_setup():
        import jax, jax.numpy as jnp
        import numpy as np
        N_NODES = 3125
        F_DIM = 256
        NNZ = 50000

        def _prelu(x, a):
            return jnp.where(x >= 0, x, a * x)

        def _hconv(x, W, b, src, dst, n):
            xt = x @ W
            ones = jnp.ones(src.shape, xt.dtype)
            D = jax.ops.segment_sum(ones, src, num_segments=n)
            B = jax.ops.segment_sum(ones, dst, num_segments=n)
            Dinv = jnp.where(D > 0, 1.0 / D, 0.0)
            Binv = jnp.where(B > 0, 1.0 / B, 0.0)
            m = jax.ops.segment_sum(xt[src], dst, num_segments=n) * Binv[:, None]
            out = jax.ops.segment_sum(m[dst], src, num_segments=n) * Dinv[:, None]
            return out + b
        key = jax.random.key(seed)
        k0, k1, k2, k3 = jax.random.split(key, 4)
        x = jax.random.normal(k0, (N_NODES, F_DIM), dtype=jnp.float32)
        edge_index = jax.random.randint(k1, (2, NNZ), 0, N_NODES, dtype=jnp.int32)
        scale = (2.0 / F_DIM) ** 0.5
        W1 = jax.random.normal(k2, (F_DIM, F_DIM), dtype=jnp.float32) * scale
        W2 = jax.random.normal(k3, (F_DIM, F_DIM), dtype=jnp.float32) * scale
        b1 = jnp.zeros((F_DIM,), jnp.float32)
        b2 = jnp.zeros((F_DIM,), jnp.float32)
        a = jnp.full((1,), 0.25, jnp.float32)
        return {'x': x, 'edge_index': edge_index, 'W1': W1, 'b1': b1, 'W2': W2, 'b2': b2, 'a': a}
    _L2_gnn_all = _L2_gnn_setup()
    _L2_gnn_in = {k: v for k, v in _L2_gnn_all.items() if k in ('W1', 'b1', 'W2', 'b2', 'a')}
    del _L2_gnn_all

    def _L3_gnn_setup():
        import jax, jax.numpy as jnp
        import numpy as np
        MUL = 64
        N_NODES = 50000
        N_EDGES = 25000
        NUM_NEIGHBORS = 16.0
        SILU_NORM = 1.679177
        key = jax.random.key(seed)
        ks = jax.random.split(key, 9)
        node_in = jax.random.normal(ks[0], (N_NODES, 4 * MUL), dtype=jnp.float32)
        edge_src = jax.random.randint(ks[1], (N_EDGES,), 0, N_NODES)
        edge_dst = jax.random.randint(ks[2], (N_EDGES,), 0, N_NODES)
        edge_attr = jax.random.normal(ks[3], (N_EDGES, 4), dtype=jnp.float32)
        edge_len_emb = jax.random.uniform(ks[4], (N_EDGES, 10), dtype=jnp.float32)
        w_00_0 = jax.random.normal(ks[5], (MUL, MUL), dtype=jnp.float32)
        w_11_0 = jax.random.normal(ks[6], (MUL, MUL), dtype=jnp.float32)
        w_01_1 = jax.random.normal(ks[7], (MUL, MUL), dtype=jnp.float32)
        w_10_1 = jax.random.normal(ks[8], (MUL, MUL), dtype=jnp.float32)
        kf = jax.random.split(jax.random.fold_in(key, 1), 2)
        fc_w1 = jax.random.normal(kf[0], (10, 64), dtype=jnp.float32)
        fc_w2 = jax.random.normal(kf[1], (64, 1), dtype=jnp.float32)
        return {'node_in': node_in, 'edge_attr': edge_attr, 'edge_len_emb': edge_len_emb, 'w_00_0': w_00_0, 'w_11_0': w_11_0, 'w_01_1': w_01_1, 'w_10_1': w_10_1, 'fc_w1': fc_w1, 'fc_w2': fc_w2, 'edge_src': edge_src, 'edge_dst': edge_dst}
    _L3_gnn_all = _L3_gnn_setup()
    _L3_gnn_in = {k: v for k, v in _L3_gnn_all.items() if k in ('w_00_0', 'w_11_0', 'w_01_1', 'w_10_1', 'fc_w1', 'fc_w2')}
    del _L3_gnn_all
    return {'x': x, 'src': src, 'dst': dst, 'edge_attr_10': edge_attr_10, 'edge_attr_4': edge_attr_4, 'L0_gnn_w_in': _L0_gnn_in['w_in'], 'L0_gnn_b_in': _L0_gnn_in['b_in'], 'L0_gnn_ln1_g': _L0_gnn_in['ln1_g'], 'L0_gnn_ln1_b': _L0_gnn_in['ln1_b'], 'L0_gnn_ln2_g': _L0_gnn_in['ln2_g'], 'L0_gnn_ln2_b': _L0_gnn_in['ln2_b'], 'L0_gnn_wq': _L0_gnn_in['wq'], 'L0_gnn_bq': _L0_gnn_in['bq'], 'L0_gnn_wk': _L0_gnn_in['wk'], 'L0_gnn_bk': _L0_gnn_in['bk'], 'L0_gnn_wv': _L0_gnn_in['wv'], 'L0_gnn_bv': _L0_gnn_in['bv'], 'L0_gnn_wo': _L0_gnn_in['wo'], 'L0_gnn_bo': _L0_gnn_in['bo'], 'L0_gnn_w1': _L0_gnn_in['w1'], 'L0_gnn_b1': _L0_gnn_in['b1'], 'L0_gnn_w2': _L0_gnn_in['w2'], 'L0_gnn_b2': _L0_gnn_in['b2'], 'L1_gnn_W': _L1_gnn_in['W'], 'L1_gnn_Wl': _L1_gnn_in['Wl'], 'L1_gnn_Wr': _L1_gnn_in['Wr'], 'L1_gnn_b': _L1_gnn_in['b'], 'L2_gnn_W1': _L2_gnn_in['W1'], 'L2_gnn_b1': _L2_gnn_in['b1'], 'L2_gnn_W2': _L2_gnn_in['W2'], 'L2_gnn_b2': _L2_gnn_in['b2'], 'L2_gnn_a': _L2_gnn_in['a'], 'L3_gnn_w_00_0': _L3_gnn_in['w_00_0'], 'L3_gnn_w_11_0': _L3_gnn_in['w_11_0'], 'L3_gnn_w_01_1': _L3_gnn_in['w_01_1'], 'L3_gnn_w_10_1': _L3_gnn_in['w_10_1'], 'L3_gnn_fc_w1': _L3_gnn_in['fc_w1'], 'L3_gnn_fc_w2': _L3_gnn_in['fc_w2']}

def reference(x, src, dst, edge_attr_10, edge_attr_4, L0_gnn_w_in, L0_gnn_b_in, L0_gnn_ln1_g, L0_gnn_ln1_b, L0_gnn_ln2_g, L0_gnn_ln2_b, L0_gnn_wq, L0_gnn_bq, L0_gnn_wk, L0_gnn_bk, L0_gnn_wv, L0_gnn_bv, L0_gnn_wo, L0_gnn_bo, L0_gnn_w1, L0_gnn_b1, L0_gnn_w2, L0_gnn_b2, L1_gnn_W, L1_gnn_Wl, L1_gnn_Wr, L1_gnn_b, L2_gnn_W1, L2_gnn_b1, L2_gnn_W2, L2_gnn_b2, L2_gnn_a, L3_gnn_w_00_0, L3_gnn_w_11_0, L3_gnn_w_01_1, L3_gnn_w_10_1, L3_gnn_fc_w1, L3_gnn_fc_w2):
    import jax
    import jax.numpy as jnp

    def _L0_gnn_ref(x, edge_index, w_in, b_in, ln1_g, ln1_b, ln2_g, ln2_b, wq, bq, wk, bk, wv, bv, wo, bo, w1, b1, w2, b2):
        import jax, jax.numpy as jnp
        import numpy as np
        import math
        N = 1024
        E = N * 16
        D = 256
        H = 8
        DH = 32
        TD = H * DH
        FFN = 1024
        L = 2
        EPS = 1e-05

        def _layernorm(x, g, b):
            mu = jnp.mean(x, axis=-1, keepdims=True)
            var = jnp.mean(jnp.square(x - mu), axis=-1, keepdims=True)
            return (x - mu) * jax.lax.rsqrt(var + EPS) * g + b
        n = x.shape[0]
        src0, dst0 = (edge_index[0], edge_index[1])
        deg = jax.ops.segment_sum(jnp.ones_like(src0, jnp.float32), dst0, num_segments=n)
        ar = jnp.arange(n, dtype=src0.dtype)
        src = jnp.concatenate([src0, ar])
        dst = jnp.concatenate([dst0, ar])
        h = x @ w_in + b_in
        scale = 1.0 / math.sqrt(DH)
        for l in range(L):
            xn = _layernorm(h, ln1_g[l], ln1_b[l])
            q = (xn @ wq[l] + bq[l]).reshape(n, H, DH)
            k = (xn @ wk[l] + bk[l]).reshape(n, H, DH)
            v = (xn @ wv[l] + bv[l]).reshape(n, H, DH)
            scores = jnp.einsum('ehd,ehd->eh', q[dst], k[src]) * scale
            m = jax.ops.segment_max(scores, dst, num_segments=n)
            ex = jnp.exp(scores - m[dst])
            z = jax.ops.segment_sum(ex, dst, num_segments=n)
            attn = ex / z[dst]
            agg = jax.ops.segment_sum(attn[:, :, None] * v[src], dst, num_segments=n)
            agg = jnp.where((deg > 0)[:, None, None], agg, 0.0)
            h = h + agg.reshape(n, TD) @ wo[l] + bo[l] * jnp.where(deg > 0, 1.0, 1.0)[:, None] * 0 + agg.reshape(n, TD) @ wo[l] * 0
            h = h - agg.reshape(n, TD) @ wo[l]
            h = h + (agg.reshape(n, TD) @ wo[l] + bo[l]) - bo[l] * 0
            xn2 = _layernorm(h, ln2_g[l], ln2_b[l])
            ffn = jax.nn.gelu(xn2 @ w1[l] + b1[l], approximate=False) @ w2[l] + b2[l]
            h = h + ffn
        return h

    def _L1_gnn_ref(h, W, Wl, Wr, b, edge_index):
        import jax, jax.numpy as jnp
        import numpy as np
        N_NODES = 50000
        N_EDGES = 50000
        IN_DIM, OUT_DIM, N_HEADS = (256, 64, 4)
        EPS = 1e-12
        N = h.shape[0]
        H = Wl.shape[0]
        x = h @ W
        el = x @ Wl.T
        er = x @ Wr.T
        src, dst = (edge_index[0], edge_index[1])
        e = el[src] + er[dst]
        e = jnp.exp(jax.nn.leaky_relu(e, negative_slope=0.2))
        rowsum = jax.ops.segment_sum(e, src, num_segments=N)
        w = e / jnp.maximum(rowsum, EPS)[src]
        heads = [jax.ops.segment_sum(w[:, hd:hd + 1] * x[dst], src, num_segments=N) for hd in range(H)]
        out = jnp.stack(heads, axis=1)
        out = jax.nn.elu(out + b)
        return out.reshape(N, H * x.shape[1])

    def _L2_gnn_ref(x, edge_index, W1, b1, W2, b2, a):
        import jax, jax.numpy as jnp
        import numpy as np
        N_NODES = 3125
        F_DIM = 256
        NNZ = 50000

        def _prelu(x, a):
            return jnp.where(x >= 0, x, a * x)

        def _hconv(x, W, b, src, dst, n):
            xt = x @ W
            ones = jnp.ones(src.shape, xt.dtype)
            D = jax.ops.segment_sum(ones, src, num_segments=n)
            B = jax.ops.segment_sum(ones, dst, num_segments=n)
            Dinv = jnp.where(D > 0, 1.0 / D, 0.0)
            Binv = jnp.where(B > 0, 1.0 / B, 0.0)
            m = jax.ops.segment_sum(xt[src], dst, num_segments=n) * Binv[:, None]
            out = jax.ops.segment_sum(m[dst], src, num_segments=n) * Dinv[:, None]
            return out + b
        src, dst = (edge_index[0], edge_index[1])
        n = x.shape[0]
        h = _prelu(_hconv(x, W1, b1, src, dst, n), a)
        h = _hconv(h, W2, b2, src, dst, n) + x
        return _prelu(h, a)

    def _L3_gnn_ref(node_in, edge_attr, edge_len_emb, w_00_0, w_11_0, w_01_1, w_10_1, fc_w1, fc_w2, edge_src, edge_dst):
        import jax, jax.numpy as jnp
        import numpy as np
        MUL = 64
        N_NODES = 50000
        N_EDGES = 25000
        NUM_NEIGHBORS = 16.0
        SILU_NORM = 1.679177
        src = node_in[edge_src]
        s0 = src[:, :MUL]
        s1 = src[:, MUL:].reshape(-1, MUL, 3)
        a0 = edge_attr[:, 0:1]
        a1 = edge_attr[:, 1:4]
        alpha = np.float32(1.0 / np.sqrt(2.0 * MUL))
        inv_sqrt3 = np.float32(1.0 / np.sqrt(3.0))
        out0 = alpha * (jnp.einsum('ei,io->eo', s0 * a0, w_00_0) + inv_sqrt3 * jnp.einsum('eim,em,io->eo', s1, a1, w_11_0))
        out1 = alpha * (jnp.einsum('ei,io,em->eom', s0, w_01_1, a1) + jnp.einsum('eim,io->eom', s1 * a0[:, :, None], w_10_1))
        msg_ang = jnp.concatenate([out0, out1.reshape(-1, 3 * MUL)], axis=1)
        h = jax.nn.silu(edge_len_emb @ fc_w1 / np.float32(np.sqrt(10.0))) * np.float32(SILU_NORM)
        msg_rad = h @ fc_w2 / np.float32(np.sqrt(64.0))
        messages = msg_ang * msg_rad
        agg = jax.ops.segment_sum(messages, edge_dst, num_segments=node_in.shape[0])
        return agg / np.float32(np.sqrt(NUM_NEIGHBORS))
    edge_index = jnp.stack([src, dst])
    x = _layernorm(x + _L0_gnn_ref(x, edge_index, L0_gnn_w_in, L0_gnn_b_in, L0_gnn_ln1_g, L0_gnn_ln1_b, L0_gnn_ln2_g, L0_gnn_ln2_b, L0_gnn_wq, L0_gnn_bq, L0_gnn_wk, L0_gnn_bk, L0_gnn_wv, L0_gnn_bv, L0_gnn_wo, L0_gnn_bo, L0_gnn_w1, L0_gnn_b1, L0_gnn_w2, L0_gnn_b2), axis=-1)
    x = _layernorm(x + _L1_gnn_ref(x, L1_gnn_W, L1_gnn_Wl, L1_gnn_Wr, L1_gnn_b, edge_index), axis=-1)
    x = _layernorm(x + _L2_gnn_ref(x, edge_index, L2_gnn_W1, L2_gnn_b1, L2_gnn_W2, L2_gnn_b2, L2_gnn_a), axis=-1)
    x = _layernorm(x + _L3_gnn_ref(x, edge_attr_4, edge_attr_10, L3_gnn_w_00_0, L3_gnn_w_11_0, L3_gnn_w_01_1, L3_gnn_w_10_1, L3_gnn_fc_w1, L3_gnn_fc_w2, src, dst), axis=-1)
    return x

_drawn_inputs = setup_inputs


def setup_inputs(seed=0):
    import zlib

    import numpy as np

    out = dict(_drawn_inputs(seed))
    spreads = {'L0_gnn_b_in': (0.0, 0.1),
     'L0_gnn_ln1_g': (1.0, 0.6),
     'L0_gnn_ln1_b': (0.0, 0.386),
     'L0_gnn_ln2_g': (1.0, 0.2),
     'L0_gnn_ln2_b': (0.0, 0.365),
     'L0_gnn_bq': (0.0, 0.8),
     'L0_gnn_bk': (0.0, 0.8),
     'L0_gnn_bv': (0.0, 0.1),
     'L0_gnn_bo': (0.0, 0.1),
     'L0_gnn_b1': (0.0, 0.1),
     'L0_gnn_b2': (0.0, 0.1),
     'L1_gnn_b': (0.0, 0.1),
     'L2_gnn_b1': (0.0, 0.1),
     'L2_gnn_b2': (0.0, 0.1)}
    factors = {'L0_gnn_wq': 8.0, 'L0_gnn_wk': 8.0, 'L1_gnn_Wl': 3.982}
    for name, (base, spread) in spreads.items():
        noise = np.random.default_rng([zlib.crc32(name.encode()), seed]).standard_normal(out[name].shape)
        drawn = base * np.exp(spread * noise) if base else spread * noise
        out[name] = jnp.asarray(drawn.astype(out[name].dtype))
    for name, factor in factors.items():
        out[name] = (out[name] * factor).astype(out[name].dtype)
    return out
```

```python
import numpy as np
import concourse.bass as bass
from concourse import mybir

F = mybir.dt.float32
I = mybir.dt.int32
ALU = mybir.AluOpType
ACT = mybir.ActivationFunctionType
AX = mybir.AxisListType.X

NN = 3125
NE = 50000
W = 25
NP = W * 128
C = 391
T = 416
G = T // 4
SB = 26
L = SB * 128
NEG = -1e38
PADKEY = -100000.0
KS = 4


class Queue:

    def __init__(self, nc, eng, name):
        self.eng = eng
        self.sem = nc.alloc_semaphore("done_" + name)
        self.n = 0
        self.seen = {}

    def wait(self, *marks):
        for m in marks:
            if m is None:
                continue
            sem, v = m
            k = id(sem)
            if self.seen.get(k, 0) < v:
                self.eng.wait_ge(sem, v)
                self.seen[k] = v

    def mark(self, ins):
        ins.then_inc(self.sem, 1)
        self.n += 1
        return (self.sem, self.n)


class Slot:

    def __init__(self, nc, name):
        self.sem = nc.alloc_semaphore(name)
        self.n = 0

    def mark(self, ins):
        ins.then_inc(self.sem, 16)
        self.n += 16
        return (self.sem, self.n)


def program(nc, a, out, dbg=None, stop=99):
    v = Queue(nc, nc.vector, "dve")
    s = Queue(nc, nc.scalar, "act")
    p = Queue(nc, nc.tensor, "pe")
    g = Queue(nc, nc.gpsimd, "pool")
    y = Queue(nc, nc.sync, "sp")
    V, S, P, GP, SY = nc.vector, nc.scalar, nc.tensor, nc.gpsimd, nc.sync

    def dram(name, shape, dt=F):
        return nc.dram_tensor(name, shape, dt, kind="Internal").ap()

    top = [0]
    arena = nc.alloc_sbuf_tensor("arena", [128, 52600], F)

    def take(n):
        o = top[0]
        top[0] += (n + 7) // 8 * 8
        assert top[0] <= 52600, top[0]
        return o

    def view(o, *dims):
        n = int(np.prod(dims))
        ap = arena[:, o:o + n]
        if len(dims) == 1:
            return ap
        names = "abcd"[:len(dims)]
        return ap.rearrange("p (%s) -> p %s" % (" ".join(names), " ".join(names)),
                            **{names[i]: dims[i] for i in range(len(dims))})

    o_pa = take(T * 8)
    o_pb = take(T * 2)
    o_misc = take(4 * T + 1280)
    o_B = take(L + 8)
    o_S = take(T * 16)
    o_acc = take(W * 272)
    o_h = take(W * 256)
    o_q = take(W * 264)
    o_w = take(5640)
    o_ring = take(16 * 256)
    o_wv = take(2 * 1024)
    o_oh = take(3 * 512)
    o_oht = take(2 * 512)
    o_sm = take(1200)

    PA = view(o_pa, T, 8)
    PB = view(o_pb, T, 2)
    mo = [o_misc]

    def misc(*dims, dt=F):
        ap = view(mo[0], *dims)
        mo[0] += int(np.prod(dims))
        assert mo[0] <= o_misc + 4 * T + 1280
        return ap if dt == F else ap.bitcast(dt)

    wd_i = misc(T, dt=I)
    ws_i = misc(T, dt=I)
    isrc = misc(T, dt=I)
    idst = misc(T, dt=I)
    ident = misc(128)
    iota = misc(128)
    ones = misc(128)
    tri = misc(128)
    sh_f = misc(128)
    sh_b = misc(128)
    g0 = misc(1)
    g1 = misc(1)
    a_bc = misc(1)
    pcol = misc(1)
    locd = misc(T)
    B = view(o_B, L + 1)
    SC = view(o_S, T, 16)
    ACC = view(o_acc, W, 272)
    H = view(o_h, W, 256)
    QT = view(o_q, W, 264)
    WV = view(o_wv, 2, 1024)
    OH = view(o_oh, 3, 512)
    OHT = view(o_oht, 2, 512)
    bank = [nc.alloc_psum_tensor(f"bank{i}", [128, 512], F) for i in range(8)]

    pre = Slot(nc, "pre")
    m = g.mark(GP.memset(ident, 0.0))
    g.mark(GP.memset(ones, 1.0))
    g.mark(GP.memset(tri, 1.0))
    g.mark(GP.memset(sh_f, 0.0))
    g.mark(GP.memset(sh_b, 0.0))
    g.mark(GP.memset(g0, 0.0))
    m = g.mark(GP.memset(g1, 0.0))
    g.wait(m)

    def sel(t, base, mult, op, fill, pat=[[-1, 128]]):
        return g.mark(GP.affine_select(out=t, in_=t, compare_op=op, fill=fill, base=base,
                                       pattern=pat, channel_multiplier=mult))
    sel(ident, 0, 1, ALU.not_equal, 1.0)
    sel(tri, 0, -1, ALU.is_gt, 0.0, [[1, 128]])
    sel(sh_f, 8, 1, ALU.not_equal, 1.0)
    sel(sh_b, -8, 1, ALU.not_equal, 1.0)
    sel(g0, -8, 1, ALU.is_ge, NEG, [[0, 1]])
    sel(g1, 119, -1, ALU.is_ge, NEG, [[0, 1]])
    m_i = g.mark(GP.iota(iota.bitcast(I), [[1, 128]], base=0, channel_multiplier=0))
    tstart = view(o_S, T)
    g.mark(GP.iota(tstart.bitcast(I), [[128, T]], base=0, channel_multiplier=0))
    m_i = g.mark(GP.iota(pcol.bitcast(I), [[0, 1]], base=0, channel_multiplier=1))
    v.wait(m_i)
    v.mark(V.tensor_copy(iota, iota.bitcast(I)))
    v.mark(V.tensor_copy(tstart, tstart.bitcast(I)))
    m_const = v.mark(V.tensor_copy(pcol, pcol.bitcast(I)))
    m_g = m_i

    o_key = take(0)
    big = o_acc
    OHB = view(big, 25, C)
    FS = view(big + 9776, 25, C)
    assert big + 2 * 9776 <= o_w
    kf = view(o_w, C)
    posf = view(o_w + 392, C)
    posi = view(o_w + 784, C).bitcast(I)
    t1 = view(o_w + 1176, C)
    t1i = view(o_w + 1568, C).bitcast(I)
    PW = view(o_ring, C, 8)
    small = o_sm
    lastF = view(small, 26)
    cnt = view(small + 32, 26)
    tot = view(small + 64, 26)
    base = view(small + 96, 27)
    off = view(small + 128, 26)
    basei = view(small + 160, 27).bitcast(I)
    baseS = view(small + 192, 27)
    ldc = Slot(nc, "ldc")
    srci = view(o_B, C).bitcast(I)
    dsti = view(o_B + 400, C).bitcast(I)
    attr = view(o_pb, C * 2)[:, 0:1]

    if dbg is not None:
        v.wait(v.mark(V.memset(PB, 0.0)))
    m0 = v.mark(V.memset(srci, NP))
    m1 = v.mark(V.memset(dsti, NP))
    m2 = v.mark(V.memset(PW, 0.0))
    y.wait(m2)
    for (dst_t, nm) in ((srci, "src"), (dsti, "dst")):
        ldc.mark(SY.dma_start(dst_t[0:127, :], a[nm][0:127 * C].rearrange("(p c) -> p c", c=C)))
        ml = ldc.mark(SY.dma_start(dst_t[127:128, 0:NE - 127 * C],
                                   a[nm][127 * C:NE].rearrange("(o c) -> o c", o=1)))
    at4 = view(o_B + 800, C, 4)
    m3 = v.mark(V.memset(at4, 0.0))
    y.wait(m3)
    ldc.mark(SY.dma_start(at4[0:127], a["edge_attr_4"][0:127 * C, :].rearrange("(p c) k -> p c k", c=C)))
    fc1 = view(o_B + 2400, 64)
    fc2 = view(o_B + 2470, 1)
    ldc.mark(SY.dma_start(fc1[0:10, :], a["L3_gnn_fc_w1"]))
    ldc.mark(SY.dma_start(fc2[0:64, :], a["L3_gnn_fc_w2"]))
    ldc.mark(SY.dma_start(a_bc, a["L2_gnn_a"].rearrange("(o k) -> o k", o=1).to_broadcast([128, 1])))
    m_ld = ldc.mark(SY.dma_start(at4[127:128, 0:NE - 127 * C, :],
                                 a["edge_attr_4"][127 * C:NE, :].rearrange("(o c) k -> o c k", o=1)))
    emb = [view(o_acc + i * 512, 512) for i in range(4)]
    hid = [view(o_acc + 2048 + i * 512, 512) for i in range(2)]
    es = [Slot(nc, f"emb{i}") for i in range(4)]
    m_mm1, m_silu, m_r = [None] * 98, [None] * 98, [None] * 98
    p.wait(m_ld, m_g, m_const)
    m_emb = {}
    NC4 = 98

    def n4(i):
        return 4 if i < 97 else 3
    for i in range(NC4 + 1):
        if i < NC4:
            if i >= 4:
                y.wait(m_mm1[i - 4])
            w4 = 128 * n4(i)
            m_emb[i] = es[i % 4].mark(SY.dma_start(emb[i % 4][0:10, 0:w4], a["embT"][:, i * 512:i * 512 + w4]))
            if i >= 2:
                p.wait(m_silu[i - 2])
            p.wait(m_emb[i])
            m_mm1[i] = p.mark(P.matmul(bank[i % 2][0:64, 0:w4], fc1[0:10, :], emb[i % 4][0:10, 0:w4],
                                       start=True, stop=True))
            s.wait(m_mm1[i])
            if i >= 2:
                s.wait(m_r[i - 2])
            m_silu[i] = s.mark(S.activation(hid[i % 2][0:64, 0:w4], bank[i % 2][0:64, 0:w4], ACT.Silu,
                                            scale=float(np.float32(1) / np.float32(np.sqrt(10.0)))))
        if i >= 1:
            j = i - 1
            p.wait(m_silu[j])
            for k in range(n4(j)):
                col = 4 * j + k
                mm = P.matmul(bank[2][:, col:col + 1], hid[j % 2][0:64, k * 128:k * 128 + 128],
                              fc2[0:64, :], start=True, stop=True)
            m_r[j] = p.mark(mm)
    v.wait(m_ld, m_r[97])
    rr = view(o_w + 2000, C)
    cst = float(1.0 / np.sqrt(128.0) * 1.679177 / 8.0 / 4.0)
    mr = v.mark(V.tensor_scalar(rr, bank[2][:, 0:C], cst, None, ALU.mult))
    v.mark(V.tensor_copy(PW[:, :, 0], srci))
    md = v.mark(V.tensor_copy(PW[:, :, 1], dsti))
    v.wait(mr)
    m_pw = v.mark(V.tensor_tensor(PW[:, :, 2:6], at4, rr.unsqueeze(2).to_broadcast([128, C, 4]), ALU.mult))
    m_pw = v.mark(V.memset(PW[:, :, 7:8], 1.0))

    def buckets(field_int, nb, b0, dense_base, padded):
        m = None
        for b in range(nb):
            m = v.mark(V.tensor_scalar(OHB[:, b, :], kf, float(b0 + b), None, ALU.is_equal))
        v.wait(m)
        of = OHB[:, 0:nb, :].rearrange("p b c -> p (b c)")
        ff = FS[:, 0:nb, :].rearrange("p b c -> p (b c)")
        v.wait(v.mark(V.tensor_tensor_scan(ff, of, of, 0.0, ALU.add, ALU.max)))
        v.wait(v.mark(V.tensor_copy(lastF[:, 0:nb], FS[:, 0:nb, C - 1])))
        v.mark(V.tensor_copy(cnt[:, 0:1], lastF[:, 0:1]))
        mc = v.mark(V.tensor_tensor(cnt[:, 1:nb], lastF[:, 1:nb], lastF[:, 0:nb - 1], ALU.subtract))
        p.wait(mc)
        P.matmul(bank[3][:, 0:nb], tri, cnt[:, 0:nb], start=True, stop=True)
        mp = p.mark(P.matmul(bank[4][:, 0:nb], ones, cnt[:, 0:nb], start=True, stop=True))
        v.wait(mp)
        if padded:
            v.wait(v.mark(V.tensor_scalar(tot[:, 0:nb], bank[4][:, 0:nb], 127.0, None, ALU.add)))
            v.wait(v.mark(V.tensor_copy(basei[:, 0:nb], tot[:, 0:nb])))
            v.wait(v.mark(V.tensor_scalar(basei[:, 0:nb], basei[:, 0:nb], 7, 7,
                                          ALU.logical_shift_right, ALU.logical_shift_left)))
            v.wait(v.mark(V.tensor_copy(tot[:, 0:nb], basei[:, 0:nb])))
        else:
            v.wait(v.mark(V.tensor_copy(tot[:, 0:nb], bank[4][:, 0:nb])))
        if dense_base is None:
            v.wait(v.mark(V.memset(base[:, 0:1], 0.0)))
        else:
            v.wait(v.mark(V.tensor_copy(base[:, 0:1], dense_base)))
        v.wait(v.mark(V.tensor_tensor_scan(base[:, 1:nb + 1], tot[:, 0:nb], tot[:, 0:nb], base[:, 0:1],
                                           ALU.add, ALU.max)))
        v.wait(v.mark(V.tensor_tensor(off[:, 0:nb], base[:, 0:nb], bank[3][:, 0:nb], ALU.add)))
        v.wait(v.mark(V.tensor_tensor(off[:, 1:nb], off[:, 1:nb], lastF[:, 0:nb - 1], ALU.subtract)))
        v.wait(v.mark(V.tensor_scalar(off[:, 0:nb], off[:, 0:nb], -1.0, None, ALU.add)))
        fb = FS[:, 0:nb, :]
        v.wait(v.mark(V.tensor_tensor(fb, fb, off[:, 0:nb].unsqueeze(2).to_broadcast([128, nb, C]), ALU.add)))
        v.wait(v.mark(V.tensor_tensor(fb, fb, OHB[:, 0:nb, :], ALU.mult)))
        v.wait(v.mark(V.tensor_reduce(t1, fb.rearrange("p b c -> p c b"), AX, ALU.add)))
        return v.mark(V.tensor_tensor(posf, posf, t1, ALU.add))

    sct = [Slot(nc, f"sct{k}") for k in range(KS)]
    zs = Slot(nc, "zs")
    rl = Slot(nc, "rl")

    def scatter(targets, rows, words, src_tile, m_pos, m_src):
        g.wait(m_pos, m_src)
        for c in range(C):
            k = c % KS
            if sct[k].n:
                g.wait((sct[k].sem, sct[k].n))
            sct[k].mark(GP.indirect_dma_start(
                out=targets[k], out_offset=bass.IndirectOffsetOnAxis(ap=posi[:, c:c + 1], axis=0),
                in_=src_tile[:, c, 0:words], in_offset=None, bounds_check=rows - 1, oob_is_err=False))
        return [(sct[k].sem, sct[k].n) for k in range(KS)]

    zero = view(o_q, 3328)
    m_z = v.mark(V.memset(zero, 0.0))
    y.wait(m_z)
    R1, R2 = 128 * C, 128 * T
    tg1 = [dram(f"sa{k}", [R1, 8]) for k in range(KS)]
    tg2 = [dram(f"sb{k}", [R2, 8]) for k in range(KS)]
    tg3 = [dram(f"sc{k}", [R2, 4]) for k in range(KS)]
    for k in range(KS):
        zs.mark(SY.dma_start(tg1[k].rearrange("(p c) k -> p (c k)", c=C), zero[:, 0:C * 8]))
        zs.mark(SY.dma_start(tg2[k].rearrange("(p c) k -> p (c k)", c=T), zero[:, 0:T * 8]))
        m_zs = zs.mark(SY.dma_start(tg3[k].rearrange("(p c) k -> p (c k)", c=T), zero[:, 0:T * 4]))
    v.wait(m_zs)

    def reload(targets, ncol, words, dst, marks):
        y.wait(*marks)
        n = ncol * words
        parts = [view(o_acc + k * 3328, n) for k in range(KS)]
        y.wait((v.sem, v.n))
        for k in range(KS):
            mm = rl.mark(SY.dma_start(parts[k], targets[k].rearrange("(p c) k -> p (c k)", c=ncol)))
        v.wait(mm)
        v.mark(V.tensor_tensor(parts[0], parts[0], parts[1], ALU.add))
        mm = v.mark(V.tensor_tensor(parts[2], parts[2], parts[3], ALU.add))
        v.wait(mm)
        mm = v.mark(V.tensor_tensor(dst, parts[0], parts[2], ALU.add))
        v.wait(mm)
        return mm

    def split_key(src_f, want_high):
        v.wait(v.mark(V.tensor_copy(t1i, src_f)))
        if want_high:
            v.wait(v.mark(V.tensor_scalar(t1i, t1i, 7, None, ALU.logical_shift_right)))
        else:
            v.wait(v.mark(V.tensor_scalar(t1i, t1i, 127, None, ALU.bitwise_and)))
        v.wait(v.mark(V.tensor_copy(kf, t1i)))

    def padded_rows():
        v.wait(v.mark(V.tensor_copy(t1i, posf)))
        v.wait(v.mark(V.tensor_scalar(posi, t1i, 127, None, ALU.bitwise_and)))
        v.wait(v.mark(V.tensor_copy(t1, posi)))
        v.wait(v.mark(V.tensor_scalar(posi, t1i, 7, None, ALU.logical_shift_right)))
        v.wait(v.mark(V.tensor_copy(posf, posi)))
        v.wait(v.mark(V.scalar_tensor_tensor(posf, t1, float(T), posf, ALU.mult, ALU.add)))
        v.wait(v.mark(V.tensor_scalar(kf, kf, float(W), 1e6, ALU.is_ge, ALU.mult)))
        v.wait(v.mark(V.tensor_tensor(posf, posf, kf, ALU.add)))
        return v.mark(V.tensor_copy(posi, posf))

    def windows(wi):
        wide = view(o_acc, T, 24)
        v.wait(v.mark(V.tensor_tensor(wide, tstart.unsqueeze(2).to_broadcast([128, T, 24]),
                                      base[:, 1:25].unsqueeze(1).to_broadcast([128, T, 24]), ALU.is_ge)))
        v.wait(v.mark(V.tensor_reduce(wi, wide, AX, ALU.add)))

    wf_d = view(o_w + 2400, T)
    wf_s = view(o_w + 2820, T)
    v.wait(m_pw, m_r[97], m_g)
    split_key(PW[:, :, 1], False)
    v.wait(v.mark(V.memset(posf, 0.0)))
    nb = 25
    b0 = 0
    carry = view(small + 230, 1)
    first = True
    while b0 < 128:
        n = min(nb, 128 - b0)
        v.wait(buckets(None, n, b0, None if first else carry, False))
        v.wait(v.mark(V.tensor_copy(carry, base[:, n:n + 1])))
        first = False
        b0 += n
    mpos = v.mark(V.tensor_copy(posi, posf))
    marks = scatter(tg1, R1, 8, PW, mpos, m_pw)
    for mk in marks:
        v.wait(mk)
    split_key(PW[:, :, 0], True)
    v.wait(v.mark(V.memset(posf, 0.0)))
    v.wait(buckets(None, 25, 0, None, True))
    windows(wf_s)
    mpos = padded_rows()
    PW4 = view(o_B, C, 4)
    v.mark(V.memset(PW4[:, :, 2:3], 1.0))
    v.mark(V.memset(PW4[:, :, 3:4], 0.0))
    v.mark(V.tensor_copy(PW4[:, :, 0], PW[:, :, 1]))
    m4 = v.mark(V.tensor_copy(PW4[:, :, 1], PW[:, :, 0]))
    marks3 = scatter(tg3, R2, 4, PW4, mpos, m4)
    y.wait(m4)
    mm = reload(tg1, C, 8, PW.rearrange("p c k -> p (c k)"), marks)
    for mk in marks3:
        v.wait(mk)
    split_key(PW[:, :, 1], True)
    v.wait(v.mark(V.memset(posf, 0.0)))
    v.wait(buckets(None, 25, 0, None, True))
    windows(wf_d)
    mpos = padded_rows()
    marks2 = scatter(tg2, R2, 8, PW, mpos, mm)
    T4 = view(o_q, T, 4)
    reload(tg3, T, 4, T4.rearrange("p c k -> p (c k)"), marks3)
    v.mark(V.tensor_copy(idst, T4[:, :, 0]))
    v.mark(V.tensor_copy(ws_i, wf_s))
    v.wait(v.mark(V.tensor_scalar(T4[:, :, 3], T4[:, :, 2], -PADKEY, PADKEY, ALU.mult, ALU.add)))
    v.wait(v.mark(V.tensor_tensor(T4[:, :, 1], T4[:, :, 1], T4[:, :, 3], ALU.add)))
    v.wait(v.mark(V.scalar_tensor_tensor(PB[:, :, 1], wf_s, -128.0, T4[:, :, 1], ALU.mult, ALU.add)))
    reload(tg2, T, 8, PA.rearrange("p c k -> p (c k)"), marks2)
    v.mark(V.tensor_copy(isrc, PA[:, :, 0]))
    v.mark(V.tensor_copy(wd_i, wf_d))
    v.wait(v.mark(V.tensor_scalar(PA[:, :, 7], PA[:, :, 7], -PADKEY, PADKEY, ALU.mult, ALU.add)))
    v.wait(v.mark(V.tensor_tensor(PA[:, :, 1], PA[:, :, 1], PA[:, :, 7], ALU.add)))
    m_edges = v.mark(V.scalar_tensor_tensor(locd, wf_d, -128.0, PA[:, :, 1], ALU.mult, ALU.add))
    v.wait(m_edges)

    D8 = view(o_q, SB, 16, 8)

    def blocked(x):
        return x.rearrange("p (b j) k -> p j b k", j=SB)
    bank_rd = [None] * 8

    def to_scan(src, dst, m_src):
        p.wait(m_src)
        last = None
        for q in range(0, SB, 4):
            n = min(4, SB - q)
            bk = (q // 4) % 4
            p.wait(bank_rd[bk])
            for k in range(n):
                mm = P.matmul(bank[bk][:, k * 128:(k + 1) * 128],
                              src[:, (q + k) * 128:(q + k + 1) * 128],
                              ident, start=True, stop=True)
            s.wait(p.mark(mm))
            last = bank_rd[bk] = s.mark(S.activation(dst[:, q * 128:(q + n) * 128], bank[bk][:, 0:n * 128], ACT.Copy))
        return last

    def from_scan(src, m_src, use):
        p.wait(m_src)
        for j in range(SB):
            bk = j % 4
            p.wait(bank_rd[bk])
            mt = p.mark(P.matmul(bank[bk][:, 0:128], src[:, j * 128:(j + 1) * 128], ident, start=True, stop=True))
            bank_rd[bk] = use(j, bank[bk][:, 0:128], mt)

    DS = view(o_acc, L)
    md = v.mark(V.tensor_copy(D8, blocked(PA[:, :, 1:2].to_broadcast([128, T, 8]))))
    md = to_scan(view(o_q, L), DS, md)
    p.wait(md)
    mp = p.mark(P.matmul(bank[4][:, 0:1], sh_f, DS[:, L - 1:L], start=True, stop=True))
    v.wait(md, mp)
    v.mark(V.tensor_tensor(B[:, 1:L], DS[:, 1:L], DS[:, 0:L - 1], ALU.not_equal))
    v.wait(v.mark(V.tensor_tensor(B[:, 0:1], DS[:, 0:1], bank[4][:, 0:1], ALU.not_equal)))
    v.wait(v.mark(V.tensor_scalar(B[:, 0:L], B[:, 0:L], NEG, None, ALU.mult)))
    mb = v.mark(V.tensor_tensor(B[:, 0:1], B[:, 0:1], g0, ALU.add))
    p.wait(mb)
    mp = p.mark(P.matmul(bank[4][:, 0:1], sh_b, B[:, 0:1], start=True, stop=True))
    v.wait(mb, mp)
    v.wait(v.mark(V.tensor_tensor(B[:, L:L + 1], bank[4][:, 0:1], g1, ALU.add)))
    anyf = view(small + 240, 1)
    anyb = view(small + 241, 1)
    v.mark(V.tensor_reduce(anyf, B[:, 0:L], AX, ALU.min))
    m_any = v.mark(V.tensor_reduce(anyb, B[:, 1:L + 1], AX, ALU.min))
    FL = PA[:, :, 6]

    def put_flag(j, ps, mt):
        v.wait(mt)
        return v.mark(V.tensor_scalar(FL.rearrange("p (b j) -> p j b", j=SB)[:, j],
                                      ps.rearrange("p (b h) -> p b h", h=8)[:, :, 0],
                                      NEG / 2, None, ALU.is_lt))
    from_scan(B, m_any, put_flag)
    v.wait(bank_rd[0], bank_rd[1], bank_rd[2], bank_rd[3])

    rowA = view(o_sm + 256, 128)[0:1]
    rowAb = view(o_sm + 384, 128)[0:1]
    rowE = view(o_sm + 512, 128)[0:1]
    rowC = view(o_sm + 640, 128)[0:1]
    ccol = view(o_sm + 770, 1)
    p.wait((v.sem, v.n))
    P.matmul(bank[4][0:1, 0:128], anyf, ident, start=True, stop=True)
    mp = p.mark(P.matmul(bank[4][0:1, 128:256], anyb, ident, start=True, stop=True))
    v.wait(mp)
    v.mark(V.tensor_copy(rowA, bank[4][0:1, 0:128]))
    v.wait(v.mark(V.tensor_copy(rowAb, bank[4][0:1, 128:256])))

    def segment_max(SP, FB, BB, m_in):
        v.wait(m_in)
        for back in (False, True):
            dst = BB if back else FB
            st = B[:, 1:L + 1][:, ::-1] if back else B[:, 0:L]
            sp = SP[:, ::-1] if back else SP
            dv = dst[:, ::-1] if back else dst
            v.wait(v.mark(V.tensor_tensor_scan(dv, st, sp, NEG, ALU.add, ALU.max)))
            end = dst[:, 0:1] if back else dst[:, L - 1:L]
            p.wait((v.sem, v.n))
            mp = p.mark(P.matmul(bank[4][0:1, 0:128], end, ident, start=True, stop=True))
            v.wait(mp)
            v.wait(v.mark(V.tensor_copy(rowE, bank[4][0:1, 0:128])))
            row = rowAb if back else rowA
            prev = None
            order = range(15, -1, -1) if back else range(16)
            for b in order:
                cb = slice(b * 8, b * 8 + 8)
                if prev is None:
                    v.wait(v.mark(V.memset(rowC[:, cb], NEG)))
                else:
                    pb = slice(prev * 8, prev * 8 + 8)
                    v.wait(v.mark(V.tensor_tensor(rowC[:, cb], rowC[:, pb], row[:, pb], ALU.add)))
                    v.wait(v.mark(V.tensor_tensor(rowC[:, cb], rowC[:, cb], rowE[:, pb], ALU.max)))
                prev = b
            p.wait((v.sem, v.n))
            mp = p.mark(P.matmul(bank[4][:, 256:257], rowC, ones[0:1, 0:1], start=True, stop=True))
            v.wait(mp)
            v.wait(v.mark(V.tensor_copy(ccol, bank[4][:, 256:257])))
            v.wait(v.mark(V.tensor_tensor_scan(dv, st, sp, ccol, ALU.add, ALU.max)))
        return v.mark(V.tensor_tensor(FB, FB, BB, ALU.max))

    wl = Slot(nc, "wl")
    tb = Slot(nc, "tb")
    xs = Slot(nc, "xs")

    def all_done(*qs):
        return [(q.sem, q.n) for q in qs]

    def fence(*qs):
        ms = all_done(v, s, p, g)
        for q in qs:
            q.wait(*[m for m in ms if m[0] is not q.sem or q is not p])

    def load_w(ap, src):
        return wl.mark(SY.dma_start(ap, src))

    MS = view(o_sm + 256 + 520, 2 * W)
    RS = view(o_sm + 256 + 580, W)
    EP = view(o_sm + 256 + 610, 1)
    m_ep = v.mark(V.memset(EP, 1e-5))
    ST = view(o_sm + 960, 6 * W)

    def ln_stats(X):
        m = None
        for w in range(W):
            m = v.mark(V.bn_stats(ST[:, 6 * w:6 * w + 6], X[:, w, :]))
        v.wait(m)
        for w in range(W):
            m = v.mark(V.bn_aggr(MS[:, 2 * w:2 * w + 2], ST[:, 6 * w:6 * w + 6]))
        s.wait(m)
        ms = s.mark(S.activation(RS, MS.rearrange("p (w k) -> p w k", k=2)[:, :, 1], ACT.Sqrt, bias=EP))
        v.wait(m, ms)
        m = v.mark(V.reciprocal(RS, RS))
        v.wait(m)
        return m

    def normed(dst, src, w):
        return V.tensor_scalar(dst, src, MS[:, 2 * w:2 * w + 1], RS[:, w:w + 1], ALU.subtract, ALU.mult)

    XN = view(o_ring, 2, 256)
    XT = view(o_ring + 512, 2, 512)
    OUTB = view(o_ring + 1536, 2, 768)

    def transposed(n, get, after, gb=None):
        done = [None] * n
        cp = [None] * n

        def first(w):
            ap, m = get(w)
            p.wait(m, bank_rd[w % 2])
            for k in range(2):
                mm = P.matmul(bank[w % 2][:, k * 128:(k + 1) * 128], ap[:, k * 128:(k + 1) * 128], ident,
                              start=True, stop=True)
            mt = p.mark(mm)
            s.wait(mt)
            if w >= 2:
                s.wait(done[w - 2])
            for k in range(2):
                o = XT[:, w % 2, k * 128:(k + 1) * 128]
                i = bank[w % 2][:, k * 128:(k + 1) * 128]
                if gb is None:
                    cp[w] = s.mark(S.activation(o, i, ACT.Copy))
                else:
                    cp[w] = s.mark(S.activation(o, i, ACT.Identity, scale=gb[0][:, k:k + 1], bias=gb[1][:, k:k + 1]))
            bank_rd[w % 2] = cp[w]
            return mt
        mts = {}
        for w in range(n + 1):
            if w < n:
                mts[w] = first(w)
            if w >= 1:
                done[w - 1] = after(w - 1, XT[:, (w - 1) % 2, :], cp[w - 1])
        return mts, done

    def proj(xt, wt, cols, bk):
        for k in range(2):
            mm = P.matmul(bank[bk][:, 0:cols], xt[:, k * 128:(k + 1) * 128], wt[:, k, :], start=(k == 0), stop=(k == 1))
        return mm

    def rows_bc(ap1, n):
        return ap1.rearrange("(o n) -> o n", o=1).to_broadcast([128, n])

    def kview(ap):
        return ap.rearrange("(k p) n -> p k n", p=128)

    def col(ap1, k):
        return ap1.rearrange("(k p) -> p k", p=128)

    gs = [Slot(nc, f"gs{i}") for i in range(16)]

    def edge_loop(table, width, idx, loc, wi, ring_o, ngrp, stageB, expand, need_oht):
        ring = view(ring_o, ngrp, 4, width)
        rd_rows = {}
        rd_oh = {}
        rd_oht = {}
        mg, moh, moht = {}, {}, {}

        def gather(i):
            if i >= ngrp:
                g.wait(*rd_rows[i - ngrp])
            ms = []
            for k in range(4):
                sl = (i % ngrp) * 4 + k
                ms.append(gs[sl].mark(GP.indirect_dma_start(
                    out=ring[:, i % ngrp, k, :], out_offset=None, in_=table,
                    in_offset=bass.IndirectOffsetOnAxis(ap=idx[:, 4 * i + k:4 * i + k + 1], axis=0))))
            mg[i] = ms

        def onehot(i):
            if i >= 3:
                v.wait(*rd_oh[i - 3])
            moh[i] = v.mark(V.tensor_tensor(
                OH[:, i % 3, :].rearrange("p (k n) -> p k n", k=4),
                loc[:, 4 * i:4 * i + 4].unsqueeze(2).to_broadcast([128, 4, 128]),
                iota.unsqueeze(1).to_broadcast([128, 4, 128]), ALU.is_equal))
            if need_oht:
                p.wait(moh[i], bank_rd[i % 2])
                for k in range(4):
                    mm = P.matmul(bank[i % 2][:, k * 128:(k + 1) * 128], OH[:, i % 3, k * 128:(k + 1) * 128],
                                  ident, start=True, stop=True)
                mt = p.mark(mm)
                s.wait(mt)
                if i >= 2:
                    s.wait(*rd_oht[i - 2])
                moht[i] = bank_rd[i % 2] = s.mark(S.activation(OHT[:, i % 2, :], bank[i % 2][:, :], ACT.Copy))
        ahead = ngrp - 1
        for i in range(min(ahead, G)):
            gather(i)
        onehot(0)
        for i in range(G):
            if i + 1 < G:
                onehot(i + 1)
            a_, b_, c_ = stageB(i, ring[:, i % ngrp], OH[:, i % 3, :], OHT[:, i % 2, :], mg[i], moh[i], moht.get(i))
            rd_rows[i], rd_oh[i], rd_oht[i] = a_, b_, c_
            if i + ahead < G:
                gather(i + ahead)

    regs = {}

    def win(q, wi, i):
        k = id(q)
        if k not in regs:
            regs[k] = [q.eng.alloc_register(f"w{j}_{len(regs)}") for j in range(4)]
        q.eng.reg_load(regs[k], wi[0:1, 4 * i:4 * i + 4])
        return [q.eng.snap(r, min_val=0, max_val=W - 1) for r in regs[k]]

    def accumulate(width, wi):
        def add(i, marks, bks):
            ws = win(v, wi, i)
            res = []
            for k in range(4):
                v.wait(marks[k])
                if add.last:
                    v.wait(add.last)
                d = ACC[:, bass.ds(ws[k], 1), 0:width]
                add.last = v.mark(V.tensor_tensor(d, d, bank[bks[k]][:, 0:width].unsqueeze(1), ALU.add))
                bank_rd[bks[k]] = add.last
        add.last = None
        return add

    KT, VT = dram("KT", [NP, 256]), dram("VT", [NP, 256])
    X1T = dram("X1T", [NP, 72])
    XA = dram("XA", [NP, 256])
    MT = [dram(f"MT{i}", [NP, 256]) for i in range(4)]
    YT = dram("YT", [NP, 512])

    def load_x(dst):
        m = v.mark(V.memset(dst[:, 24, :], 0.0))
        y.wait(m)
        xs.mark(SY.dma_start(dst[:, 0:24, :], a["x"][0:3072, :].rearrange("(w p) f -> p w f", p=128)))
        return xs.mark(SY.dma_start(dst[0:NN - 3072, 24, :], a["x"][3072:NN, :]))

    if dbg is not None and stop == 0:
        dd = Slot(nc, "dbg")
        y.wait(*all_done(v, s, p))
        for nm, ap in (("PA", view(o_pa, T * 8)), ("PB", view(o_pb, T * 2)), ("B", view(o_B, L + 1)),
                       ("wd", wd_i.bitcast(F)), ("ws", ws_i.bitcast(F)), ("idst", idst.bitcast(F)), ("locd", locd)):
            m = dd.mark(SY.dma_start(dbg[nm], ap))
        y.wait(m)
        return

    WM = view(o_w, 5640)
    fence(y, v, s, p)
    w_in = WM[:, 0:512].rearrange("p (k n) -> p k n", k=2)
    b_bc = WM[:, 512:768]
    load_w(w_in, kview(a["L0_gnn_w_in"]))
    m_w = load_w(b_bc, rows_bc(a["L0_gnn_b_in"], 256))
    XX = view(o_acc, W, 256)
    mx = load_x(XX)
    p.wait(m_w)
    v.wait(m_w)

    def aft(w, xt, m):
        p.wait(m, bank_rd[2 + w % 2])
        mm = p.mark(proj(xt, w_in, 256, 2 + w % 2))
        v.wait(mm)
        bank_rd[2 + w % 2] = v.mark(V.tensor_tensor(H[:, w, :], bank[2 + w % 2][:, 0:256], b_bc, ALU.add))
        return mm
    transposed(W, lambda w: (XX[:, w, :], mx), aft)

    wq = WM[:, 0:512].rearrange("p (k n) -> p k n", k=2)
    wk = WM[:, 512:1024].rearrange("p (k n) -> p k n", k=2)
    wv = WM[:, 1024:1536].rearrange("p (k n) -> p k n", k=2)
    bq, bk_, bv = WM[:, 1536:1792], WM[:, 1792:2048], WM[:, 2048:2304]
    gb = WM[:, 2304:2312].rearrange("p (j k) -> p j k", k=2)
    wo = WM[:, 2320:2832].rearrange("p (k n) -> p k n", k=2)
    bo = WM[:, 2832:3088]
    w1 = WM[:, 0:2048].rearrange("p (k n) -> p k n", k=2)
    w2 = WM[:, 3328:5376].rearrange("p (k n) -> p k n", k=8)
    b1c = WM[:, 3088:3096]
    b2 = WM[:, 3096:3352 - 24] if False else WM[:, 5376:5632]
    scale = 1.0 / np.sqrt(32.0)

    for l in range(2):
        fence(y, v, s, p)
        load_w(wq, kview(a["L0_gnn_wq"][l]))
        load_w(wk, kview(a["L0_gnn_wk"][l]))
        load_w(wv, kview(a["L0_gnn_wv"][l]))
        load_w(bq, rows_bc(a["L0_gnn_bq"][l], 256))
        load_w(bk_, rows_bc(a["L0_gnn_bk"][l], 256))
        load_w(bv, rows_bc(a["L0_gnn_bv"][l], 256))
        load_w(wo, kview(a["L0_gnn_wo"][l]))
        load_w(bo, rows_bc(a["L0_gnn_bo"][l], 256))
        with nc.allow_non_contiguous_dma(reason="small columns"):
            load_w(gb[:, 0, :], col(a["L0_gnn_ln1_g"][l], 2))
            load_w(gb[:, 1, :], col(a["L0_gnn_ln1_b"][l], 2))
            load_w(gb[:, 2, :], col(a["L0_gnn_ln2_g"][l], 2))
            load_w(gb[:, 3, :], col(a["L0_gnn_ln2_b"][l], 2))
            load_w(b1c, col(a["L0_gnn_b1"][l], 8))
        load_w(w2, a["L0_gnn_w2"][l].rearrange("(k p) n -> p k n", p=128))
        m_w = load_w(b2, rows_bc(a["L0_gnn_b2"][l], 256))
        ln_stats(H)
        s.wait(m_w)
        p.wait(m_w)
        v.wait(m_w)
        mts = {}
        st_out = [None, None]

        def get(w):
            if w >= 2:
                v.wait(mts[w - 2])
            m = v.mark(normed(XN[:, w % 2, :], H[:, w, :], w))
            return XN[:, w % 2, :], m

        def aft(w, xt, m):
            o = OUTB[:, w % 2, :]
            p.wait(m)
            for k, (wt, bb) in enumerate(((wq, bq), (wk, bk_), (wv, bv))):
                bk = 2 + (3 * w + k) % 6
                p.wait(bank_rd[bk])
                mm = p.mark(proj(xt, wt, 256, bk))
                v.wait(mm)
                if k == 0:
                    v.wait(st_out[w % 2])
                bank_rd[bk] = v.mark(V.tensor_tensor(o[:, k * 256:(k + 1) * 256], bank[bk][:, 0:256], bb, ALU.add))
            v.wait(bank_rd[bk])
            mq = v.mark(V.tensor_scalar(QT[:, w, 0:256], o[:, 0:256], float(scale), None, ALU.mult))
            v.wait(mq)
            v.wait(v.mark(V.tensor_tensor(o[:, 0:256], QT[:, w, 0:256], o[:, 256:512], ALU.mult)))
            ml = v.mark(V.tensor_reduce(QT[:, w, 256:264], o[:, 0:256].rearrange("p (h d) -> p h d", d=32), AX, ALU.add))
            y.wait(ml)
            tbs = tbl[w % 2]
            tbs.mark(SY.dma_start(KT[w * 128:(w + 1) * 128, :], o[:, 256:512]))
            st_out[w % 2] = tbs.mark(SY.dma_start(VT[w * 128:(w + 1) * 128, :], o[:, 512:768]))
            return mm
        if l == 0:
            tbl = [Slot(nc, "tb0"), Slot(nc, "tb1")]
        n_t, n_d = {}, {}

        done = [None] * W
        cp = [None] * W
        for w in range(W + 1):
            if w < W:
                ap, m = get(w)
                p.wait(m, bank_rd[w % 2])
                for k in range(2):
                    mm = P.matmul(bank[w % 2][:, k * 128:(k + 1) * 128], ap[:, k * 128:(k + 1) * 128], ident,
                                  start=True, stop=True)
                mts[w] = p.mark(mm)
                s.wait(mts[w])
                if w >= 2:
                    s.wait(done[w - 2])
                for k in range(2):
                    cp[w] = s.mark(S.activation(XT[:, w % 2, k * 128:(k + 1) * 128],
                                                bank[w % 2][:, k * 128:(k + 1) * 128], ACT.Identity,
                                                scale=gb[:, 0, k:k + 1], bias=gb[:, 1, k:k + 1]))
                bank_rd[w % 2] = cp[w]
            if w >= 1:
                done[w - 1] = aft(w - 1, XT[:, (w - 1) % 2, :], cp[w - 1])
        fence(v, s, p, g)
        g.wait(st_out[0], st_out[1])

        rd_ps = {}
        WV4 = [WV[:, j, :].rearrange("p (k f) -> p k f", k=4) for j in range(2)]

        def scores(i, rows, oh, oht, mg, moh, moht):
            ws = win(p, wd_i, i)
            ms = []
            for k in range(4):
                p.wait(moht, bank_rd[4 + k])
                ms.append(p.mark(P.matmul(bank[4 + k][:, 0:264], oht[:, k * 128:(k + 1) * 128],
                                          QT[:, bass.ds(ws[k], 1), :], start=True, stop=True)))
            tmp = WV4[i % 2]
            mv = []
            for k in range(4):
                v.wait(ms[k], mg[k])
                mv.append(v.mark(V.tensor_tensor(tmp[:, k, :], rows[:, k, :], bank[4 + k][:, 0:256], ALU.mult)))
                s.wait(ms[k], mv[k])
                bank_rd[4 + k] = s.mark(S.activation(SC[:, 4 * i + k, 8:16], bank[4 + k][:, 256:264], ACT.Copy))
            v.wait(mv[3])
            v.mark(V.tensor_reduce(SC[:, 4 * i:4 * i + 4, 0:8],
                                   tmp.rearrange("p k (h d) -> p k h d", d=32), AX, ALU.add))
            return [mv[3]], [moht], [ms[3]]
        edge_loop(KT, 256, isrc, locd, wd_i, o_ring, 4, scores, None, True)
        SP8 = view(o_q, SB, 16, 8)
        fence(v, s, p)
        mm = v.mark(V.tensor_tensor(SP8, blocked(SC[:, :, 0:8]), blocked(SC[:, :, 8:16]), ALU.max))
        SPs, FB, BB = view(o_acc, L), view(o_acc + L, L), view(o_q, L)
        mm = to_scan(view(o_q, L), SPs, mm)
        v.wait(*all_done(p))
        mm = segment_max(SPs, FB, BB, mm)

        def put_m(j, ps, mt):
            v.wait(mt)
            d = SC.rearrange("p (b j) k -> p j b k", j=SB)[:, j]
            pv = ps.rearrange("p (b h) -> p b h", h=8)
            v.mark(V.tensor_tensor(d[:, :, 0:8], d[:, :, 0:8], pv, ALU.subtract))
            return v.mark(V.tensor_tensor(d[:, :, 8:16], d[:, :, 8:16], pv, ALU.subtract))
        from_scan(FB, mm, put_m)
        s.wait(bank_rd[0], bank_rd[1], bank_rd[2], bank_rd[3])
        me = s.mark(S.activation(SC, SC, ACT.Exp))
        v.wait(me)
        v.mark(V.tensor_tensor(SC[:, :, 8:16], SC[:, :, 8:16], FL.unsqueeze(2).to_broadcast([128, T, 8]), ALU.mult))
        m_acc0 = v.mark(V.memset(ACC, 0.0))
        v.wait(m_acc0)
        fence(p, v, g)
        add = accumulate(272, wd_i)

        def values(i, rows, oh, oht, mg, moh, moht):
            j = i % 2
            w_ = WV4[j]
            v.wait(*mg, *( [rdwv[j]] if rdwv[j] else []))
            mw = v.mark(V.tensor_tensor(w_.rearrange("p k (h d) -> p k h d", d=32),
                                        rows.rearrange("p k (h d) -> p k h d", d=32),
                                        SC[:, 4 * i:4 * i + 4, 0:8].unsqueeze(3).to_broadcast([128, 4, 8, 32]), ALU.mult))
            p.wait(mw, moh)
            ms = []
            bks = [4 * (i % 2) + k for k in range(4)]
            for k in range(4):
                p.wait(bank_rd[bks[k]])
                P.matmul(bank[bks[k]][:, 0:256], oh[:, k * 128:(k + 1) * 128], w_[:, k, :], start=True, stop=True)
                ms.append(p.mark(P.matmul(bank[bks[k]][:, 256:272], oh[:, k * 128:(k + 1) * 128], SC[:, 4 * i + k, :],
                                          start=True, stop=True)))
            rdwv[j] = ms[3]
            pend.append((i, ms, bks))
            if len(pend) > 1:
                add(*pend.pop(0))
            return [mw], [ms[3]], []
        rdwv = [None, None]
        pend = []
        edge_loop(VT, 256, isrc, locd, wd_i, o_ring, 4, values, None, False)
        add(*pend.pop(0))

        fence(v, s, p, y)
        VB = view(o_q, 4, 256)
        vb_s = [Slot(nc, f"vb{l}{k}") for k in range(4)]
        AG = XN
        rz = view(o_sm + 1112, 8)
        lv = {}

        def ldv(w):
            if w >= 4:
                y.wait(cons[w - 4])
            lv[w] = vb_s[w % 4].mark(SY.dma_start(VB[:, w % 4, :], VT[w * 128:(w + 1) * 128, :]))
        cons = {}
        ldv(0)
        ldv(1)
        ldv(2)
        mts = {}
        done = [None] * W
        cp = [None] * W
        for w in range(W + 1):
            if w < W:
                if w + 3 < W:
                    ldv(w + 3)
                hd = "p (h d) -> p h d"
                v.wait(lv[w])
                if w >= 2:
                    v.wait(mts[w - 2])
                ag = AG[:, w % 2, :]
                v.mark(V.tensor_tensor(rz, ACC[:, w, 256:264], ACC[:, w, 264:272], ALU.add))
                ma = v.mark(V.tensor_tensor(ag.rearrange(hd, d=32), VB[:, w % 4, :].rearrange(hd, d=32),
                                            ACC[:, w, 264:272].unsqueeze(2).to_broadcast([128, 8, 32]), ALU.mult))
                cons[w] = ma
                v.wait(ma)
                v.mark(V.tensor_tensor(ag, ag, ACC[:, w, 0:256], ALU.add))
                v.wait(v.mark(V.tensor_scalar(rz, rz, 1e-30, None, ALU.max)))
                v.wait(v.mark(V.reciprocal(rz, rz)))
                m = v.mark(V.tensor_tensor(ag.rearrange(hd, d=32), ag.rearrange(hd, d=32),
                                           rz.unsqueeze(2).to_broadcast([128, 8, 32]), ALU.mult))
                v.wait(m)
                p.wait(m, bank_rd[w % 2])
                for k in range(2):
                    mm = P.matmul(bank[w % 2][:, k * 128:(k + 1) * 128], ag[:, k * 128:(k + 1) * 128], ident,
                                  start=True, stop=True)
                mts[w] = p.mark(mm)
                s.wait(mts[w])
                if w >= 2:
                    s.wait(done[w - 2])
                cp[w] = bank_rd[w % 2] = s.mark(S.activation(XT[:, w % 2, 0:256], bank[w % 2][:, 0:256], ACT.Copy))
            if w >= 1:
                u = w - 1
                p.wait(cp[u], bank_rd[2 + u % 2])
                done[u] = p.mark(proj(XT[:, u % 2, :], wo, 256, 2 + u % 2))
                v.wait(done[u])
                v.mark(V.tensor_tensor(H[:, u, :], H[:, u, :], bo, ALU.add))
                v.wait((v.sem, v.n))
                bank_rd[2 + u % 2] = v.mark(V.tensor_tensor(H[:, u, :], H[:, u, :], bank[2 + u % 2][:, 0:256], ALU.add))
        v.wait((v.sem, v.n))
        fence(y, v, s, p)
        m_w1 = load_w(w1, kview(a["L0_gnn_w1"][l]))
        ln_stats(H)
        p.wait(m_w1)
        XT4 = view(o_acc, 2, 2, 512)
        HT = view(o_acc + 2048, 8, 512)
        XN8 = view(o_q, 8, 256)
        ht_rd = None
        xn_rd = {}
        for gr in range(7):
            ws_ = list(range(gr * 4, min(gr * 4 + 4, W)))
            n = len(ws_) * 128
            for w in ws_:
                if w >= 8:
                    v.wait(xn_rd[w - 8])
                m = v.mark(normed(XN8[:, w % 8, :], H[:, w, :], w))
                bk = w % 2
                p.wait(m, bank_rd[bk])
                for k in range(2):
                    mm = P.matmul(bank[bk][:, k * 128:(k + 1) * 128], XN8[:, w % 8, k * 128:(k + 1) * 128], ident,
                                  start=True, stop=True)
                xn_rd[w] = p.mark(mm)
                s.wait(xn_rd[w])
                for k in range(2):
                    mc = s.mark(S.activation(XT4[:, gr % 2, k, (w % 4) * 128:(w % 4) * 128 + 128],
                                             bank[bk][:, k * 128:(k + 1) * 128], ACT.Identity,
                                             scale=gb[:, 2, k:k + 1], bias=gb[:, 3, k:k + 1]))
                bank_rd[bk] = mc
            p.wait(mc)
            mh = []
            for j in range(8):
                bk = 2 + j % 4
                p.wait(bank_rd[bk])
                for k in range(2):
                    mm = P.matmul(bank[bk][:, 0:n], w1[:, k, j * 128:(j + 1) * 128], XT4[:, gr % 2, k, 0:n],
                                  start=(k == 0), stop=(k == 1))
                s.wait(p.mark(mm), ht_rd)
                mc = s.mark(S.activation(HT[:, j, 0:n], bank[bk][:, 0:n], ACT.Gelu, bias=b1c[:, j:j + 1]))
                bank_rd[bk] = mc
                mh.append(mc)
            for w in ws_:
                bk = 6 + w % 2
                p.wait(bank_rd[bk])
                for j in range(8):
                    p.wait(mh[j])
                    mm = P.matmul(bank[bk][:, 0:256], HT[:, j, (w % 4) * 128:(w % 4) * 128 + 128], w2[:, j, :],
                                  start=(j == 0), stop=(j == 7))
                ht_rd = p.mark(mm)
                v.wait(ht_rd)
                v.wait(v.mark(V.tensor_tensor(H[:, w, :], H[:, w, :], b2, ALU.add)))
                bank_rd[bk] = v.mark(V.tensor_tensor(H[:, w, :], H[:, w, :], bank[bk][:, 0:256], ALU.add))
        v.wait((v.sem, v.n))

    def norm_all(X):
        ln_stats(X)
        for w in range(W):
            m = v.mark(normed(X[:, w, :], X[:, w, :], w))
        v.wait(m)
        return m

    fence(y, v)
    XX = view(o_q, W, 256)
    mx = load_x(XX)
    v.wait(mx)
    v.wait(v.mark(V.tensor_tensor(H, H, XX, ALU.add)))
    norm_all(H)

    def dump(ap, m):
        dd = Slot(nc, "dbgx")
        y.wait(*all_done(v, s, p), m)
        y.wait(dd.mark(SY.dma_start(dbg["H"].rearrange("(w p) f -> p w f", p=128), ap)))
    if dbg is not None and stop == 1:
        dump(H, None)
        return

    fence(y, s, p, v)
    W1_ = WM[:, 0:128].rearrange("p (k n) -> p k n", k=2)
    wlr = WM[:, 128:136]
    b_1 = WM[:, 144:208]
    load_w(W1_, kview(a["L1_gnn_W"]))
    with nc.allow_non_contiguous_dma(reason="small transposed weights"):
        load_w(wlr[0:64, 0:4], a["L1_gnn_Wl"].rearrange("h o -> o h"))
        load_w(wlr[0:64, 4:8], a["L1_gnn_Wr"].rearrange("h o -> o h"))
    m_w = load_w(b_1, rows_bc(a["L1_gnn_b"], 64))
    p.wait(m_w)
    v.wait(m_w)
    EL = view(o_q, W, 4)
    X1 = view(o_q + 128, 4, 72)
    X1c = view(o_q + 512, 4, 128)
    mz = v.mark(V.memset(X1, 0.0))
    st4 = [Slot(nc, f"x1s{k}") for k in range(4)]
    st_m = [None] * 4
    m_h = (v.sem, v.n)
    x1t_rd = {}

    def aft(w, xt, m):
        p.wait(m, bank_rd[2 + w % 2])
        bkk = bank[2 + w % 2]
        proj(xt, W1_, 64, 2 + w % 2)
        for k in range(2):
            mm = P.matmul(bkk[0:64, 128:256], W1_[:, k, :], xt[:, k * 128:(k + 1) * 128], start=(k == 0), stop=(k == 1))
        mm = p.mark(mm)
        s.wait(mm)
        if w >= 4:
            s.wait(x1t_rd[w - 4])
        mc = s.mark(S.activation(X1c[0:64, w % 4, :], bkk[0:64, 128:256], ACT.Copy))
        p.wait(mc, bank_rd[4 + w % 2])
        x1t_rd[w] = p.mark(P.matmul(bank[4 + w % 2][:, 0:8], X1c[0:64, w % 4, :], wlr[0:64, :], start=True, stop=True))
        v.wait(mz, st_m[w % 4], x1t_rd[w])
        bank_rd[2 + w % 2] = v.mark(V.tensor_copy(X1[:, w % 4, 0:64], bkk[:, 0:64]))
        v.mark(V.tensor_copy(X1[:, w % 4, 64:68], bank[4 + w % 2][:, 4:8]))
        bank_rd[4 + w % 2] = v.mark(V.tensor_copy(EL[:, w, :], bank[4 + w % 2][:, 0:4]))
        y.wait(bank_rd[4 + w % 2])
        st_m[w % 4] = st4[w % 4].mark(SY.dma_start(X1T[w * 128:(w + 1) * 128, :], X1[:, w % 4, :]))
        return mm
    transposed(W, lambda w: (H[:, w, :], m_h), aft)
    v.wait(v.mark(V.memset(ACC, 0.0)))
    fence(p, s, v, g)
    g.wait(*st_m)
    locs = PB[:, :, 1]
    E4 = view(o_q + 1100, 2, 16)
    Z4 = view(o_q + 1140, 2, 16)
    add = accumulate(260, ws_i)
    rdwv, rdz = [None, None], [None, None]
    pend = []

    def gat(i, rows, oh, oht, mg, moh, moht):
        j = i % 2
        ws = win(p, ws_i, i)
        p.wait(moht, bank_rd[2 + j])
        for k in range(4):
            mm = P.matmul(bank[2 + j][:, 4 * k:4 * k + 4], oht[:, k * 128:(k + 1) * 128], EL[:, bass.ds(ws[k], 1), :],
                          start=True, stop=True)
        mel = p.mark(mm)
        v.wait(mel, *mg, rdwv[j])
        z, e = Z4[:, j, :], E4[:, j, :]
        z3 = z.rearrange("p (k h) -> p k h", h=4)
        m = v.mark(V.tensor_tensor(z3, bank[2 + j][:, 0:16].rearrange("p (k h) -> p k h", h=4), rows[:, :, 64:68], ALU.add))
        bank_rd[2 + j] = m
        v.wait(m)
        m = v.mark(V.scalar_tensor_tensor(z, z, 0.2, z, ALU.mult, ALU.max))
        s.wait(m, rdwv[j])
        me = s.mark(S.activation(e, z, ACT.Exp))
        v.wait(me)
        w_ = WV[:, j, :].rearrange("p (k h d) -> p k h d", k=4, h=4)
        mw = v.mark(V.tensor_tensor(w_[:, 0:4],
                                    rows[:, :, 0:64].unsqueeze(2).to_broadcast([128, 4, 4, 64]),
                                    e.rearrange("p (k h) -> p k h", h=4).unsqueeze(3).to_broadcast([128, 4, 4, 64]),
                                    ALU.mult)) if False else None
        for k in range(4):
            mw = v.mark(V.tensor_tensor(w_[:, k], rows[:, k, 0:64].unsqueeze(1).to_broadcast([128, 4, 64]),
                                        e[:, 4 * k:4 * k + 4].unsqueeze(2).to_broadcast([128, 4, 64]), ALU.mult))
        p.wait(mw, moh)
        ms = []
        bks = [4, 5, 6, 7]
        if pend:
            add(*pend.pop(0))
        for k in range(4):
            p.wait(bank_rd[4 + k])
            P.matmul(bank[4 + k][:, 0:256], oh[:, k * 128:(k + 1) * 128], WV[:, j, k * 256:(k + 1) * 256], start=True, stop=True)
            ms.append(p.mark(P.matmul(bank[4 + k][:, 256:260], oh[:, k * 128:(k + 1) * 128], e[:, 4 * k:4 * k + 4],
                                      start=True, stop=True)))
        rdwv[j] = ms[3]
        pend.append((i, ms, bks))
        return [mw], [ms[3]], [mel]
    edge_loop(X1T, 72, idst, locs, ws_i, o_ring, 4, gat, None, True)
    add(*pend.pop(0))
    fence(v, s)
    hd = "p (h d) -> p h d"
    TA = view(o_ring, 4, 256)
    rs4 = view(o_sm + 1112, 4)
    ex_m = {}
    for w in range(W):
        t = TA[:, w % 4, :]
        v.wait(v.mark(V.tensor_scalar(rs4, ACC[:, w, 256:260], 1e-12, None, ALU.max)))
        v.wait(v.mark(V.reciprocal(rs4, rs4)))
        av = ACC[:, w, 0:256].rearrange(hd, d=64)
        v.wait(v.mark(V.tensor_tensor(av, av, rs4.unsqueeze(2).to_broadcast([128, 4, 64]), ALU.mult)))
        v.wait(v.mark(V.tensor_tensor(av, av, b_1.unsqueeze(1).to_broadcast([128, 4, 64]), ALU.add)))
        m = v.mark(V.tensor_scalar(t, ACC[:, w, 0:256], 0.0, None, ALU.min))
        s.wait(m)
        me = s.mark(S.activation(t, t, ACT.Exp))
        v.mark(V.scalar_tensor_tensor(H[:, w, :], ACC[:, w, 0:256], 0.0, H[:, w, :], ALU.max, ALU.add))
        v.wait(me, (v.sem, v.n))
        v.mark(V.scalar_tensor_tensor(H[:, w, :], t, -1.0, H[:, w, :], ALU.add, ALU.add))
    v.wait((v.sem, v.n))
    norm_all(H)
    if dbg is not None and stop == 2:
        dump(H, None)
        return

    fence(y, s, p, v)
    WA = WM[:, 0:512].rearrange("p (k n) -> p k n", k=2)
    WB = WM[:, 512:1024].rearrange("p (k n) -> p k n", k=2)
    b1_, b2_ = WM[:, 1024:1280], WM[:, 1280:1536]
    load_w(WA, kview(a["L2_gnn_W1"]))
    load_w(WB, kview(a["L2_gnn_W2"]))
    load_w(b1_, rows_bc(a["L2_gnn_b1"], 256))
    m_w = load_w(b2_, rows_bc(a["L2_gnn_b2"], 256))
    p.wait(m_w)
    v.wait(m_w)
    ST8 = view(o_q, 8, 256)
    sts = [Slot(nc, f"st{k}") for k in range(8)]
    st_m = [None] * 8
    HX = view(o_S, W, 256)

    def to_table(dst, src, wt):
        m_h = (v.sem, v.n)

        def aft(w, xt, m):
            p.wait(m, bank_rd[2 + w % 2])
            mm = p.mark(proj(xt, wt, 256, 2 + w % 2))
            v.wait(mm, st_m[w % 8])
            bank_rd[2 + w % 2] = v.mark(V.tensor_copy(ST8[:, w % 8, :], bank[2 + w % 2][:, 0:256]))
            y.wait(bank_rd[2 + w % 2])
            st_m[w % 8] = sts[w % 8].mark(SY.dma_start(dst[w * 128:(w + 1) * 128, :], ST8[:, w % 8, :]))
            return mm
        transposed(W, lambda w: (src[:, w, :], m_h), aft)

    def hop(table, idx, loc, wi):
        v.wait(v.mark(V.memset(ACC, 0.0)))
        fence(p, s, v, g)
        g.wait(*st_m)
        add = accumulate(257, wi)
        pend = []

        def body(i, rows, oh, oht, mg, moh, moht):
            ms = []
            bks = [4 * (i % 2) + k for k in range(4)]
            p.wait(moh)
            for k in range(4):
                p.wait(bank_rd[bks[k]], mg[k])
                P.matmul(bank[bks[k]][:, 0:256], oh[:, k * 128:(k + 1) * 128], rows[:, k, :], start=True, stop=True)
                ms.append(p.mark(P.matmul(bank[bks[k]][:, 256:257], oh[:, k * 128:(k + 1) * 128], ones[:, 0:1],
                                          start=True, stop=True)))
            pend.append((i, ms, bks))
            if len(pend) > 1:
                add(*pend.pop(0))
            return [ms[3]], [ms[3]], []
        edge_loop(table, 256, idx, loc, wi, o_ring, 4, body, None, False)
        add(*pend.pop(0))
        v.wait((v.sem, v.n))
        v.wait(v.mark(V.tensor_scalar(ACC[:, :, 256:257], ACC[:, :, 256:257], 1.0, None, ALU.max)))
        v.wait(v.mark(V.reciprocal(ACC[:, :, 256:257], ACC[:, :, 256:257])))
        v.wait(v.mark(V.tensor_tensor(ACC[:, :, 0:256], ACC[:, :, 0:256],
                                      ACC[:, :, 256:257].to_broadcast([128, W, 256]), ALU.mult)))

    def prelu(dst, src, tmp):
        v.wait(v.mark(V.tensor_scalar(tmp, src, 0.0, a_bc, ALU.min, ALU.mult)))
        v.wait(v.mark(V.scalar_tensor_tensor(dst, src, 0.0, tmp, ALU.max, ALU.add)))

    for r in range(2):
        to_table(MT[2 * r], H if r == 0 else HX, WA if r == 0 else WB)
        hop(MT[2 * r], isrc, locd, wd_i)
        y.wait((v.sem, v.n))
        st_m[0] = sts[0].mark(SY.dma_start(MT[2 * r + 1].rearrange("(w p) f -> p w f", p=128), ACC[:, :, 0:256]))
        v.wait(st_m[0])
        hop(MT[2 * r + 1], idst, locs, ws_i)
        bb = b1_ if r == 0 else b2_
        v.wait(v.mark(V.tensor_tensor(HX, ACC[:, :, 0:256], bb.unsqueeze(1).to_broadcast([128, W, 256]), ALU.add)))
        if r == 1:
            v.wait(v.mark(V.tensor_tensor(HX, HX, H, ALU.add)))
        prelu(HX, HX, view(o_q, W, 256))
    v.wait(v.mark(V.tensor_tensor(H, H, HX, ALU.add)))
    norm_all(H)
    if dbg is not None and stop == 3:
        dump(H, None)
        return

    fence(y, s, p, v)
    W0 = WM[:, 0:128]
    W1c = WM[:, 128:256]
    load_w(W0[0:64, 0:64], a["L3_gnn_w_00_0"])
    load_w(W0[0:64, 64:128], a["L3_gnn_w_01_1"])
    load_w(W1c[0:64, 0:64], a["L3_gnn_w_10_1"])
    m_w = load_w(W1c[0:64, 64:128], a["L3_gnn_w_11_0"])
    v.wait(m_w)
    mw3 = v.mark(V.tensor_scalar(W1c[0:64, 64:128], W1c[0:64, 64:128], float(1.0 / np.sqrt(3.0)), None, ALU.mult))
    p.wait(m_w, mw3)
    XT3 = view(o_ring, 2, 512)
    YB = view(o_S, 4, 512)
    y_m = [None] * 4
    yss = [Slot(nc, f"ys{k}") for k in range(4)]
    x_rd = {}
    cp = {}
    for w in range(W + 1):
        if w < W:
            p.wait((v.sem, v.n) if w == 0 else None, bank_rd[w % 2])
            for k in range(4):
                src = H[:, w, 0:64] if k == 0 else H[:, w, 64:256].rearrange("p (i m) -> p m i", m=3)[:, k - 1]
                mm = P.matmul(bank[w % 2][0:64, k * 128:(k + 1) * 128], src, ident, start=True, stop=True)
            s.wait(p.mark(mm), x_rd.get(w - 2))
            cp[w] = bank_rd[w % 2] = s.mark(S.activation(XT3[0:64, w % 2, :], bank[w % 2][0:64, :], ACT.Copy))
        if w >= 1:
            u = w - 1
            bk = 2 + u % 2
            p.wait(cp[u], bank_rd[bk])
            for k in range(4):
                mm = P.matmul(bank[bk][:, k * 128:(k + 1) * 128], XT3[0:64, u % 2, k * 128:(k + 1) * 128],
                              (W0 if k == 0 else W1c)[0:64, :], start=True, stop=True)
            x_rd[u] = p.mark(mm)
            v.wait(x_rd[u], y_m[u % 4])
            bank_rd[bk] = v.mark(V.tensor_copy(YB[:, u % 4, :], bank[bk][:, :]))
            y.wait(bank_rd[bk])
            y_m[u % 4] = yss[u % 4].mark(SY.dma_start(YT[u * 128:(u + 1) * 128, :], YB[:, u % 4, :]))
    v.wait(v.mark(V.memset(ACC, 0.0)))
    fence(p, s, v, g)
    g.wait(*y_m)
    add = accumulate(256, wd_i)
    MSG = view(o_S, 2, 4, 256)
    T1 = view(o_S + 2048, 2, 4, 192)
    T2 = view(o_S + 3584, 2, 4, 192)
    pend = []
    rdm = [None, None]

    def tp(i, rows, oh, oht, mg, moh, moht):
        j = i % 2
        v.wait(*mg, rdm[j])
        s.wait(*mg, rdm[j])
        for k in range(4):
            r = rows[:, k, :].rearrange("p (m t o) -> p m t o", m=4, t=2)
            cc = PA[:, 4 * i + k, 2:6]
            ma = s.mark(S.activation(MSG[:, j, k, :].rearrange("p (m o) -> p m o", m=4), r[:, :, 0, :], ACT.Copy,
                                     scale=cc[:, 0:1]))
            c3 = cc[:, 1:4].unsqueeze(2).to_broadcast([128, 3, 64])
            v.mark(V.tensor_tensor(T1[:, j, k, :].rearrange("p (m o) -> p m o", m=3),
                                   r[:, 0:1, 1, :].to_broadcast([128, 3, 64]), c3, ALU.mult))
            mv = v.mark(V.tensor_tensor(T2[:, j, k, :].rearrange("p (m o) -> p m o", m=3), r[:, 1:4, 1, :], c3, ALU.mult))
        p.wait(ma, mv, moh)
        ms = []
        bks = [4 * (i % 2) + k for k in range(4)]
        for k in range(4):
            p.wait(bank_rd[bks[k]])
            o_ = oh[:, k * 128:(k + 1) * 128]
            P.matmul(bank[bks[k]][:, 0:256], o_, MSG[:, j, k, :], start=True, stop=False, skip_group_check=True)
            P.matmul(bank[bks[k]][:, 64:256], o_, T1[:, j, k, :], start=False, stop=False, skip_group_check=True)
            for m_ in range(3):
                mm = P.matmul(bank[bks[k]][:, 0:64], o_, T2[:, j, k, m_ * 64:(m_ + 1) * 64], start=False, stop=(m_ == 2),
                              skip_group_check=True)
            ms.append(p.mark(mm))
        rdm[j] = ms[3]
        pend.append((i, ms, bks))
        if len(pend) > 1:
            add(*pend.pop(0))
        return [ma, mv], [ms[3]], []
    edge_loop(YT, 512, isrc, locd, wd_i, o_q, 3, tp, None, False)
    add(*pend.pop(0))
    v.wait((v.sem, v.n))
    for w in range(W):
        v.mark(V.tensor_tensor(H[:, w, 0:64], H[:, w, 0:64], ACC[:, w, 0:64], ALU.add))
        hv = H[:, w, 64:256].rearrange("p (o m) -> p o m", m=3)
        v.mark(V.tensor_tensor(hv, hv, ACC[:, w, 64:256].rearrange("p (m o) -> p o m", m=3), ALU.add))
    v.wait((v.sem, v.n))
    m = norm_all(H)
    y.wait(m)
    fin = Slot(nc, "fin")
    fin.mark(SY.dma_start(out[0:3072, :].rearrange("(w p) f -> p w f", p=128), H[:, 0:24, :]))
    m = fin.mark(SY.dma_start(out[3072:NN, :], H[0:NN - 3072, 24, :]))
    y.wait(m)


def kernel(**inputs):
    import concourse.bacc as bacc
    from concourse.bass_utils import run_bass_kernel_spmd

    nc = bacc.Bacc("TRN2", target_bir_lowering=False, num_devices=1)
    arrays, aps = {}, {}
    for name, val in inputs.items():
        x = np.ascontiguousarray(val)
        if name == "edge_attr_10":
            name = "embT"
            x = np.concatenate([x, np.zeros((128 * C - NE, 10), x.dtype)])
            x = np.ascontiguousarray(x.reshape(128, C, 10).transpose(2, 1, 0).reshape(10, 128 * C))
        arrays["in_" + name] = x
        aps[name] = nc.dram_tensor("in_" + name, x.shape, mybir.dt.from_np(x.dtype), kind="ExternalInput").ap()
    out = nc.dram_tensor("out_0", [NN, 256], F, kind="ExternalOutput").ap()
    program(nc, aps, out)
    r = run_bass_kernel_spmd(nc, [arrays], core_ids=[0])
    return r.results[0]["out_0"]
```

```python
import numpy as np
import concourse.bass as bass
from concourse import mybir

F = mybir.dt.float32
I = mybir.dt.int32
BF = mybir.dt.bfloat16
ALU = mybir.AluOpType
ACT = mybir.ActivationFunctionType
AX = mybir.AxisListType.X

NN = 3125
NE = 50000
W = 25
NP = W * 128
C = 391
T = 416
G = T // 4
SB = 26
L = SB * 128
NEG = -1e38
PADKEY = -100000.0
KS = 4


class Queue:

    def __init__(self, nc, eng, name):
        self.eng = eng
        self.sem = nc.alloc_semaphore("done_" + name)
        self.n = 0
        self.seen = {}
        self.held = None

    def emit(self, fn):
        if self.held is None:
            fn()
        else:
            self.held.append(fn)

    def wait(self, *marks):
        for m in marks:
            if m is None:
                continue
            sem, v = m
            k = id(sem)
            if self.seen.get(k, 0) < v:
                self.emit(lambda sem=sem, v=v: self.eng.wait_ge(sem, v))
                self.seen[k] = v

    def mark(self, ins):
        if callable(ins):
            self.emit(lambda: ins().then_inc(self.sem, 1))
        else:
            ins.then_inc(self.sem, 1)
        self.n += 1
        return (self.sem, self.n)


class Slot:

    def __init__(self, nc, name):
        self.sem = nc.alloc_semaphore(name)
        self.n = 0

    def mark(self, ins, q=None):
        if callable(ins):
            q.emit(lambda: ins().then_inc(self.sem, 16))
        else:
            ins.then_inc(self.sem, 16)
        self.n += 16
        return (self.sem, self.n)


def program(nc, a, out, dbg=None, stop=99):
    v = Queue(nc, nc.vector, "dve")
    s = Queue(nc, nc.scalar, "act")
    p = Queue(nc, nc.tensor, "pe")
    g = Queue(nc, nc.gpsimd, "pool")
    y = Queue(nc, nc.sync, "sp")
    V, S, P, GP, SY = nc.vector, nc.scalar, nc.tensor, nc.gpsimd, nc.sync

    def dram(name, shape, dt=F):
        return nc.dram_tensor(name, shape, dt, kind="Internal").ap()

    top = [0]
    arena = nc.alloc_sbuf_tensor("arena", [128, 53200], F)

    def take(n):
        o = top[0]
        top[0] += (n + 7) // 8 * 8
        assert top[0] <= 53200, top[0]
        return o

    def view(o, *dims):
        n = int(np.prod(dims))
        ap = arena[:, o:o + n]
        if len(dims) == 1:
            return ap
        names = "abcd"[:len(dims)]
        return ap.rearrange("p (%s) -> p %s" % (" ".join(names), " ".join(names)),
                            **{names[i]: dims[i] for i in range(len(dims))})

    o_pa = take(T * 8)
    o_pb = take(T * 2)
    o_misc = take(4 * T + 1280)
    o_B = take(L + 8)
    o_S = take(T * 16)
    o_acc = take(W * 272)
    o_h = take(W * 256)
    o_q = take(W * 264)
    o_w = take(5640)
    o_ring = take(16 * 260)
    o_wv = take(2 * 4 * 272)
    o_oh = take(3 * 512)
    o_oht = take(3 * 256)
    o_sm = take(1200)

    PA = view(o_pa, T, 8)
    PB = view(o_pb, T, 2)
    mo = [o_misc]

    def misc(*dims, dt=F):
        ap = view(mo[0], *dims)
        mo[0] += int(np.prod(dims))
        assert mo[0] <= o_misc + 4 * T + 1280
        return ap if dt == F else ap.bitcast(dt)

    wd_i = misc(T, dt=I)
    ws_i = misc(T, dt=I)
    isrc = misc(T, dt=I)
    idst = misc(T, dt=I)
    ident = misc(128)
    iota = misc(128)
    ones = misc(128)
    tri = misc(128)
    sh_f = misc(128)
    sh_b = misc(128)
    g0 = misc(1)
    g1 = misc(1)
    a_bc = misc(1)
    pcol = misc(1)
    locd = misc(T)
    ident16 = misc(64, dt=BF)
    B = view(o_B, L + 1)
    SC = view(o_S, T, 16)
    ACC = view(o_acc, W, 272)
    H = view(o_h, W, 256)
    QT = view(o_q, W, 264)
    WV = view(o_wv, 2, 4 * 272)
    OH = view(o_oh, 3, 512)
    OHT = view(o_oht, 3, 256).bitcast(BF)
    OHB16 = view(o_oh, 3, 512)[:, :, 0:256].bitcast(BF)
    bank = [nc.alloc_psum_tensor(f"bank{i}", [128, 512], F) for i in range(8)]

    pre = Slot(nc, "pre")
    m = g.mark(GP.memset(ident, 0.0))
    g.mark(GP.memset(ones, 1.0))
    g.mark(GP.memset(tri, 1.0))
    g.mark(GP.memset(sh_f, 0.0))
    g.mark(GP.memset(sh_b, 0.0))
    g.mark(GP.memset(g0, 0.0))
    m = g.mark(GP.memset(g1, 0.0))
    g.wait(m)

    def sel(t, base, mult, op, fill, pat=[[-1, 128]]):
        return g.mark(GP.affine_select(out=t, in_=t, compare_op=op, fill=fill, base=base,
                                       pattern=pat, channel_multiplier=mult))
    sel(ident, 0, 1, ALU.not_equal, 1.0)
    sel(tri, 0, -1, ALU.is_gt, 0.0, [[1, 128]])
    sel(sh_f, 8, 1, ALU.not_equal, 1.0)
    sel(sh_b, -8, 1, ALU.not_equal, 1.0)
    sel(g0, -8, 1, ALU.is_ge, NEG, [[0, 1]])
    sel(g1, 119, -1, ALU.is_ge, NEG, [[0, 1]])
    m_i = g.mark(GP.iota(iota.bitcast(I), [[1, 128]], base=0, channel_multiplier=0))
    tstart = view(o_oht, T)
    g.mark(GP.iota(tstart.bitcast(I), [[128, T]], base=0, channel_multiplier=0))
    m_i = g.mark(GP.iota(pcol.bitcast(I), [[0, 1]], base=0, channel_multiplier=1))
    v.wait(m_i)
    v.mark(V.tensor_copy(iota, iota.bitcast(I)))
    v.mark(V.tensor_copy(tstart, tstart.bitcast(I)))
    m_const = v.mark(V.tensor_copy(pcol, pcol.bitcast(I)))
    v.mark(V.tensor_copy(ident16, ident))
    m_g = m_i

    OHB = view(o_acc, 25, C)
    FS = view(o_acc + 9776, 25, C)
    assert o_acc + 2 * 9776 <= o_w
    PW = view(o_S, C, 8)
    kf = view(o_S + 3128, C)
    posf = view(o_S + 3520, C)
    posi = view(o_S + 3912, C).bitcast(I)
    t1 = view(o_S + 4304, C)
    t1i = view(o_S + 4696, C).bitcast(I)
    rr = view(o_S + 5088, C)
    wf = view(o_S + 5480, T)
    code = view(o_pb, 392)
    poss = view(o_pb + 400, C).bitcast(I)
    small = o_sm
    lastF = view(small, 26)
    cnt = view(small + 32, 26)
    tot = view(small + 64, 26)
    base = view(small + 96, 27)
    off = view(small + 128, 26)
    basei = view(small + 160, 27).bitcast(I)
    ldc = Slot(nc, "ldc")
    srci = view(o_B, C).bitcast(I)
    dsti = view(o_B + 400, C).bitcast(I)
    dstn = view(o_B + 800, C).bitcast(I)
    at4 = view(o_B + 1200, C, 4)
    flag = view(o_B + 2900, 1).bitcast(I)
    viol = view(o_B + 2904, 1)
    fc1 = view(o_ring + 1100, 128)
    fc2 = view(o_ring + 1240, 2)

    m0 = v.mark(V.memset(srci, NP))
    m1 = v.mark(V.memset(dsti, NP))
    m1 = v.mark(V.memset(dstn, NP))
    m2 = v.mark(V.memset(at4, 0.0))
    v.mark(V.memset(fc1[0:20, :], 0.0))
    m3 = v.mark(V.memset(fc2, 0.0))
    y.wait(m1)
    tail = NE - 127 * C
    for t_, nm in ((dsti, "dst"), (srci, "src")):
        ldc.mark(SY.dma_start(t_[0:127, :], a[nm][0:127 * C].rearrange("(p c) -> p c", c=C)))
        ml = ldc.mark(SY.dma_start(t_[127:128, 0:tail], a[nm][127 * C:NE].rearrange("(o c) -> o c", o=1)))
    ldc.mark(SY.dma_start(dstn[0:127, :], a["dst"][1:127 * C + 1].rearrange("(p c) -> p c", c=C)))
    m_key = ldc.mark(SY.dma_start(dstn[127:128, 0:tail - 1], a["dst"][127 * C + 1:NE].rearrange("(o c) -> o c", o=1)))
    y.wait(m3)
    lda = Slot(nc, "lda")
    lda.mark(SY.dma_start(fc1[0:10, 0:64], a["L3_gnn_fc_w1"]))
    lda.mark(SY.dma_start(fc1[10:20, 64:128], a["L3_gnn_fc_w1"]))
    lda.mark(SY.dma_start(fc2[0:64, 0:1], a["L3_gnn_fc_w2"]))
    m_fc = lda.mark(SY.dma_start(fc2[64:128, 1:2], a["L3_gnn_fc_w2"]))

    v.wait(m_key)
    v.wait(v.mark(V.tensor_tensor(t1, dsti, dstn, ALU.is_gt)))
    mv = v.mark(V.tensor_reduce(viol, t1, AX, ALU.add))
    p.wait(mv, m_g, m_const)
    mp = p.mark(P.matmul(bank[7][:, 0:1], ones, viol, start=True, stop=True))
    v.wait(mp)
    m_flag = v.mark(V.tensor_copy(flag, bank[7][:, 0:1]))

    NCH = 10
    emb = [view(o_w + i * 2560, 2560) for i in range(2)]
    hid = [view(o_ring + i * 512, 512) for i in range(2)]
    es = [Slot(nc, f"emb{i}") for i in range(2)]
    m_emb, m_mm1, m_silu, m_r = {}, {}, {}, {}
    n_mm = 49

    def load_emb(i):
        if i >= 2:
            y.wait(m_mm1[5 * i - 6])
        n_ = min(2560, 25088 - i * 2560)
        m_emb[i] = es[i % 2].mark(SY.dma_start(emb[i % 2][0:20, 0:n_], a["embT"][:, i * 2560:i * 2560 + n_]))
    load_emb(0)
    load_emb(1)
    lda = Slot(nc, "ldt")
    lda.mark(SY.dma_start(a_bc, a["L2_gnn_a"].rearrange("(o k) -> o k", o=1).to_broadcast([128, 1])))
    y.wait(m2)
    lda.mark(SY.dma_start(at4[0:127], a["edge_attr_4"][0:127 * C, :].rearrange("(p c) k -> p c k", c=C)))
    m_at = lda.mark(SY.dma_start(at4[127:128, 0:tail, :],
                                 a["edge_attr_4"][127 * C:NE, :].rearrange("(o c) k -> o c k", o=1)))
    p.wait(m_fc)
    for i in range(n_mm + 1):
        if i < n_mm:
            if i >= 2:
                p.wait(m_silu[i - 2])
            p.wait(m_emb[i // 5])
            m_mm1[i] = p.mark(P.matmul(bank[i % 2][:, :], fc1[0:20, :],
                                       emb[(i // 5) % 2][0:20, (i % 5) * 512:(i % 5) * 512 + 512],
                                       start=True, stop=True))
            s.wait(m_mm1[i])
            if i >= 2:
                s.wait(m_r[i - 2])
            m_silu[i] = s.mark(S.activation(hid[i % 2], bank[i % 2][:, :], ACT.Silu,
                                            scale=float(np.float32(1) / np.float32(np.sqrt(10.0)))))
            if i % 5 == 4 and i // 5 + 2 < NCH:
                load_emb(i // 5 + 2)
        if i >= 1:
            j = i - 1
            p.wait(m_silu[j])
            for k in range(4):
                col_ = 8 * j + 2 * k
                mm = P.matmul(bank[2][:, col_:col_ + 2], hid[j % 2][:, k * 128:k * 128 + 128], fc2,
                              start=True, stop=True)
            m_r[j] = p.mark(mm)
    cst = float(1.0 / np.sqrt(128.0) * 1.679177 / 8.0 / 4.0)
    v.mark(V.tensor_copy(PW[:, :, 0], srci))
    v.mark(V.tensor_copy(PW[:, :, 1], dsti))
    v.mark(V.memset(PW[:, :, 6:8], 1.0))
    v.wait(v.mark(V.tensor_scalar(t1i, srci, 127, 12, ALU.bitwise_and, ALU.logical_shift_left)))
    v.mark(V.tensor_copy(code[:, 0:C], t1i))
    m_key = v.mark(V.memset(code[:, C:392], 0.0))
    v.wait(m_key)
    m_key = v.mark(V.scalar_tensor_tensor(code[:, 0:C], PW[:, :, 1], 1.0, code[:, 0:C], ALU.add, ALU.add))
    v.wait(m_key)

    def coefficients():
        v.wait(m_at, m_r[n_mm - 1])
        v.wait(v.mark(lambda: V.tensor_scalar(rr, bank[2][:, 0:C], cst, None, ALU.mult)))
        return v.mark(lambda: V.tensor_tensor(PW[:, :, 2:6], at4, rr.unsqueeze(2).to_broadcast([128, C, 4]), ALU.mult))

    def step(fn):
        v.wait(v.mark(fn))

    def buckets(nb, b0, dense_base, padded):
        m = None
        for b in range(nb):
            m = v.mark(lambda b=b: V.tensor_scalar(OHB[:, b, :], kf, float(b0 + b), None, ALU.is_equal))
        v.wait(m)
        of = OHB[:, 0:nb, :].rearrange("p b c -> p (b c)")
        ff = FS[:, 0:nb, :].rearrange("p b c -> p (b c)")
        step(lambda: V.tensor_tensor_scan(ff, of, of, 0.0, ALU.add, ALU.max))
        step(lambda: V.tensor_copy(lastF[:, 0:nb], FS[:, 0:nb, C - 1]))
        v.mark(lambda: V.tensor_copy(cnt[:, 0:1], lastF[:, 0:1]))
        mc = v.mark(lambda: V.tensor_tensor(cnt[:, 1:nb], lastF[:, 1:nb], lastF[:, 0:nb - 1], ALU.subtract))
        p.wait(mc)
        p.mark(lambda: P.matmul(bank[3][:, 0:nb], tri, cnt[:, 0:nb], start=True, stop=True))
        mp = p.mark(lambda: P.matmul(bank[4][:, 0:nb], ones, cnt[:, 0:nb], start=True, stop=True))
        v.wait(mp)
        if padded:
            step(lambda: V.tensor_scalar(tot[:, 0:nb], bank[4][:, 0:nb], 127.0, None, ALU.add))
            step(lambda: V.tensor_copy(basei[:, 0:nb], tot[:, 0:nb]))
            step(lambda: V.tensor_scalar(basei[:, 0:nb], basei[:, 0:nb], 7, 7,
                                         ALU.logical_shift_right, ALU.logical_shift_left))
            step(lambda: V.tensor_copy(tot[:, 0:nb], basei[:, 0:nb]))
        else:
            step(lambda: V.tensor_copy(tot[:, 0:nb], bank[4][:, 0:nb]))
        if dense_base is None:
            step(lambda: V.memset(base[:, 0:1], 0.0))
        else:
            step(lambda: V.tensor_copy(base[:, 0:1], dense_base))
        step(lambda: V.tensor_tensor_scan(base[:, 1:nb + 1], tot[:, 0:nb], tot[:, 0:nb], base[:, 0:1],
                                          ALU.add, ALU.max))
        step(lambda: V.tensor_tensor(off[:, 0:nb], base[:, 0:nb], bank[3][:, 0:nb], ALU.add))
        step(lambda: V.tensor_tensor(off[:, 1:nb], off[:, 1:nb], lastF[:, 0:nb - 1], ALU.subtract))
        step(lambda: V.tensor_scalar(off[:, 0:nb], off[:, 0:nb], -1.0, None, ALU.add))
        fb = FS[:, 0:nb, :]
        step(lambda: V.tensor_tensor(fb, fb, off[:, 0:nb].unsqueeze(2).to_broadcast([128, nb, C]), ALU.add))
        step(lambda: V.tensor_tensor(fb, fb, OHB[:, 0:nb, :], ALU.mult))
        step(lambda: V.tensor_reduce(t1, fb.rearrange("p b c -> p c b"), AX, ALU.add))
        step(lambda: V.tensor_tensor(posf, posf, t1, ALU.add))

    sct = [Slot(nc, f"sct{k}") for k in range(KS)]
    zs = Slot(nc, "zs")
    zs1 = Slot(nc, "zs1")
    rl = Slot(nc, "rl")
    sct1 = [Slot(nc, f"sct1{k}") for k in range(KS)]
    rl1 = Slot(nc, "rl1")

    def scatter(targets, rows, source, index, cols=range(C), sct=sct):
        for c in cols:
            k = c % KS
            if sct[k].n:
                g.wait((sct[k].sem, sct[k].n))
            sct[k].mark(lambda c=c, k=k: GP.indirect_dma_start(
                out=targets[k], out_offset=bass.IndirectOffsetOnAxis(ap=index[:, c:c + 1], axis=0),
                in_=source(c), in_offset=None, bounds_check=rows - 1, oob_is_err=False), g)
        return [(sct[k].sem, sct[k].n) for k in range(KS)]

    zero = view(o_wv, 2176)
    m_z = v.mark(V.memset(zero, 0.0))
    R1, R2 = 128 * C, 128 * T
    tg1 = [dram(f"sa{k}", [R1, 8]) for k in range(KS)]
    tg2 = [dram(f"sb{k}", [R2, 8]) for k in range(KS)]
    tg3 = [dram(f"sc{k}", [R2, 2]) for k in range(KS)]
    y.wait(m_z)

    def flat(t, ncol):
        return t.rearrange("(p c) k -> p (c k)", c=ncol)
    for k in range(KS):
        for h in range(2):
            zs.mark(SY.dma_start(flat(tg2[k], T)[:, h * 1664:(h + 1) * 1664], zero[:, 0:1664]))
        m_zs = zs.mark(SY.dma_start(flat(tg3[k], T), zero[:, 0:T * 2]))

    def reload(targets, ncol, lo, n, dst, marks, at, rl=rl):
        y.wait(*marks)
        parts = [view(at + k * n, n) for k in range(KS)]
        y.wait((v.sem, v.n))
        for k in range(KS):
            mm = rl.mark(lambda k=k: SY.dma_start(parts[k], flat(targets[k], ncol)[:, lo:lo + n]), y)
        v.wait(mm)
        v.mark(lambda: V.tensor_tensor(parts[0], parts[0], parts[1], ALU.add))
        step(lambda: V.tensor_tensor(parts[2], parts[2], parts[3], ALU.add))
        step(lambda: V.tensor_tensor(dst, parts[0], parts[2], ALU.add))

    def split_key(src_f, want_high):
        step(lambda: V.tensor_copy(t1i, src_f))
        if want_high:
            step(lambda: V.tensor_scalar(t1i, t1i, 7, None, ALU.logical_shift_right))
        else:
            step(lambda: V.tensor_scalar(t1i, t1i, 127, None, ALU.bitwise_and))
        step(lambda: V.tensor_copy(kf, t1i))

    def padded_rows(rows_):
        step(lambda: V.tensor_copy(t1i, posf))
        step(lambda: V.tensor_scalar(rows_, t1i, 127, None, ALU.bitwise_and))
        step(lambda: V.tensor_copy(t1, rows_))
        step(lambda: V.tensor_scalar(rows_, t1i, 7, None, ALU.logical_shift_right))
        step(lambda: V.tensor_copy(posf, rows_))
        step(lambda: V.scalar_tensor_tensor(posf, t1, float(T), posf, ALU.mult, ALU.add))
        step(lambda: V.tensor_scalar(kf, kf, float(W), 1e6, ALU.is_ge, ALU.mult))
        step(lambda: V.tensor_tensor(posf, posf, kf, ALU.add))
        return v.mark(lambda: V.tensor_copy(rows_, posf))

    def windows(wi):
        wide = view(o_acc, T, 24)
        step(lambda: V.tensor_tensor(wide, tstart.unsqueeze(2).to_broadcast([128, T, 24]),
                                     base[:, 1:25].unsqueeze(1).to_broadcast([128, T, 24]), ALU.is_ge))
        step(lambda: V.tensor_reduce(wf, wide, AX, ALU.add))
        step(lambda: V.tensor_copy(wi, wf))

    def first_pass():
        v.wait(coefficients())
        split_key(PW[:, :, 1], False)
        step(lambda: V.memset(posf, 0.0))
        carry = view(small + 230, 1)
        for b0 in range(0, 128, 25):
            n = min(25, 128 - b0)
            buckets(n, b0, carry if b0 else None, False)
            step(lambda n=n: V.tensor_copy(carry, base[:, n:n + 1]))
        mpos = v.mark(lambda: V.tensor_copy(posi, posf))
        for k in range(KS):
            zs1.mark(lambda k=k: SY.dma_start(flat(tg1[k], C)[:, 0:1664], zero[:, 0:1664]), y)
            mz = zs1.mark(lambda k=k: SY.dma_start(flat(tg1[k], C)[:, 1664:C * 8], zero[:, 0:C * 8 - 1664]), y)
        g.wait(mpos, mz)
        marks = scatter(tg1, R1, lambda c: PW[:, c, 0:8], posi, sct=sct1)
        reload(tg1, C, 0, C * 8, PW.rearrange("p c k -> p (c k)"), marks, o_acc, rl1)

    def conditional(part, queues):
        qs = queues
        before = {id(q): (q.n, dict(q.seen)) for q in qs}
        for q in qs:
            q.held = []
        part()
        for q in qs:
            held, q.held = q.held, None
            n0, seen = before[id(q)]
            q.seen = seen
            q.wait(m_flag)
            r = q.eng.alloc_register("unsorted")
            q.eng.reg_load(r, flag[0:1, 0:1])
            with q.eng.If_ne(r, 0):
                for fn in held:
                    fn()
            with q.eng.Else():
                if q.n > n0:
                    q.eng.wait_ge(q.sem, n0)
                    q.eng.sem_inc(q.sem, q.n - n0)
            q.eng.end_ifs()

    conditional(first_pass, [v, p, g, y])

    split_key(PW[:, :, 1], True)
    step(lambda: V.memset(posf, 0.0))
    buckets(25, 0, None, True)
    windows(wd_i)
    mpos = padded_rows(posi)

    def coefficients_sorted():
        v.wait(coefficients())
    v.wait(mpos)
    r_ = v.eng.alloc_register("in_order")
    v.eng.reg_load(r_, flag[0:1, 0:1])
    n0 = v.n
    seen0 = dict(v.seen)
    with v.eng.If_eq(r_, 0):
        coefficients_sorted()
    v.seen = seen0
    with v.eng.Else():
        v.eng.wait_ge(v.sem, n0)
        v.eng.sem_inc(v.sem, v.n - n0)
    v.eng.end_ifs()
    v.wait((v.sem, v.n), m_at, m_r[n_mm - 1])
    g.wait((v.sem, v.n), m_zs, m_at)
    marks2 = scatter(tg2, R2, lambda c: PW[:, c, 0:8], posi)
    kf_src = srci
    step(lambda: V.tensor_scalar(t1i, kf_src, 7, None, ALU.logical_shift_right))
    step(lambda: V.tensor_copy(kf, t1i))
    step(lambda: V.memset(posf, 0.0))
    buckets(25, 0, None, True)
    windows(ws_i)
    m_poss = padded_rows(poss)
    v.wait(m_poss)
    D8 = view(o_S, SB, 16, 8)

    def blocked(x):
        return x.rearrange("p (b j) k -> p j b k", j=SB)
    bank_rd = [None] * 8

    def to_scan(src, dst, m_src):
        p.wait(m_src)
        last = None
        for q in range(0, SB, 4):
            n = min(4, SB - q)
            bk = (q // 4) % 4
            p.wait(bank_rd[bk])
            for k in range(n):
                mm = P.matmul(bank[bk][:, k * 128:(k + 1) * 128],
                              src[:, (q + k) * 128:(q + k + 1) * 128],
                              ident, start=True, stop=True)
            s.wait(p.mark(mm))
            last = bank_rd[bk] = s.mark(S.activation(dst[:, q * 128:(q + n) * 128], bank[bk][:, 0:n * 128], ACT.Copy))
        return last

    def from_scan(src, m_src, use):
        p.wait(m_src)
        for j in range(SB):
            bk = j % 4
            p.wait(bank_rd[bk])
            mt = p.mark(P.matmul(bank[bk][:, 0:128], src[:, j * 128:(j + 1) * 128], ident, start=True, stop=True))
            bank_rd[bk] = use(j, bank[bk][:, 0:128], mt)

    rowA = view(o_sm + 256, 128)[0:1]
    rowAb = view(o_sm + 384, 128)[0:1]
    rowE = view(o_sm + 512, 128)[0:1]
    rowC = view(o_sm + 640, 128)[0:1]
    ccol = view(o_sm + 770, 1)
    def segment_max(SP, FB, BB, m_in):
        v.wait(m_in)
        for back in (False, True):
            dst = BB if back else FB
            st = B[:, 1:L + 1][:, ::-1] if back else B[:, 0:L]
            sp = SP[:, ::-1] if back else SP
            dv = dst[:, ::-1] if back else dst
            v.wait(v.mark(V.tensor_tensor_scan(dv, st, sp, NEG, ALU.add, ALU.max)))
            end = dst[:, 0:1] if back else dst[:, L - 1:L]
            p.wait((v.sem, v.n))
            mp = p.mark(P.matmul(bank[4][0:1, 0:128], end, ident, start=True, stop=True))
            v.wait(mp)
            v.wait(v.mark(V.tensor_copy(rowE, bank[4][0:1, 0:128])))
            row = rowAb if back else rowA
            prev = None
            order = range(15, -1, -1) if back else range(16)
            for b in order:
                cb = slice(b * 8, b * 8 + 8)
                if prev is None:
                    v.wait(v.mark(V.memset(rowC[:, cb], NEG)))
                else:
                    pb = slice(prev * 8, prev * 8 + 8)
                    v.wait(v.mark(V.tensor_tensor(rowC[:, cb], rowC[:, pb], row[:, pb], ALU.add)))
                    v.wait(v.mark(V.tensor_tensor(rowC[:, cb], rowC[:, cb], rowE[:, pb], ALU.max)))
                prev = b
            p.wait((v.sem, v.n))
            mp = p.mark(P.matmul(bank[4][:, 256:257], rowC, ones[0:1, 0:1], start=True, stop=True))
            v.wait(mp)
            v.wait(v.mark(V.tensor_copy(ccol, bank[4][:, 256:257])))
            v.wait(v.mark(V.tensor_tensor_scan(dv, st, sp, ccol, ALU.add, ALU.max)))
        return v.mark(V.tensor_tensor(FB, FB, BB, ALU.max))

    wl = Slot(nc, "wl")
    tb = Slot(nc, "tb")
    xs = Slot(nc, "xs")

    def all_done(*qs):
        return [(q.sem, q.n) for q in qs]

    def fence(*qs):
        ms = all_done(v, s, p, g)
        for q in qs:
            q.wait(*[m for m in ms if m[0] is not q.sem or q is not p])

    def load_w(ap, src):
        return wl.mark(SY.dma_start(ap, src))

    MS = view(o_sm + 256 + 520, 2 * W)
    RS = view(o_sm + 256 + 580, W)
    EP = view(o_sm + 256 + 610, 1)
    m_ep = v.mark(V.memset(EP, 1e-5))
    ST = view(o_sm + 960, 6 * W)

    def ln_stats(X):
        m = None
        for w in range(W):
            m = v.mark(V.bn_stats(ST[:, 6 * w:6 * w + 6], X[:, w, :]))
        v.wait(m)
        for w in range(W):
            m = v.mark(V.bn_aggr(MS[:, 2 * w:2 * w + 2], ST[:, 6 * w:6 * w + 6]))
        s.wait(m)
        ms = s.mark(S.activation(RS, MS.rearrange("p (w k) -> p w k", k=2)[:, :, 1], ACT.Sqrt, bias=EP))
        v.wait(m, ms)
        m = v.mark(V.reciprocal(RS, RS))
        v.wait(m)
        return m

    def normed(dst, src, w):
        return V.tensor_scalar(dst, src, MS[:, 2 * w:2 * w + 1], RS[:, w:w + 1], ALU.subtract, ALU.mult)

    XN = view(o_ring, 2, 256)
    XT = view(o_ring + 512, 2, 512)
    OUTB = view(o_ring + 1536, 2, 768)

    def transposed(n, get, after, gb=None):
        done = [None] * n
        cp = [None] * n

        def first(w):
            ap, m = get(w)
            p.wait(m, bank_rd[w % 2])
            for k in range(2):
                mm = P.matmul(bank[w % 2][:, k * 128:(k + 1) * 128], ap[:, k * 128:(k + 1) * 128], ident,
                              start=True, stop=True)
            mt = p.mark(mm)
            s.wait(mt)
            if w >= 2:
                s.wait(done[w - 2])
            for k in range(2):
                o = XT[:, w % 2, k * 128:(k + 1) * 128]
                i = bank[w % 2][:, k * 128:(k + 1) * 128]
                if gb is None:
                    cp[w] = s.mark(S.activation(o, i, ACT.Copy))
                else:
                    cp[w] = s.mark(S.activation(o, i, ACT.Identity, scale=gb[0][:, k:k + 1], bias=gb[1][:, k:k + 1]))
            bank_rd[w % 2] = cp[w]
            return mt
        mts = {}
        for w in range(n + 1):
            if w < n:
                mts[w] = first(w)
            if w >= 1:
                done[w - 1] = after(w - 1, XT[:, (w - 1) % 2, :], cp[w - 1])
        return mts, done

    def proj(xt, wt, cols, bk):
        for k in range(2):
            mm = P.matmul(bank[bk][:, 0:cols], xt[:, k * 128:(k + 1) * 128], wt[:, k, :], start=(k == 0), stop=(k == 1))
        return mm

    def rows_bc(ap1, n):
        return ap1.rearrange("(o n) -> o n", o=1).to_broadcast([128, n])

    def kview(ap):
        return ap.rearrange("(k p) n -> p k n", p=128)

    def col(ap1, k):
        return ap1.rearrange("(k p) -> p k", p=128)

    gs = [Slot(nc, f"gs{i}") for i in range(16)]

    def edge_loop(table, width, idx, loc, ring_o, ngrp, stages, lag, transposed_oh, oh_at=None):
        ring = view(ring_o, ngrp, 4, width)
        noh = 3 if oh_at is None else 6
        OH = view(o_oh if oh_at is None else oh_at, noh, 512)
        st = [{"rows": ring[:, i % ngrp], "oh": OH[:, i % noh, :], "oht": OHT[:, i % 3, :]} for i in range(G)]
        nst = len(stages)

        def gather(i):
            d = st[i]
            if i >= ngrp:
                g.wait(*st[i - ngrp]["rows_read"])
            d["g"] = []
            for k in range(4):
                sl = (i % ngrp) * 4 + k
                d["g"].append(gs[sl].mark(GP.indirect_dma_start(
                    out=ring[:, i % ngrp, k, :], out_offset=None, in_=table,
                    in_offset=bass.IndirectOffsetOnAxis(ap=idx[:, 4 * i + k:4 * i + k + 1], axis=0))))

        def onehot(i):
            d = st[i]
            if i >= noh:
                v.wait(*st[i - noh]["oh_read"])
            o = (OHB16 if transposed_oh is True else OH)[:, i % noh, :]
            d["moh"] = v.mark(V.tensor_tensor(
                o.rearrange("p (k n) -> p k n", k=4),
                loc[:, 4 * i:4 * i + 4].unsqueeze(2).to_broadcast([128, 4, 128]),
                iota.unsqueeze(1).to_broadcast([128, 4, 128]), ALU.is_equal))

        def transpose(i):
            d = st[i]
            p.wait(d["moh"], bank_rd[i % 2])
            src, idn = (OHB16, ident16) if transposed_oh is True else (OH, ident)
            for k in range(4):
                mm = P.matmul(bank[i % 2][:, k * 128:(k + 1) * 128], src[:, i % noh, k * 128:(k + 1) * 128],
                              idn, start=True, stop=True)
            mt = p.mark(mm)
            d["oh_read"] = [mt]
            s.wait(mt)
            if i >= 3:
                s.wait(*st[i - 3]["oht_read"])
            d["moht"] = bank_rd[i % 2] = s.mark(S.activation(OHT[:, i % 3, :], bank[i % 2][:, :], ACT.Copy))
        for i in range(min(ngrp, G)):
            gather(i)
        nx = 3 if transposed_oh else 1
        for i in range(nx):
            onehot(i)
        if transposed_oh:
            transpose(0)
        for it in range(G + nst - 1):
            if transposed_oh and it + 1 < G:
                transpose(it + 1)
            for k in range(nst):
                if 0 <= it - k < G:
                    stages[k](it - k, st[it - k])
            if it + nx < G:
                onehot(it + nx)
            j = it - lag + ngrp
            if ngrp <= j < G:
                gather(j)

    regs = {}

    def win(q, wi, i):
        k = id(q)
        if k not in regs:
            regs[k] = [q.eng.alloc_register(f"w{j}_{len(regs)}") for j in range(4)]
        q.eng.reg_load(regs[k], wi[0:1, 4 * i:4 * i + 4])
        return [q.eng.snap(r, min_val=0, max_val=W - 1) for r in regs[k]]

    def accumulate(width, wi):
        def add(i, d):
            marks, bks = d["ms"], d["bks"]
            ws = win(v, wi, i)
            res = []
            for k in range(4):
                v.wait(marks[k])
                if add.last:
                    v.wait(add.last)
                d = ACC[:, bass.ds(ws[k], 1), 0:width]
                add.last = v.mark(V.tensor_tensor(d, d, bank[bks[k]][:, 0:width].unsqueeze(1), ALU.add))
                bank_rd[bks[k]] = add.last
        add.last = None
        return add

    KT, VT = dram("KT", [NP, 256]), dram("VT", [NP, 256])
    X1T = dram("X1T", [NP, 72])
    XA = dram("XA", [NP, 256])
    MT = [dram(f"MT{i}", [NP, 260]) for i in range(4)]
    YT = dram("YT", [NP, 512])

    def load_x(dst):
        m = v.mark(V.memset(dst[:, 24, :], 0.0))
        y.wait(m)
        xs.mark(SY.dma_start(dst[:, 0:24, :], a["x"][0:3072, :].rearrange("(w p) f -> p w f", p=128)))
        return xs.mark(SY.dma_start(dst[0:NN - 3072, 24, :], a["x"][3072:NN, :]))

    WM = view(o_w, 5640)
    fence(y, v, s, p)
    w_in = WM[:, 0:512].rearrange("p (k n) -> p k n", k=2)
    b_bc = WM[:, 512:768]
    load_w(w_in, kview(a["L0_gnn_w_in"]))
    m_w = load_w(b_bc, rows_bc(a["L0_gnn_b_in"], 256))
    XX = view(o_acc, W, 256)
    mx = load_x(XX)
    p.wait(m_w)
    v.wait(m_w)

    def aft(w, xt, m):
        p.wait(m, bank_rd[2 + w % 2])
        mm = p.mark(proj(xt, w_in, 256, 2 + w % 2))
        v.wait(mm)
        bank_rd[2 + w % 2] = v.mark(V.tensor_tensor(H[:, w, :], bank[2 + w % 2][:, 0:256], b_bc, ALU.add))
        return mm
    transposed(W, lambda w: (XX[:, w, :], mx), aft)

    wq = WM[:, 0:512].rearrange("p (k n) -> p k n", k=2)
    wk = WM[:, 512:1024].rearrange("p (k n) -> p k n", k=2)
    wv = WM[:, 1024:1536].rearrange("p (k n) -> p k n", k=2)
    bq, bk_, bv = WM[:, 1536:1792], WM[:, 1792:2048], WM[:, 2048:2304]
    gb = WM[:, 2304:2312].rearrange("p (j k) -> p j k", k=2)
    wo = WM[:, 2320:2832].rearrange("p (k n) -> p k n", k=2)
    bo = WM[:, 2832:3088]
    w1 = WM[:, 0:2048].rearrange("p (k n) -> p k n", k=2)
    w2 = WM[:, 3328:5376].rearrange("p (k n) -> p k n", k=8)
    b1c = WM[:, 3088:3096]
    b2 = WM[:, 3096:3352 - 24] if False else WM[:, 5376:5632]
    scale = 1.0 / np.sqrt(32.0)
    Q3 = view(o_q, W, 2, 132).bitcast(BF)
    QL = view(o_acc, W, 132).bitcast(BF)
    QW = view(o_wv, 264)

    tbl = [Slot(nc, "tb0"), Slot(nc, "tb1")]
    st_out = [None, None]

    def load_and_project(l):
        fence(y, v, s, p)
        load_w(wq, kview(a["L0_gnn_wq"][l]))
        load_w(wk, kview(a["L0_gnn_wk"][l]))
        load_w(wv, kview(a["L0_gnn_wv"][l]))
        load_w(bq, rows_bc(a["L0_gnn_bq"][l], 256))
        load_w(bk_, rows_bc(a["L0_gnn_bk"][l], 256))
        load_w(bv, rows_bc(a["L0_gnn_bv"][l], 256))
        load_w(wo, kview(a["L0_gnn_wo"][l]))
        load_w(bo, rows_bc(a["L0_gnn_bo"][l], 256))
        with nc.allow_non_contiguous_dma(reason="small columns"):
            load_w(gb[:, 0, :], col(a["L0_gnn_ln1_g"][l], 2))
            load_w(gb[:, 1, :], col(a["L0_gnn_ln1_b"][l], 2))
            load_w(gb[:, 2, :], col(a["L0_gnn_ln2_g"][l], 2))
            load_w(gb[:, 3, :], col(a["L0_gnn_ln2_b"][l], 2))
            load_w(b1c, col(a["L0_gnn_b1"][l], 8))
        load_w(w2, a["L0_gnn_w2"][l].rearrange("(k p) n -> p k n", p=128))
        m_w = load_w(b2, rows_bc(a["L0_gnn_b2"][l], 256))
        ln_stats(H)
        s.wait(m_w)
        p.wait(m_w)
        v.wait(m_w)
        mts = {}

        def get(w):
            if w >= 2:
                v.wait(mts[w - 2])
            m = v.mark(normed(XN[:, w % 2, :], H[:, w, :], w))
            return XN[:, w % 2, :], m

        def aft(w, xt, m):
            o = OUTB[:, w % 2, :]
            p.wait(m)
            for k, (wt, bb) in enumerate(((wq, bq), (wk, bk_), (wv, bv))):
                bk = 2 + (3 * w + k) % 6
                p.wait(bank_rd[bk])
                mm = p.mark(proj(xt, wt, 256, bk))
                v.wait(mm)
                if k == 0:
                    v.wait(st_out[w % 2])
                bank_rd[bk] = v.mark(V.tensor_tensor(o[:, k * 256:(k + 1) * 256], bank[bk][:, 0:256], bb, ALU.add))
            v.wait(bank_rd[bk])
            mq = v.mark(V.tensor_scalar(QW[:, 0:256], o[:, 0:256], float(scale), None, ALU.mult))
            v.wait(mq)
            v.wait(v.mark(V.tensor_tensor(o[:, 0:256], QW[:, 0:256], o[:, 256:512], ALU.mult)))
            ml = v.mark(V.tensor_reduce(QW[:, 256:264], o[:, 0:256].rearrange("p (h d) -> p h d", d=32), AX, ALU.add))
            v.wait(ml)
            v.wait(v.mark(V.tensor_copy(Q3[:, w, 0, :], QW)))
            v.wait(v.mark(V.tensor_tensor(QW, QW, Q3[:, w, 0, :], ALU.subtract)))
            v.wait(v.mark(V.tensor_copy(Q3[:, w, 1, :], QW)))
            v.wait(v.mark(V.tensor_tensor(QL[:, w, :], QW, Q3[:, w, 1, :], ALU.subtract)))
            y.wait(ml)
            tbs = tbl[w % 2]
            tbs.mark(SY.dma_start(KT[w * 128:(w + 1) * 128, :], o[:, 256:512]))
            st_out[w % 2] = tbs.mark(SY.dma_start(VT[w * 128:(w + 1) * 128, :], o[:, 512:768]))
            return mm
        n_t, n_d = {}, {}

        done = [None] * W
        cp = [None] * W
        for w in range(W + 1):
            if w < W:
                ap, m = get(w)
                p.wait(m, bank_rd[w % 2])
                for k in range(2):
                    mm = P.matmul(bank[w % 2][:, k * 128:(k + 1) * 128], ap[:, k * 128:(k + 1) * 128], ident,
                                  start=True, stop=True)
                mts[w] = p.mark(mm)
                s.wait(mts[w])
                if w >= 2:
                    s.wait(done[w - 2])
                for k in range(2):
                    cp[w] = s.mark(S.activation(XT[:, w % 2, k * 128:(k + 1) * 128],
                                                bank[w % 2][:, k * 128:(k + 1) * 128], ACT.Identity,
                                                scale=gb[:, 0, k:k + 1], bias=gb[:, 1, k:k + 1]))
                bank_rd[w % 2] = cp[w]
            if w >= 1:
                done[w - 1] = aft(w - 1, XT[:, (w - 1) % 2, :], cp[w - 1])

    load_and_project(0)

    for h in range(2):
        reload(tg2, T, h * 1664, 1664, PA.rearrange("p c k -> p (c k)")[:, h * 1664:(h + 1) * 1664], marks2, o_S)
    wfl = view(o_oht, T)
    v.mark(V.tensor_copy(isrc, PA[:, :, 0]))
    v.mark(V.tensor_copy(wfl, wd_i))
    v.wait(v.mark(V.tensor_scalar(PA[:, :, 7], PA[:, :, 7], -PADKEY, PADKEY, ALU.mult, ALU.add)))
    v.wait(v.mark(V.tensor_tensor(PA[:, :, 1], PA[:, :, 1], PA[:, :, 7], ALU.add)))
    v.wait(v.mark(V.scalar_tensor_tensor(locd, wfl, -128.0, PA[:, :, 1], ALU.mult, ALU.add)))

    DS = view(o_S + L, L)
    md = v.mark(V.tensor_copy(D8, blocked(PA[:, :, 1:2].to_broadcast([128, T, 8]))))
    md = to_scan(view(o_S, L), DS, md)
    p.wait(md)
    mp = p.mark(P.matmul(bank[4][:, 0:1], sh_f, DS[:, L - 1:L], start=True, stop=True))
    v.wait(md, mp)
    v.mark(V.tensor_tensor(B[:, 1:L], DS[:, 1:L], DS[:, 0:L - 1], ALU.not_equal))
    v.wait(v.mark(V.tensor_tensor(B[:, 0:1], DS[:, 0:1], bank[4][:, 0:1], ALU.not_equal)))
    v.wait(v.mark(V.tensor_scalar(B[:, 0:L], B[:, 0:L], NEG, None, ALU.mult)))
    mb = v.mark(V.tensor_tensor(B[:, 0:1], B[:, 0:1], g0, ALU.add))
    p.wait(mb)
    mp = p.mark(P.matmul(bank[4][:, 0:1], sh_b, B[:, 0:1], start=True, stop=True))
    v.wait(mb, mp)
    v.wait(v.mark(V.tensor_tensor(B[:, L:L + 1], bank[4][:, 0:1], g1, ALU.add)))
    anyf = view(small + 240, 1)
    anyb = view(small + 241, 1)
    v.mark(V.tensor_reduce(anyf, B[:, 0:L], AX, ALU.min))
    m_any = v.mark(V.tensor_reduce(anyb, B[:, 1:L + 1], AX, ALU.min))
    FL = PA[:, :, 6]

    def put_flag(j, ps, mt):
        v.wait(mt)
        return v.mark(V.tensor_scalar(FL.rearrange("p (b j) -> p j b", j=SB)[:, j],
                                      ps.rearrange("p (b h) -> p b h", h=8)[:, :, 0],
                                      NEG / 2, None, ALU.is_lt))
    from_scan(B, m_any, put_flag)
    v.wait(bank_rd[0], bank_rd[1], bank_rd[2], bank_rd[3])

    p.wait((v.sem, v.n))
    P.matmul(bank[4][0:1, 0:128], anyf, ident, start=True, stop=True)
    mp = p.mark(P.matmul(bank[4][0:1, 128:256], anyb, ident, start=True, stop=True))
    v.wait(mp)
    v.mark(V.tensor_copy(rowA, bank[4][0:1, 0:128]))
    v.wait(v.mark(V.tensor_copy(rowAb, bank[4][0:1, 128:256])))


    for l in range(2):
        if l == 1:
            load_and_project(l)
        fence(v, s, p, g)
        g.wait(st_out[0], st_out[1])

        WV4 = [WV[:, j, :].rearrange("p (k f) -> p k f", k=4) for j in range(2)]

        def expand(i, d):
            ws = win(p, wd_i, i)
            d["ms"] = []
            d["bks"] = [2 + (4 * i + k) % 6 for k in range(4)]
            for k in range(4):
                bk = d["bks"][k]
                p.wait(d["moht"], bank_rd[bk])
                lhs = d["oht"][:, k * 128:(k + 1) * 128]
                P.matmul(bank[bk][:, 0:264], lhs, Q3[:, bass.ds(ws[k], 1), 0, :], start=True, stop=False)
                P.matmul(bank[bk][:, 0:264], lhs, Q3[:, bass.ds(ws[k], 1), 1, :], start=False, stop=False)
                d["ms"].append(p.mark(P.matmul(bank[bk][:, 0:264], lhs, QL[:, bass.ds(ws[k], 1), :],
                                               start=False, stop=True)))
            d["oht_read"] = [d["ms"][3]]

        def scores(i, d):
            tmp = WV4[i % 2]
            for k in range(4):
                bk = d["bks"][k]
                v.wait(d["ms"][k], d["g"][k])
                mv = v.mark(V.tensor_tensor(tmp[:, k, 0:256], d["rows"][:, k, :], bank[bk][:, 0:256], ALU.mult))
                s.wait(d["ms"][k], mv)
                bank_rd[bk] = s.mark(S.activation(SC[:, 4 * i + k, 8:16], bank[bk][:, 256:264], ACT.Copy))
            d["rows_read"] = [mv]
            v.wait(mv)
            v.mark(V.tensor_reduce(SC[:, 4 * i:4 * i + 4, 0:8],
                                   tmp[:, :, 0:256].rearrange("p k (h d) -> p k h d", d=32), AX, ALU.add))

        def both(i, d):
            expand(i, d)
            scores(i, d)
        edge_loop(KT, 256, isrc, locd, o_ring, 4, [both], 0, True)
        SP8 = view(o_q, SB, 16, 8)
        fence(v, s, p)
        mm = v.mark(V.tensor_tensor(SP8, blocked(SC[:, :, 0:8]), blocked(SC[:, :, 8:16]), ALU.max))
        SPs, FB, BB = view(o_acc, L), view(o_acc + L, L), view(o_q, L)
        mm = to_scan(view(o_q, L), SPs, mm)
        v.wait(*all_done(p))
        mm = segment_max(SPs, FB, BB, mm)

        def put_m(j, ps, mt):
            v.wait(mt)
            d = SC.rearrange("p (b j) k -> p j b k", j=SB)[:, j]
            pv = ps.rearrange("p (b h) -> p b h", h=8)
            v.mark(V.tensor_tensor(d[:, :, 0:8], d[:, :, 0:8], pv, ALU.subtract))
            return v.mark(V.tensor_tensor(d[:, :, 8:16], d[:, :, 8:16], pv, ALU.subtract))
        from_scan(FB, mm, put_m)
        s.wait(bank_rd[0], bank_rd[1], bank_rd[2], bank_rd[3])
        me = s.mark(S.activation(SC, SC, ACT.Exp))
        v.wait(me)
        v.mark(V.tensor_tensor(SC[:, :, 8:16], SC[:, :, 8:16], FL.unsqueeze(2).to_broadcast([128, T, 8]), ALU.mult))
        m_acc0 = v.mark(V.memset(ACC, 0.0))
        v.wait(m_acc0)
        fence(p, v, g, s)
        add = accumulate(272, wd_i)

        def weigh(i, d):
            j = i % 2
            w_ = WV4[j]
            v.wait(*d["g"], rdwv[j])
            s.wait(rdwv[j])
            mc = s.mark(S.activation(w_[:, :, 256:272], SC[:, 4 * i:4 * i + 4, :], ACT.Copy))
            mw = v.mark(V.tensor_tensor(w_[:, :, 0:256].rearrange("p k (h d) -> p k h d", d=32),
                                        d["rows"].rearrange("p k (h d) -> p k h d", d=32),
                                        SC[:, 4 * i:4 * i + 4, 0:8].unsqueeze(3).to_broadcast([128, 4, 8, 32]), ALU.mult))
            d["rows_read"] = [mw]
            p.wait(mw, mc, d["moh"])
            d["ms"] = []
            d["bks"] = [4 * (i % 2) + k for k in range(4)]
            for k in range(4):
                bk = d["bks"][k]
                p.wait(bank_rd[bk])
                d["ms"].append(p.mark(P.matmul(bank[bk][:, 0:272], d["oh"][:, k * 128:(k + 1) * 128], w_[:, k, :],
                                               start=True, stop=True)))
            rdwv[j] = d["ms"][3]
            d["oh_read"] = [rdwv[j]]
        rdwv = [None, None]
        edge_loop(VT, 256, isrc, locd, o_ring, 4, [weigh, add], 0, False)

        g.wait(m_poss, m_zs)
        marks3 = scatter(tg3, R2, lambda c: code[:, c:c + 2], poss, (range(0, 240), range(240, C))[l])

        fence(v, s, p, y)
        VB = view(o_q, 4, 256)
        vb_s = [Slot(nc, f"vb{l}{k}") for k in range(4)]
        AG = XN
        rz = view(o_sm + 1112, 8)
        lv = {}

        def ldv(w):
            if w >= 4:
                y.wait(cons[w - 4])
            lv[w] = vb_s[w % 4].mark(SY.dma_start(VB[:, w % 4, :], VT[w * 128:(w + 1) * 128, :]))
        cons = {}
        ldv(0)
        ldv(1)
        ldv(2)
        mts = {}
        done = [None] * W
        cp = [None] * W
        for w in range(W + 1):
            if w < W:
                if w + 3 < W:
                    ldv(w + 3)
                hd = "p (h d) -> p h d"
                v.wait(lv[w])
                if w >= 2:
                    v.wait(mts[w - 2])
                ag = AG[:, w % 2, :]
                v.mark(V.tensor_tensor(rz, ACC[:, w, 256:264], ACC[:, w, 264:272], ALU.add))
                ma = v.mark(V.tensor_tensor(ag.rearrange(hd, d=32), VB[:, w % 4, :].rearrange(hd, d=32),
                                            ACC[:, w, 264:272].unsqueeze(2).to_broadcast([128, 8, 32]), ALU.mult))
                cons[w] = ma
                v.wait(ma)
                v.mark(V.tensor_tensor(ag, ag, ACC[:, w, 0:256], ALU.add))
                v.wait(v.mark(V.tensor_scalar(rz, rz, 1e-30, None, ALU.max)))
                v.wait(v.mark(V.reciprocal(rz, rz)))
                m = v.mark(V.tensor_tensor(ag.rearrange(hd, d=32), ag.rearrange(hd, d=32),
                                           rz.unsqueeze(2).to_broadcast([128, 8, 32]), ALU.mult))
                v.wait(m)
                p.wait(m, bank_rd[w % 2])
                for k in range(2):
                    mm = P.matmul(bank[w % 2][:, k * 128:(k + 1) * 128], ag[:, k * 128:(k + 1) * 128], ident,
                                  start=True, stop=True)
                mts[w] = p.mark(mm)
                s.wait(mts[w])
                if w >= 2:
                    s.wait(done[w - 2])
                cp[w] = bank_rd[w % 2] = s.mark(S.activation(XT[:, w % 2, 0:256], bank[w % 2][:, 0:256], ACT.Copy))
            if w >= 1:
                u = w - 1
                p.wait(cp[u], bank_rd[2 + u % 2])
                done[u] = p.mark(proj(XT[:, u % 2, :], wo, 256, 2 + u % 2))
                v.wait(done[u])
                v.mark(V.tensor_tensor(H[:, u, :], H[:, u, :], bo, ALU.add))
                v.wait((v.sem, v.n))
                bank_rd[2 + u % 2] = v.mark(V.tensor_tensor(H[:, u, :], H[:, u, :], bank[2 + u % 2][:, 0:256], ALU.add))
        v.wait((v.sem, v.n))
        fence(y, v, s, p)
        m_w1 = load_w(w1, kview(a["L0_gnn_w1"][l]))
        ln_stats(H)
        p.wait(m_w1)
        XT4 = view(o_acc, 2, 2, 512)
        HT = view(o_acc + 2048, 8, 512)
        XN8 = view(o_q, 8, 256)
        ht_rd = None
        xn_rd = {}
        for gr in range(7):
            ws_ = list(range(gr * 4, min(gr * 4 + 4, W)))
            n = len(ws_) * 128
            for w in ws_:
                if w >= 8:
                    v.wait(xn_rd[w - 8])
                m = v.mark(normed(XN8[:, w % 8, :], H[:, w, :], w))
                bk = w % 2
                p.wait(m, bank_rd[bk])
                for k in range(2):
                    mm = P.matmul(bank[bk][:, k * 128:(k + 1) * 128], XN8[:, w % 8, k * 128:(k + 1) * 128], ident,
                                  start=True, stop=True)
                xn_rd[w] = p.mark(mm)
                s.wait(xn_rd[w])
                for k in range(2):
                    mc = s.mark(S.activation(XT4[:, gr % 2, k, (w % 4) * 128:(w % 4) * 128 + 128],
                                             bank[bk][:, k * 128:(k + 1) * 128], ACT.Identity,
                                             scale=gb[:, 2, k:k + 1], bias=gb[:, 3, k:k + 1]))
                bank_rd[bk] = mc
            p.wait(mc)
            mh = []
            for j in range(8):
                bk = 2 + j % 4
                p.wait(bank_rd[bk])
                for k in range(2):
                    mm = P.matmul(bank[bk][:, 0:n], w1[:, k, j * 128:(j + 1) * 128], XT4[:, gr % 2, k, 0:n],
                                  start=(k == 0), stop=(k == 1))
                s.wait(p.mark(mm), ht_rd)
                mc = s.mark(S.activation(HT[:, j, 0:n], bank[bk][:, 0:n], ACT.Gelu, bias=b1c[:, j:j + 1]))
                bank_rd[bk] = mc
                mh.append(mc)
            for w in ws_:
                bk = 6 + w % 2
                p.wait(bank_rd[bk])
                for j in range(8):
                    p.wait(mh[j])
                    mm = P.matmul(bank[bk][:, 0:256], HT[:, j, (w % 4) * 128:(w % 4) * 128 + 128], w2[:, j, :],
                                  start=(j == 0), stop=(j == 7))
                ht_rd = p.mark(mm)
                v.wait(ht_rd)
                v.wait(v.mark(V.tensor_tensor(H[:, w, :], H[:, w, :], b2, ALU.add)))
                bank_rd[bk] = v.mark(V.tensor_tensor(H[:, w, :], H[:, w, :], bank[bk][:, 0:256], ALU.add))
        v.wait((v.sem, v.n))

    def norm_all(X):
        ln_stats(X)
        for w in range(W):
            m = v.mark(normed(X[:, w, :], X[:, w, :], w))
        v.wait(m)
        return m

    fence(y, v)
    XX = view(o_q, W, 256)
    mx = load_x(XX)
    v.wait(mx)
    v.wait(v.mark(V.tensor_tensor(H, H, XX, ALU.add)))
    norm_all(H)

    def dump(ap, m):
        dd = Slot(nc, "dbgx")
        y.wait(*all_done(v, s, p), m)
        y.wait(dd.mark(SY.dma_start(dbg["H"].rearrange("(w p) f -> p w f", p=128), ap)))
    if dbg is not None and stop == 1:
        dump(H, None)
        return

    fence(y, s, p, v)
    T2 = view(o_q + 3328, T, 2)
    reload(tg3, T, 0, 2 * T, T2.rearrange("p c k -> p (c k)"), marks3, o_q)
    wsf = view(o_q + 4200, T)
    ti = view(o_q + 4700, T).bitcast(I)
    tv = view(o_q + 5200, T)
    step(lambda: V.tensor_scalar(tv, T2[:, :, 0], -1.0, 0.0, ALU.add, ALU.max))
    step(lambda: V.tensor_copy(ti, tv))
    step(lambda: V.tensor_scalar(idst, ti, 4095, None, ALU.bitwise_and))
    step(lambda: V.tensor_scalar(ti, ti, 12, None, ALU.logical_shift_right))
    step(lambda: V.tensor_copy(tv, ti))
    step(lambda: V.tensor_scalar(wsf, T2[:, :, 0], 1.0, PADKEY, ALU.is_lt, ALU.mult))
    step(lambda: V.tensor_tensor(PB[:, :, 1], tv, wsf, ALU.add))
    W1_ = WM[:, 0:128].rearrange("p (k n) -> p k n", k=2)
    wlr = WM[:, 128:136]
    b_1 = WM[:, 144:208]
    load_w(W1_, kview(a["L1_gnn_W"]))
    with nc.allow_non_contiguous_dma(reason="small transposed weights"):
        load_w(wlr[0:64, 0:4], a["L1_gnn_Wl"].rearrange("h o -> o h"))
        load_w(wlr[0:64, 4:8], a["L1_gnn_Wr"].rearrange("h o -> o h"))
    m_w = load_w(b_1, rows_bc(a["L1_gnn_b"], 64))
    p.wait(m_w)
    v.wait(m_w)
    EL = view(o_q, W, 4)
    X1 = view(o_q + 128, 4, 72)
    X1c = view(o_q + 512, 4, 128)
    mz = v.mark(V.memset(X1, 0.0))
    st4 = [Slot(nc, f"x1s{k}") for k in range(4)]
    st_m = [None] * 4
    m_h = (v.sem, v.n)
    x1t_rd = {}

    def aft(w, xt, m):
        p.wait(m, bank_rd[2 + w % 2])
        bkk = bank[2 + w % 2]
        proj(xt, W1_, 64, 2 + w % 2)
        for k in range(2):
            mm = P.matmul(bkk[0:64, 128:256], W1_[:, k, :], xt[:, k * 128:(k + 1) * 128], start=(k == 0), stop=(k == 1))
        mm = p.mark(mm)
        s.wait(mm)
        if w >= 4:
            s.wait(x1t_rd[w - 4])
        mc = s.mark(S.activation(X1c[0:64, w % 4, :], bkk[0:64, 128:256], ACT.Copy))
        p.wait(mc, bank_rd[4 + w % 2])
        x1t_rd[w] = p.mark(P.matmul(bank[4 + w % 2][:, 0:8], X1c[0:64, w % 4, :], wlr[0:64, :], start=True, stop=True))
        v.wait(mz, st_m[w % 4], x1t_rd[w])
        bank_rd[2 + w % 2] = v.mark(V.tensor_copy(X1[:, w % 4, 0:64], bkk[:, 0:64]))
        v.mark(V.tensor_copy(X1[:, w % 4, 64:68], bank[4 + w % 2][:, 4:8]))
        bank_rd[4 + w % 2] = v.mark(V.tensor_copy(EL[:, w, :], bank[4 + w % 2][:, 0:4]))
        y.wait(bank_rd[4 + w % 2])
        st_m[w % 4] = st4[w % 4].mark(SY.dma_start(X1T[w * 128:(w + 1) * 128, :], X1[:, w % 4, :]))
        return mm
    transposed(W, lambda w: (H[:, w, :], m_h), aft)
    v.wait(v.mark(V.memset(ACC, 0.0)))
    fence(p, s, v, g)
    g.wait(*st_m)
    locs = PB[:, :, 1]
    E4 = view(o_q + 1100, 3, 16)
    Z4 = view(o_q + 1160, 3, 16)
    EL3 = view(o_q + 1220, W, 6).bitcast(BF).rearrange("p w (c h) -> p w c h", c=3)
    v.wait((v.sem, v.n))
    v.wait(v.mark(V.tensor_copy(EL3[:, :, 0, :], EL)))
    v.wait(v.mark(V.tensor_tensor(EL, EL, EL3[:, :, 0, :], ALU.subtract)))
    v.wait(v.mark(V.tensor_copy(EL3[:, :, 1, :], EL)))
    v.wait(v.mark(V.tensor_tensor(EL3[:, :, 2, :], EL, EL3[:, :, 1, :], ALU.subtract)))
    p.wait((v.sem, v.n))
    add = accumulate(260, ws_i)
    rdwv = [None, None]
    rde = [None, None, None]

    def logits(i, d):
        j = i % 2
        ws = win(p, ws_i, i)
        p.wait(d["moht"], bank_rd[2 + j])
        for k in range(4):
            mm = P.matmul(bank[2 + j][:, 12 * k:12 * k + 12], d["oht"][:, k * 128:(k + 1) * 128],
                          EL3[:, bass.ds(ws[k], 1), :, :], start=True, stop=True)
        mel = p.mark(mm)
        d["oht_read"] = [mel]
        j3 = i % 3
        v.wait(mel, *d["g"], rde[j3])
        z, e = Z4[:, j3, :], E4[:, j3, :]
        z3 = z.rearrange("p (k h) -> p k h", h=4)
        bank_rd[2 + j] = m = v.mark(V.tensor_reduce(
            z3, bank[2 + j][:, 0:48].rearrange("p (k c h) -> p k h c", k=4, c=3), AX, ALU.add))
        v.wait(m)
        m = v.mark(V.tensor_tensor(z3, z3, d["rows"][:, :, 64:68], ALU.add))
        v.wait(m)
        m = v.mark(V.scalar_tensor_tensor(z, z, 0.2, z, ALU.mult, ALU.max))
        s.wait(m, rde[j3])
        d["me"] = s.mark(S.activation(e, z, ACT.Exp))

    def weigh1(i, d):
        j = i % 2
        e = E4[:, i % 3, :]
        w_ = WV[:, j, :].rearrange("p (k f) -> p k f", k=4)
        v.wait(d["me"], rdwv[j])
        s.wait(rdwv[j], d["me"])
        mc = s.mark(S.activation(w_[:, :, 256:260], e.rearrange("p (k h) -> p k h", h=4), ACT.Copy))
        for k in range(4):
            mw = v.mark(V.tensor_tensor(w_[:, k, 0:256].rearrange("p (h d) -> p h d", h=4),
                                        d["rows"][:, k, 0:64].unsqueeze(1).to_broadcast([128, 4, 64]),
                                        e[:, 4 * k:4 * k + 4].unsqueeze(2).to_broadcast([128, 4, 64]), ALU.mult))
        d["rows_read"] = [mw]
        rde[i % 3] = mw
        d["mw"] = [mw, mc]

    def gather1(i, d):
        p.wait(*d["mw"], d["moh"])
        d["ms"] = []
        d["bks"] = [4, 5, 6, 7]
        j = i % 2
        w_ = WV[:, j, :].rearrange("p (k f) -> p k f", k=4)
        for k in range(4):
            p.wait(bank_rd[4 + k])
            d["ms"].append(p.mark(P.matmul(bank[4 + k][:, 0:260], d["oh"][:, k * 128:(k + 1) * 128], w_[:, k, 0:260],
                                           start=True, stop=True)))
        rdwv[j] = d["ms"][3]
        d["oh_read"] = [rdwv[j]]

    d1 = {}

    def add_gather(i, d):
        if i:
            add(i - 1, d1[i - 1])
        d1[i] = d
        gather1(i, d)
    edge_loop(X1T, 72, idst, locs, o_ring, 4, [logits, weigh1, add_gather], 1, "both", oh_at=o_q + 2048)
    add(G - 1, d1[G - 1])
    fence(v, s)
    hd = "p (h d) -> p h d"
    TA = view(o_ring, 4, 256)
    rs4 = view(o_sm + 1112, 4)
    ex_m = {}
    for w in range(W):
        t = TA[:, w % 4, :]
        v.wait(v.mark(V.tensor_scalar(rs4, ACC[:, w, 256:260], 1e-12, None, ALU.max)))
        v.wait(v.mark(V.reciprocal(rs4, rs4)))
        av = ACC[:, w, 0:256].rearrange(hd, d=64)
        v.wait(v.mark(V.tensor_tensor(av, av, rs4.unsqueeze(2).to_broadcast([128, 4, 64]), ALU.mult)))
        v.wait(v.mark(V.tensor_tensor(av, av, b_1.unsqueeze(1).to_broadcast([128, 4, 64]), ALU.add)))
        m = v.mark(V.tensor_scalar(t, ACC[:, w, 0:256], 0.0, None, ALU.min))
        s.wait(m)
        me = s.mark(S.activation(t, t, ACT.Exp))
        v.mark(V.scalar_tensor_tensor(H[:, w, :], ACC[:, w, 0:256], 0.0, H[:, w, :], ALU.max, ALU.add))
        v.wait(me, (v.sem, v.n))
        v.mark(V.scalar_tensor_tensor(H[:, w, :], t, -1.0, H[:, w, :], ALU.add, ALU.add))
    v.wait((v.sem, v.n))
    norm_all(H)
    if dbg is not None and stop == 2:
        dump(H, None)
        return

    fence(y, s, p, v)
    WA = WM[:, 0:512].rearrange("p (k n) -> p k n", k=2)
    WB = WM[:, 512:1024].rearrange("p (k n) -> p k n", k=2)
    b1_, b2_ = WM[:, 1024:1280], WM[:, 1280:1536]
    load_w(WA, kview(a["L2_gnn_W1"]))
    load_w(WB, kview(a["L2_gnn_W2"]))
    load_w(b1_, rows_bc(a["L2_gnn_b1"], 256))
    m_w = load_w(b2_, rows_bc(a["L2_gnn_b2"], 256))
    p.wait(m_w)
    v.wait(m_w)
    ST8 = view(o_q, 8, 260)
    sts = [Slot(nc, f"st{k}") for k in range(8)]
    st_m = [None] * 8
    HX = view(o_S, W, 256)

    def to_table(dst, src, wt):
        v.wait(*st_m)
        mst = v.mark(V.memset(ST8, 1.0))
        m_h = (v.sem, v.n)

        def aft(w, xt, m):
            p.wait(m, bank_rd[2 + w % 2])
            mm = p.mark(proj(xt, wt, 256, 2 + w % 2))
            v.wait(mm, mst, st_m[w % 8])
            bank_rd[2 + w % 2] = v.mark(V.tensor_copy(ST8[:, w % 8, 0:256], bank[2 + w % 2][:, 0:256]))
            y.wait(bank_rd[2 + w % 2])
            st_m[w % 8] = sts[w % 8].mark(SY.dma_start(dst[w * 128:(w + 1) * 128, :], ST8[:, w % 8, :]))
            return mm
        transposed(W, lambda w: (src[:, w, :], m_h), aft)

    def hop(table, idx, loc, wi):
        v.wait(v.mark(V.memset(ACC, 0.0)))
        fence(p, s, v, g)
        g.wait(*st_m)
        add = accumulate(257, wi)

        def body(i, d):
            d["ms"] = []
            d["bks"] = [4 * (i % 2) + k for k in range(4)]
            p.wait(d["moh"])
            for k in range(4):
                bk = d["bks"][k]
                p.wait(bank_rd[bk], d["g"][k])
                d["ms"].append(p.mark(P.matmul(bank[bk][:, 0:257], d["oh"][:, k * 128:(k + 1) * 128],
                                               d["rows"][:, k, 0:257], start=True, stop=True)))
            d["rows_read"] = d["oh_read"] = [d["ms"][3]]
        edge_loop(table, 260, idx, loc, o_ring, 4, [body, add], 0, False)
        v.wait((v.sem, v.n))
        v.wait(v.mark(V.tensor_scalar(ACC[:, :, 256:257], ACC[:, :, 256:257], 1.0, None, ALU.max)))
        v.wait(v.mark(V.reciprocal(ACC[:, :, 256:257], ACC[:, :, 256:257])))
        v.wait(v.mark(V.tensor_tensor(ACC[:, :, 0:256], ACC[:, :, 0:256],
                                      ACC[:, :, 256:257].to_broadcast([128, W, 256]), ALU.mult)))

    def prelu(dst, src, tmp):
        v.wait(v.mark(V.tensor_scalar(tmp, src, 0.0, a_bc, ALU.min, ALU.mult)))
        v.wait(v.mark(V.scalar_tensor_tensor(dst, src, 0.0, tmp, ALU.max, ALU.add)))

    for r in range(2):
        to_table(MT[2 * r], H if r == 0 else HX, WA if r == 0 else WB)
        hop(MT[2 * r], isrc, locd, wd_i)
        m = v.mark(V.memset(ACC[:, :, 256:260], 1.0))
        y.wait(m)
        st_m[0] = sts[0].mark(SY.dma_start(MT[2 * r + 1].rearrange("(w p) f -> p w f", p=128), ACC[:, :, 0:260]))
        v.wait(st_m[0])
        hop(MT[2 * r + 1], idst, locs, ws_i)
        bb = b1_ if r == 0 else b2_
        v.wait(v.mark(V.tensor_tensor(HX, ACC[:, :, 0:256], bb.unsqueeze(1).to_broadcast([128, W, 256]), ALU.add)))
        if r == 1:
            v.wait(v.mark(V.tensor_tensor(HX, HX, H, ALU.add)))
        prelu(HX, HX, view(o_q, W, 256))
    v.wait(v.mark(V.tensor_tensor(H, H, HX, ALU.add)))
    norm_all(H)
    if dbg is not None and stop == 3:
        dump(H, None)
        return

    fence(y, s, p, v)
    W0 = WM[:, 0:128]
    W1c = WM[:, 128:256]
    load_w(W0[0:64, 0:64], a["L3_gnn_w_00_0"])
    load_w(W0[0:64, 64:128], a["L3_gnn_w_01_1"])
    load_w(W1c[0:64, 0:64], a["L3_gnn_w_10_1"])
    m_w = load_w(W1c[0:64, 64:128], a["L3_gnn_w_11_0"])
    v.wait(m_w)
    mw3 = v.mark(V.tensor_scalar(W1c[0:64, 64:128], W1c[0:64, 64:128], float(1.0 / np.sqrt(3.0)), None, ALU.mult))
    p.wait(m_w, mw3)
    XT3 = view(o_ring, 2, 512)
    YB = view(o_S, 4, 512)
    y_m = [None] * 4
    yss = [Slot(nc, f"ys{k}") for k in range(4)]
    x_rd = {}
    cp = {}
    for w in range(W + 1):
        if w < W:
            p.wait((v.sem, v.n) if w == 0 else None, bank_rd[w % 2])
            for k in range(4):
                src = H[:, w, 0:64] if k == 0 else H[:, w, 64:256].rearrange("p (i m) -> p m i", m=3)[:, k - 1]
                mm = P.matmul(bank[w % 2][0:64, k * 128:(k + 1) * 128], src, ident, start=True, stop=True)
            s.wait(p.mark(mm), x_rd.get(w - 2))
            cp[w] = bank_rd[w % 2] = s.mark(S.activation(XT3[0:64, w % 2, :], bank[w % 2][0:64, :], ACT.Copy))
        if w >= 1:
            u = w - 1
            bk = 2 + u % 2
            p.wait(cp[u], bank_rd[bk])
            for k in range(4):
                mm = P.matmul(bank[bk][:, k * 128:(k + 1) * 128], XT3[0:64, u % 2, k * 128:(k + 1) * 128],
                              (W0 if k == 0 else W1c)[0:64, :], start=True, stop=True)
            x_rd[u] = p.mark(mm)
            v.wait(x_rd[u], y_m[u % 4])
            bank_rd[bk] = v.mark(V.tensor_copy(YB[:, u % 4, :], bank[bk][:, :]))
            y.wait(bank_rd[bk])
            y_m[u % 4] = yss[u % 4].mark(SY.dma_start(YT[u * 128:(u + 1) * 128, :], YB[:, u % 4, :]))
    v.wait(v.mark(V.memset(ACC, 0.0)))
    fence(p, s, v, g)
    g.wait(*y_m)
    add = accumulate(256, wd_i)
    MSG = view(o_S, 2, 4, 256)
    T1 = view(o_S + 2048, 2, 4, 192)
    T2 = view(o_S + 3584, 2, 4, 192)
    rdm = [None, None]

    def tp(i, d):
        j = i % 2
        rows, oh = d["rows"], d["oh"]
        v.wait(*d["g"], rdm[j])
        s.wait(*d["g"], rdm[j])
        for k in range(4):
            r = rows[:, k, :].rearrange("p (m t o) -> p m t o", m=4, t=2)
            cc = PA[:, 4 * i + k, 2:6]
            ma = s.mark(S.activation(MSG[:, j, k, :].rearrange("p (m o) -> p m o", m=4), r[:, :, 0, :], ACT.Copy,
                                     scale=cc[:, 0:1]))
            c3 = cc[:, 1:4].unsqueeze(2).to_broadcast([128, 3, 64])
            v.mark(V.tensor_tensor(T1[:, j, k, :].rearrange("p (m o) -> p m o", m=3),
                                   r[:, 0:1, 1, :].to_broadcast([128, 3, 64]), c3, ALU.mult))
            mv = v.mark(V.tensor_tensor(T2[:, j, k, :].rearrange("p (m o) -> p m o", m=3), r[:, 1:4, 1, :], c3, ALU.mult))
        p.wait(ma, mv, d["moh"])
        ms = []
        bks = [4 * (i % 2) + k for k in range(4)]
        for k in range(4):
            p.wait(bank_rd[bks[k]])
            o_ = oh[:, k * 128:(k + 1) * 128]
            P.matmul(bank[bks[k]][:, 0:256], o_, MSG[:, j, k, :], start=True, stop=False, skip_group_check=True)
            P.matmul(bank[bks[k]][:, 64:256], o_, T1[:, j, k, :], start=False, stop=False, skip_group_check=True)
            for m_ in range(3):
                mm = P.matmul(bank[bks[k]][:, 0:64], o_, T2[:, j, k, m_ * 64:(m_ + 1) * 64], start=False, stop=(m_ == 2),
                              skip_group_check=True)
            ms.append(p.mark(mm))
        rdm[j] = ms[3]
        d["ms"], d["bks"] = ms, bks
        d["rows_read"], d["oh_read"] = [ma, mv], [ms[3]]
    edge_loop(YT, 512, isrc, locd, o_q, 3, [tp, add], 0, False)
    v.wait((v.sem, v.n))
    for w in range(W):
        v.mark(V.tensor_tensor(H[:, w, 0:64], H[:, w, 0:64], ACC[:, w, 0:64], ALU.add))
        hv = H[:, w, 64:256].rearrange("p (o m) -> p o m", m=3)
        v.mark(V.tensor_tensor(hv, hv, ACC[:, w, 64:256].rearrange("p (m o) -> p o m", m=3), ALU.add))
    v.wait((v.sem, v.n))
    m = norm_all(H)
    y.wait(m)
    fin = Slot(nc, "fin")
    fin.mark(SY.dma_start(out[0:3072, :].rearrange("(w p) f -> p w f", p=128), H[:, 0:24, :]))
    m = fin.mark(SY.dma_start(out[3072:NN, :], H[0:NN - 3072, 24, :]))
    y.wait(m)


def paired(x):
    x = np.concatenate([x, np.zeros((128 * C - NE, 10), x.dtype)]).reshape(128, C, 10)
    x = np.concatenate([x, np.zeros((128, 1, 10), x.dtype)], 1).reshape(128, (C + 1) // 2, 2, 10)
    return np.ascontiguousarray(x.transpose(2, 3, 1, 0).reshape(20, (C + 1) // 2 * 128))


def kernel(**inputs):
    import concourse.bacc as bacc
    from concourse.bass_utils import run_bass_kernel_spmd

    nc = bacc.Bacc("TRN2", target_bir_lowering=False, num_devices=1)
    arrays, aps = {}, {}
    for name, val in inputs.items():
        x = np.ascontiguousarray(val)
        if name == "edge_attr_10":
            name = "embT"
            x = paired(x)
        arrays["in_" + name] = x
        aps[name] = nc.dram_tensor("in_" + name, x.shape, mybir.dt.from_np(x.dtype), kind="ExternalInput").ap()
    out = nc.dram_tensor("out_0", [NN, 256], F, kind="ExternalOutput").ap()
    program(nc, aps, out)
    r = run_bass_kernel_spmd(nc, [arrays], core_ids=[0])
    return r.results[0]["out_0"]
```

```python
import numpy as np
import concourse.bass as bass
from concourse import mybir

F = mybir.dt.float32
I = mybir.dt.int32
BF = mybir.dt.bfloat16
ALU = mybir.AluOpType
ACT = mybir.ActivationFunctionType
AX = mybir.AxisListType.X

NN = 3125
NE = 50000
W = 25
NP = W * 128
C = 391
T = 416
G = T // 4
SB = 26
L = SB * 128
NEG = -1e38
PADKEY = -100000.0
KS = 4


class Queue:

    def __init__(self, nc, eng, name):
        self.eng = eng
        self.sem = nc.alloc_semaphore("done_" + name)
        self.n = 0
        self.seen = {}
        self.held = None

    def emit(self, fn):
        if self.held is None:
            fn()
        else:
            self.held.append(fn)

    def wait(self, *marks):
        for m in marks:
            if m is None:
                continue
            sem, v = m
            k = id(sem)
            if self.seen.get(k, 0) < v:
                self.emit(lambda sem=sem, v=v: self.eng.wait_ge(sem, v))
                self.seen[k] = v

    def mark(self, ins):
        if callable(ins):
            self.emit(lambda: ins().then_inc(self.sem, 1))
        else:
            ins.then_inc(self.sem, 1)
        self.n += 1
        return (self.sem, self.n)


class Slot:

    def __init__(self, nc, name):
        self.sem = nc.alloc_semaphore(name)
        self.n = 0

    def mark(self, ins, q=None):
        if callable(ins):
            q.emit(lambda: ins().then_inc(self.sem, 16))
        else:
            ins.then_inc(self.sem, 16)
        self.n += 16
        return (self.sem, self.n)


def program(nc, a, out, dbg=None, stop=99):
    v = Queue(nc, nc.vector, "dve")
    s = Queue(nc, nc.scalar, "act")
    p = Queue(nc, nc.tensor, "pe")
    g = Queue(nc, nc.gpsimd, "pool")
    y = Queue(nc, nc.sync, "sp")
    V, S, P, GP, SY = nc.vector, nc.scalar, nc.tensor, nc.gpsimd, nc.sync

    def dram(name, shape, dt=F):
        return nc.dram_tensor(name, shape, dt, kind="Internal").ap()

    top = [0]
    arena = nc.alloc_sbuf_tensor("arena", [128, 53200], F)

    def take(n):
        o = top[0]
        top[0] += (n + 7) // 8 * 8
        assert top[0] <= 53200, top[0]
        return o

    def view(o, *dims):
        n = int(np.prod(dims))
        ap = arena[:, o:o + n]
        if len(dims) == 1:
            return ap
        names = "abcd"[:len(dims)]
        return ap.rearrange("p (%s) -> p %s" % (" ".join(names), " ".join(names)),
                            **{names[i]: dims[i] for i in range(len(dims))})

    o_pa = take(T * 8)
    o_pb = take(T * 2)
    o_misc = take(4 * T + 1280)
    o_B = take(L + 8)
    o_S = take(T * 16)
    o_acc = take(W * 272)
    o_h = take(W * 256)
    o_q = take(W * 264)
    o_w = take(5640)
    o_ring = take(16 * 260)
    o_wv = take(2 * 4 * 272)
    o_oh = take(3 * 512)
    o_oht = take(3 * 256)
    o_sm = take(1200)

    PA = view(o_pa, T, 8)
    PB = view(o_pb, T, 2)
    mo = [o_misc]

    def misc(*dims, dt=F):
        ap = view(mo[0], *dims)
        mo[0] += int(np.prod(dims))
        assert mo[0] <= o_misc + 4 * T + 1280
        return ap if dt == F else ap.bitcast(dt)

    wd_i = misc(T, dt=I)
    ws_i = misc(T, dt=I)
    isrc = misc(T, dt=I)
    idst = misc(T, dt=I)
    ident = misc(128)
    iota = misc(128)
    ones = misc(128)
    tri = misc(128)
    sh_f = misc(128)
    sh_b = misc(128)
    g0 = misc(1)
    g1 = misc(1)
    a_bc = misc(1)
    pcol = misc(1)
    locd = misc(T)
    ident16 = misc(64, dt=BF)
    B = view(o_B, L + 1)
    SC = view(o_S, T, 16)
    ACC = view(o_acc, W, 272)
    H = view(o_h, W, 256)
    QT = view(o_q, W, 264)
    WV = view(o_wv, 2, 4 * 272)
    OH = view(o_oh, 3, 512)
    OHT = view(o_oht, 3, 256).bitcast(BF)
    OHB16 = view(o_oh, 3, 512)[:, :, 0:256].bitcast(BF)
    bank = [nc.alloc_psum_tensor(f"bank{i}", [128, 512], F) for i in range(8)]

    pre = Slot(nc, "pre")
    m = g.mark(GP.memset(ident, 0.0))
    g.mark(GP.memset(ones, 1.0))
    g.mark(GP.memset(tri, 1.0))
    g.mark(GP.memset(sh_f, 0.0))
    g.mark(GP.memset(sh_b, 0.0))
    g.mark(GP.memset(g0, 0.0))
    m = g.mark(GP.memset(g1, 0.0))
    g.wait(m)

    def sel(t, base, mult, op, fill, pat=[[-1, 128]]):
        return g.mark(GP.affine_select(out=t, in_=t, compare_op=op, fill=fill, base=base,
                                       pattern=pat, channel_multiplier=mult))
    sel(ident, 0, 1, ALU.not_equal, 1.0)
    sel(tri, 0, -1, ALU.is_gt, 0.0, [[1, 128]])
    sel(sh_f, 8, 1, ALU.not_equal, 1.0)
    sel(sh_b, -8, 1, ALU.not_equal, 1.0)
    sel(g0, -8, 1, ALU.is_ge, NEG, [[0, 1]])
    sel(g1, 119, -1, ALU.is_ge, NEG, [[0, 1]])
    m_i = g.mark(GP.iota(iota.bitcast(I), [[1, 128]], base=0, channel_multiplier=0))
    tstart = view(o_oht, T)
    g.mark(GP.iota(tstart.bitcast(I), [[128, T]], base=0, channel_multiplier=0))
    m_i = g.mark(GP.iota(pcol.bitcast(I), [[0, 1]], base=0, channel_multiplier=1))
    v.wait(m_i)
    v.mark(V.tensor_copy(iota, iota.bitcast(I)))
    v.mark(V.tensor_copy(tstart, tstart.bitcast(I)))
    m_const = v.mark(V.tensor_copy(pcol, pcol.bitcast(I)))
    v.mark(V.tensor_copy(ident16, ident))
    m_g = m_i

    OHB = view(o_acc, 25, C)
    FS = view(o_acc + 9776, 25, C)
    assert o_acc + 2 * 9776 <= o_w
    PW = view(o_S, C, 8)
    kf = view(o_S + 3128, C)
    posf = view(o_S + 3520, C)
    posi = view(o_S + 3912, C).bitcast(I)
    t1 = view(o_S + 4304, C)
    t1i = view(o_S + 4696, C).bitcast(I)
    rr = view(o_S + 5088, C)
    wf = view(o_S + 5480, T)
    code = view(o_pb, 392)
    poss = view(o_pb + 400, C).bitcast(I)
    small = o_sm
    lastF = view(small, 26)
    cnt = view(small + 32, 26)
    tot = view(small + 64, 26)
    base = view(small + 96, 27)
    off = view(small + 128, 26)
    basei = view(small + 160, 27).bitcast(I)
    ldc = Slot(nc, "ldc")
    srci = view(o_B, C).bitcast(I)
    dsti = view(o_B + 400, C).bitcast(I)
    dstn = view(o_B + 800, C).bitcast(I)
    at4 = view(o_B + 1200, C, 4)
    flag = misc(1, dt=I)
    viol = view(o_B + 2904, 1)
    fc1 = view(o_ring + 1100, 128)
    fc2 = view(o_ring + 1240, 2)

    m0 = v.mark(V.memset(srci, NP))
    m1 = v.mark(V.memset(dsti, NP))
    m1 = v.mark(V.memset(dstn, NP))
    m2 = v.mark(V.memset(at4, 0.0))
    v.mark(V.memset(fc1[0:20, :], 0.0))
    m3 = v.mark(V.memset(fc2, 0.0))
    y.wait(m1)
    tail = NE - 127 * C
    for t_, nm in ((dsti, "dst"), (srci, "src")):
        ldc.mark(SY.dma_start(t_[0:127, :], a[nm][0:127 * C].rearrange("(p c) -> p c", c=C)))
        ml = ldc.mark(SY.dma_start(t_[127:128, 0:tail], a[nm][127 * C:NE].rearrange("(o c) -> o c", o=1)))
    ldc.mark(SY.dma_start(dstn[0:127, :], a["dst"][1:127 * C + 1].rearrange("(p c) -> p c", c=C)))
    m_key = ldc.mark(SY.dma_start(dstn[127:128, 0:tail - 1], a["dst"][127 * C + 1:NE].rearrange("(o c) -> o c", o=1)))
    y.wait(m3)
    lda = Slot(nc, "lda")
    lda.mark(SY.dma_start(fc1[0:10, 0:64], a["L3_gnn_fc_w1"]))
    lda.mark(SY.dma_start(fc1[10:20, 64:128], a["L3_gnn_fc_w1"]))
    lda.mark(SY.dma_start(fc2[0:64, 0:1], a["L3_gnn_fc_w2"]))
    m_fc = lda.mark(SY.dma_start(fc2[64:128, 1:2], a["L3_gnn_fc_w2"]))

    v.wait(m_key)
    v.wait(v.mark(V.tensor_tensor(t1, dsti, dstn, ALU.is_gt)))
    mv = v.mark(V.tensor_reduce(viol, t1, AX, ALU.add))
    p.wait(mv, m_g, m_const)
    mp = p.mark(P.matmul(bank[7][:, 0:1], ones, viol, start=True, stop=True))
    v.wait(mp)
    m_flag = v.mark(V.tensor_copy(flag, bank[7][:, 0:1]))

    NCH = 17
    emb = [view(o_pa + i * 1536, 1536) for i in range(2)]
    hid = [view(o_ring + i * 512, 512) for i in range(2)]
    es = [Slot(nc, f"emb{i}") for i in range(2)]
    m_emb, m_mm1, m_silu, m_r = {}, {}, {}, {}
    n_mm = 49

    def load_emb(i):
        if i >= 2:
            y.wait(m_mm1[3 * i - 4])
        n_ = min(1536, 25088 - i * 1536)
        m_emb[i] = es[i % 2].mark(SY.dma_start(emb[i % 2][0:20, 0:n_], a["embT"][:, i * 1536:i * 1536 + n_]))
    load_emb(0)
    load_emb(1)
    lda = Slot(nc, "ldt")
    lda.mark(SY.dma_start(a_bc, a["L2_gnn_a"].rearrange("(o k) -> o k", o=1).to_broadcast([128, 1])))
    y.wait(m2)
    lda.mark(SY.dma_start(at4[0:127], a["edge_attr_4"][0:127 * C, :].rearrange("(p c) k -> p c k", c=C)))
    m_at = lda.mark(SY.dma_start(at4[127:128, 0:tail, :],
                                 a["edge_attr_4"][127 * C:NE, :].rearrange("(o c) k -> o c k", o=1)))
    p.wait(m_fc)

    def radial(i):
        if i < n_mm:
            if i >= 2:
                p.wait(m_silu[i - 2])
            p.wait(m_emb[i // 3])
            m_mm1[i] = p.mark(P.matmul(bank[i % 2][:, :], fc1[0:20, :],
                                       emb[(i // 3) % 2][0:20, (i % 3) * 512:(i % 3) * 512 + 512],
                                       start=True, stop=True))
            s.wait(m_mm1[i])
            if i >= 2:
                s.wait(m_r[i - 2])
            m_silu[i] = s.mark(S.activation(hid[i % 2], bank[i % 2][:, :], ACT.Silu,
                                            scale=float(np.float32(1) / np.float32(np.sqrt(10.0)))))
            if i % 3 == 2 and i // 3 + 2 < NCH:
                load_emb(i // 3 + 2)
        if i >= 1:
            j = i - 1
            p.wait(m_silu[j])
            for k in range(4):
                col_ = 8 * j + 2 * k
                mm = P.matmul(bank[2][:, col_:col_ + 2], hid[j % 2][:, k * 128:k * 128 + 128], fc2,
                              start=True, stop=True)
            m_r[j] = p.mark(mm)
    cst = float(1.0 / np.sqrt(128.0) * 1.679177 / 8.0 / 4.0)
    v.mark(V.tensor_copy(PW[:, :, 0], srci))
    v.mark(V.tensor_copy(PW[:, :, 1], dsti))
    v.mark(V.memset(PW[:, :, 6:8], 1.0))
    v.wait(v.mark(V.tensor_scalar(t1i, srci, 127, 12, ALU.bitwise_and, ALU.logical_shift_left)))
    v.mark(V.tensor_copy(code[:, 0:C], t1i))
    m_key = v.mark(V.memset(code[:, C:392], 0.0))
    v.wait(m_key)
    m_key = v.mark(V.scalar_tensor_tensor(code[:, 0:C], PW[:, :, 1], 1.0, code[:, 0:C], ALU.add, ALU.add))
    v.wait(m_key)

    def coefficients():
        v.wait(m_at, m_r[n_mm - 1])
        v.wait(v.mark(lambda: V.tensor_scalar(rr, bank[2][:, 0:C], cst, None, ALU.mult)))
        return v.mark(lambda: V.tensor_tensor(PW[:, :, 2:6], at4, rr.unsqueeze(2).to_broadcast([128, C, 4]), ALU.mult))

    def step(fn):
        v.wait(v.mark(fn))

    def add_up(nb, first):
        if first is None:
            step(lambda: V.memset(base[:, 0:1], 0.0))
        else:
            step(lambda: V.tensor_copy(base[:, 0:1], first))
        step(lambda: V.tensor_tensor_scan(base[:, 1:nb + 1], tot[:, 0:nb], tot[:, 0:nb], base[:, 0:1],
                                          ALU.add, ALU.max))

    def pad_and_add(nb):
        step(lambda: V.tensor_scalar(tot[:, 0:nb], tot[:, 0:nb], 127.0, None, ALU.add))
        step(lambda: V.tensor_copy(basei[:, 0:nb], tot[:, 0:nb]))
        step(lambda: V.tensor_scalar(basei[:, 0:nb], basei[:, 0:nb], 7, 7,
                                     ALU.logical_shift_right, ALU.logical_shift_left))
        step(lambda: V.tensor_copy(tot[:, 0:nb], basei[:, 0:nb]))
        add_up(nb, None)

    def buckets(nb, b0, dense_base, padded):
        m = None
        for b in range(nb):
            m = v.mark(lambda b=b: V.tensor_scalar(OHB[:, b, :], kf, float(b0 + b), None, ALU.is_equal))
        v.wait(m)
        of = OHB[:, 0:nb, :].rearrange("p b c -> p (b c)")
        ff = FS[:, 0:nb, :].rearrange("p b c -> p (b c)")
        step(lambda: V.tensor_tensor_scan(ff, of, of, 0.0, ALU.add, ALU.max))
        step(lambda: V.tensor_copy(lastF[:, 0:nb], FS[:, 0:nb, C - 1]))
        v.mark(lambda: V.tensor_copy(cnt[:, 0:1], lastF[:, 0:1]))
        mc = v.mark(lambda: V.tensor_tensor(cnt[:, 1:nb], lastF[:, 1:nb], lastF[:, 0:nb - 1], ALU.subtract))
        p.wait(mc)
        p.mark(lambda: P.matmul(bank[3][:, 0:nb], tri, cnt[:, 0:nb], start=True, stop=True))
        mp = p.mark(lambda: P.matmul(bank[4][:, 0:nb], ones, cnt[:, 0:nb], start=True, stop=True))
        v.wait(mp)
        step(lambda: V.tensor_copy(tot[:, 0:nb], bank[4][:, 0:nb]))
        if padded:
            pad_and_add(nb)
        else:
            add_up(nb, dense_base)
        step(lambda: V.tensor_tensor(off[:, 0:nb], base[:, 0:nb], bank[3][:, 0:nb], ALU.add))
        step(lambda: V.tensor_tensor(off[:, 1:nb], off[:, 1:nb], lastF[:, 0:nb - 1], ALU.subtract))
        step(lambda: V.tensor_scalar(off[:, 0:nb], off[:, 0:nb], -1.0, None, ALU.add))
        fb = FS[:, 0:nb, :]
        step(lambda: V.tensor_tensor(fb, fb, off[:, 0:nb].unsqueeze(2).to_broadcast([128, nb, C]), ALU.add))
        step(lambda: V.tensor_tensor(fb, fb, OHB[:, 0:nb, :], ALU.mult))
        step(lambda: V.tensor_reduce(t1, fb.rearrange("p b c -> p c b"), AX, ALU.add))
        step(lambda: V.tensor_tensor(posf, posf, t1, ALU.add))

    sct = [Slot(nc, f"sct{k}") for k in range(KS)]
    zs = Slot(nc, "zs")
    zs1 = Slot(nc, "zs1")
    rl = Slot(nc, "rl")
    sct1 = [Slot(nc, f"sct1{k}") for k in range(KS)]
    sct2 = [Slot(nc, f"sct2{k}") for k in range(KS)]
    rl1 = Slot(nc, "rl1")

    def scatter(targets, rows, source, index, cols=range(C), sct=sct):
        for c in cols:
            k = c % KS
            if sct[k].n:
                g.wait((sct[k].sem, sct[k].n))
            sct[k].mark(lambda c=c, k=k: GP.indirect_dma_start(
                out=targets[k], out_offset=bass.IndirectOffsetOnAxis(ap=index[:, c:c + 1], axis=0),
                in_=source(c), in_offset=None, bounds_check=rows - 1, oob_is_err=False), g)
        return [(sct[k].sem, sct[k].n) for k in range(KS)]

    zero = view(o_wv, 2176)
    m_z = v.mark(V.memset(zero, 0.0))
    R1, R2 = 128 * C, 128 * T
    tg1 = [dram(f"sa{k}", [R1, 8]) for k in range(KS)]
    tg2 = [dram(f"sb{k}", [R2, 8]) for k in range(KS)]
    tg3 = [dram(f"sc{k}", [R2, 2]) for k in range(KS)]
    y.wait(m_z)

    def flat(t, ncol):
        return t.rearrange("(p c) k -> p (c k)", c=ncol)
    for k in range(KS):
        for h in range(2):
            zs.mark(SY.dma_start(flat(tg2[k], T)[:, h * 1664:(h + 1) * 1664], zero[:, 0:1664]))
        m_zs = zs.mark(SY.dma_start(flat(tg3[k], T), zero[:, 0:T * 2]))

    def reload(targets, ncol, lo, n, dst, marks, at, rl=rl):
        y.wait(*marks)
        parts = [view(at + k * n, n) for k in range(KS)]
        y.wait((v.sem, v.n))
        for k in range(KS):
            mm = rl.mark(lambda k=k: SY.dma_start(parts[k], flat(targets[k], ncol)[:, lo:lo + n]), y)
        v.wait(mm)
        v.mark(lambda: V.tensor_tensor(parts[0], parts[0], parts[1], ALU.add))
        step(lambda: V.tensor_tensor(parts[2], parts[2], parts[3], ALU.add))
        step(lambda: V.tensor_tensor(dst, parts[0], parts[2], ALU.add))

    def split_key(src_f, want_high):
        step(lambda: V.tensor_copy(t1i, src_f))
        if want_high:
            step(lambda: V.tensor_scalar(t1i, t1i, 7, None, ALU.logical_shift_right))
        else:
            step(lambda: V.tensor_scalar(t1i, t1i, 127, None, ALU.bitwise_and))
        step(lambda: V.tensor_copy(kf, t1i))

    def padded_rows(rows_):
        step(lambda: V.tensor_copy(t1i, posf))
        step(lambda: V.tensor_scalar(rows_, t1i, 127, None, ALU.bitwise_and))
        step(lambda: V.tensor_copy(t1, rows_))
        step(lambda: V.tensor_scalar(rows_, t1i, 7, None, ALU.logical_shift_right))
        step(lambda: V.tensor_copy(posf, rows_))
        step(lambda: V.scalar_tensor_tensor(posf, t1, float(T), posf, ALU.mult, ALU.add))
        step(lambda: V.tensor_scalar(kf, kf, float(W), 1e6, ALU.is_ge, ALU.mult))
        step(lambda: V.tensor_tensor(posf, posf, kf, ALU.add))
        return v.mark(lambda: V.tensor_copy(rows_, posf))

    def windows(wi):
        wide = view(o_acc, T, 24)
        step(lambda: V.tensor_tensor(wide, tstart.unsqueeze(2).to_broadcast([128, T, 24]),
                                     base[:, 1:25].unsqueeze(1).to_broadcast([128, T, 24]), ALU.is_ge))
        step(lambda: V.tensor_reduce(wf, wide, AX, ALU.add))
        step(lambda: V.tensor_copy(wi, wf))

    def first_pass():
        split_key(PW[:, :, 1], False)
        step(lambda: V.memset(posf, 0.0))
        carry = view(small + 230, 1)
        for b0 in range(0, 128, 25):
            n = min(25, 128 - b0)
            buckets(n, b0, carry if b0 else None, False)
            step(lambda n=n: V.tensor_copy(carry, base[:, n:n + 1]))
        mpos = v.mark(lambda: V.tensor_copy(posi, posf))
        for k in range(KS):
            zs1.mark(lambda k=k: SY.dma_start(flat(tg1[k], C)[:, 0:1664], zero[:, 0:1664]), y)
            mz = zs1.mark(lambda k=k: SY.dma_start(flat(tg1[k], C)[:, 1664:C * 8], zero[:, 0:C * 8 - 1664]), y)
        g.wait(mpos, mz)
        marks = scatter(tg1, R1, lambda c: PW[:, c, 0:8], posi, sct=sct1)
        reload(tg1, C, 0, C * 8, PW.rearrange("p c k -> p (c k)"), marks, o_acc, rl1)

    def conditional(part, queues):
        qs = queues
        before = {id(q): (q.n, dict(q.seen)) for q in qs}
        for q in qs:
            q.held = []
        part()
        for q in qs:
            held, q.held = q.held, None
            n0, seen = before[id(q)]
            q.seen = seen
            q.wait(m_flag)
            r = q.eng.alloc_register("unsorted")
            q.eng.reg_load(r, flag[0:1, 0:1])
            with q.eng.If_ne(r, 0):
                for fn in held:
                    fn()
            with q.eng.Else():
                if q.n > n0:
                    q.eng.wait_ge(q.sem, n0)
                    q.eng.sem_inc(q.sem, q.n - n0)
            q.eng.end_ifs()

    CMP = view(o_acc, 25, C)
    strt = view(small + 192, 26)
    dshift = view(small + 960, 24)
    b128 = view(small + 990, 25)
    e0 = view(o_oh + 1000, T)
    v.mark(V.memset(strt, 0.0))
    step(lambda: V.tensor_scalar(b128, iota[:, 1:26], 128.0, None, ALU.mult))
    step(lambda: V.tensor_tensor(CMP, PW[:, :, 1].unsqueeze(1).to_broadcast([128, 25, C]),
                                 b128.unsqueeze(2).to_broadcast([128, 25, C]), ALU.is_lt))
    mc = v.mark(V.tensor_reduce(lastF[:, 0:25], CMP, AX, ALU.add))
    for i in range(7):
        radial(i)
    p.wait(mc)
    mp = p.mark(P.matmul(bank[4][:, 0:25], ones, lastF[:, 0:25], start=True, stop=True))
    v.wait(mp)
    step(lambda: V.tensor_copy(strt[:, 1:26], bank[4][:, 0:25]))
    step(lambda: V.tensor_tensor(tot[:, 0:25], strt[:, 1:26], strt[:, 0:25], ALU.subtract))
    pad_and_add(25)
    windows(wd_i)
    step(lambda: V.tensor_tensor(dshift, base[:, 1:25], strt[:, 1:25], ALU.subtract))
    step(lambda: V.tensor_copy(lastF[:, 0:24], dshift))
    step(lambda: V.tensor_tensor(dshift[:, 1:24], dshift[:, 1:24], lastF[:, 0:23], ALU.subtract))
    wide = view(o_acc, T, 24)
    step(lambda: V.tensor_tensor(wide, wide, dshift.unsqueeze(1).to_broadcast([128, T, 24]), ALU.mult))
    step(lambda: V.tensor_reduce(wf, wide, AX, ALU.add))
    step(lambda: V.tensor_tensor(wf, tstart, wf, ALU.subtract))
    m_e0 = v.mark(V.tensor_copy(e0.bitcast(I), wf))
    v.wait(m_e0)

    for i in range(7, 28):
        radial(i)
    step(lambda: V.tensor_scalar(t1i, srci, 7, None, ALU.logical_shift_right))
    step(lambda: V.tensor_copy(kf, t1i))
    step(lambda: V.memset(posf, 0.0))
    buckets(25, 0, None, True)
    for i in range(28, n_mm + 1):
        radial(i)
    windows(ws_i)
    m_poss = padded_rows(poss)
    v.wait(m_poss)
    m_pw = coefficients()
    v.wait(m_pw)

    SW = dram("SW", [R2, 8])
    swr = Slot(nc, "swr")
    wl = Slot(nc, "wl")
    xs = Slot(nc, "xs")

    def load_w(ap, src):
        return wl.mark(SY.dma_start(ap, src))

    def rows_bc(ap1, n):
        return ap1.rearrange("(o n) -> o n", o=1).to_broadcast([128, n])

    def kview(ap):
        return ap.rearrange("(k p) n -> p k n", p=128)

    def col(ap1, k):
        return ap1.rearrange("(k p) -> p k", p=128)

    w_in = view(o_ring + 3072, 2, 256)
    b_bc = view(o_ring + 3584, 256)
    WM = view(o_w, 5640)
    wq = WM[:, 0:512].rearrange("p (k n) -> p k n", k=2)
    wk = WM[:, 512:1024].rearrange("p (k n) -> p k n", k=2)
    wv = WM[:, 1024:1536].rearrange("p (k n) -> p k n", k=2)
    bq, bk_, bv = WM[:, 1536:1792], WM[:, 1792:2048], WM[:, 2048:2304]
    gb = WM[:, 2304:2312].rearrange("p (j k) -> p j k", k=2)
    wo = WM[:, 2320:2832].rearrange("p (k n) -> p k n", k=2)
    bo = WM[:, 2832:3088]
    w1 = WM[:, 0:2048].rearrange("p (k n) -> p k n", k=2)
    w2 = WM[:, 3328:5376].rearrange("p (k n) -> p k n", k=8)
    b1c = WM[:, 3088:3096]
    b2 = WM[:, 5376:5632]

    def load_layer(l):
        load_w(wq, kview(a["L0_gnn_wq"][l]))
        load_w(wk, kview(a["L0_gnn_wk"][l]))
        load_w(wv, kview(a["L0_gnn_wv"][l]))
        load_w(bq, rows_bc(a["L0_gnn_bq"][l], 256))
        load_w(bk_, rows_bc(a["L0_gnn_bk"][l], 256))
        load_w(bv, rows_bc(a["L0_gnn_bv"][l], 256))
        load_w(wo, kview(a["L0_gnn_wo"][l]))
        load_w(bo, rows_bc(a["L0_gnn_bo"][l], 256))
        with nc.allow_non_contiguous_dma(reason="small columns"):
            load_w(gb[:, 0, :], col(a["L0_gnn_ln1_g"][l], 2))
            load_w(gb[:, 1, :], col(a["L0_gnn_ln1_b"][l], 2))
            load_w(gb[:, 2, :], col(a["L0_gnn_ln2_g"][l], 2))
            load_w(gb[:, 3, :], col(a["L0_gnn_ln2_b"][l], 2))
            load_w(b1c, col(a["L0_gnn_b1"][l], 8))
        load_w(w2, a["L0_gnn_w2"][l].rearrange("(k p) n -> p k n", p=128))
        return load_w(b2, rows_bc(a["L0_gnn_b2"][l], 256))
    XE = view(o_ring + 1536, 6, 256)
    xe = Slot(nc, "xe")
    m_xe = xe.mark(SY.dma_start(XE, a["x"][0:768, :].rearrange("(w p) f -> p w f", p=128)))
    load_w(w_in, kview(a["L0_gnn_w_in"]))
    load_w(b_bc, rows_bc(a["L0_gnn_b_in"], 256))
    m_w0 = load_layer(0)
    y.wait(m_pw)
    swr.mark(SY.dma_start(flat(SW[0:R1], C), PW.rearrange("p c k -> p (c k)")))
    m_sw = swr.mark(SY.dma_start(SW[R1:R2].rearrange("(p c) k -> p (c k)", p=128), zero[:, 0:(T - C) * 8]))

    rl2 = Slot(nc, "rl2")

    def general():
        first_pass()
        split_key(PW[:, :, 1], True)
        step(lambda: V.memset(posf, 0.0))
        buckets(25, 0, None, True)
        mpos = padded_rows(posi)
        g.wait(mpos, m_zs)
        marks = scatter(tg2, R2, lambda c: PW[:, c, 0:8], posi, sct=sct2)
        reload(tg2, T, 0, T * 8, PA.rearrange("p c k -> p (c k)"), marks, o_acc, rl2)
    conditional(general, [v, p, g, y])

    m_fetch = []
    for q, mine in ((y, lambda i, j: j < 2 or (j == 2 and i % 2 == 0)),
                    (g, lambda i, j: j == 3 or (j == 2 and i % 2))):
        fetch = [Slot(nc, f"fetch_{len(m_fetch)}{k}") for k in range(2)]
        q.wait(m_sw, m_e0, (v.sem, v.n))
        r = q.eng.alloc_register("in_order")
        q.eng.reg_load(r, flag[0:1, 0:1])
        rt = [q.eng.alloc_register(f"e0_{j}") for j in range(4)]
        with q.eng.If_eq(r, 0):
            for i in range(G):
                q.eng.reg_load(rt, e0.bitcast(I)[0:1, 4 * i:4 * i + 4])
                for j in range(4):
                    if mine(i, j):
                        first = q.eng.snap(rt[j], min_val=0, max_val=R2 - 128)
                        fetch[i % 2].mark(q.eng.dma_start(PA[:, 4 * i + j, :], SW[bass.ds(first, 128), :]))
        q.eng.end_ifs()
        m_fetch += [(f.sem, f.n) for f in fetch]

    D8 = view(o_S, SB, 16, 8)

    def blocked(x):
        return x.rearrange("p (b j) k -> p j b k", j=SB)
    bank_rd = [None] * 8

    def to_scan(src, dst, m_src):
        p.wait(m_src)
        last = None
        for q in range(0, SB, 4):
            n = min(4, SB - q)
            bk = (q // 4) % 4
            p.wait(bank_rd[bk])
            for k in range(n):
                mm = P.transpose(bank[bk][:, k * 128:(k + 1) * 128],
                              src[:, (q + k) * 128:(q + k + 1) * 128], ident)
            s.wait(p.mark(mm))
            last = bank_rd[bk] = s.mark(S.activation(dst[:, q * 128:(q + n) * 128], bank[bk][:, 0:n * 128], ACT.Copy))
        return last

    def from_scan(src, m_src, use):
        p.wait(m_src)
        for j in range(SB):
            bk = j % 4
            p.wait(bank_rd[bk])
            mt = p.mark(P.transpose(bank[bk][:, 0:128], src[:, j * 128:(j + 1) * 128], ident))
            bank_rd[bk] = use(j, bank[bk][:, 0:128], mt)

    rowA = view(o_sm + 256, 128)[0:1]
    rowAb = view(o_sm + 384, 128)[0:1]
    rowE = view(o_sm + 512, 128)[0:1]
    rowC = view(o_sm + 640, 128)[0:1]
    ccol = view(o_sm + 770, 1)
    rowH = view(o_oh, 384)[0:1]

    def segment_max(SP, FB, BB, m_in):
        v.wait(m_in)
        for back in (False, True):
            dst = BB if back else FB
            st = B[:, 1:L + 1][:, ::-1] if back else B[:, 0:L]
            sp = SP[:, ::-1] if back else SP
            dv = dst[:, ::-1] if back else dst
            v.wait(v.mark(V.tensor_tensor_scan(dv, st, sp, NEG, ALU.add, ALU.max)))
            end = dst[:, 0:1] if back else dst[:, L - 1:L]
            p.wait((v.sem, v.n))
            mp = p.mark(P.transpose(bank[4][0:1, 0:128], end, ident))
            v.wait(mp)
            v.wait(v.mark(V.tensor_copy(rowE, bank[4][0:1, 0:128])))
            row = rowAb if back else rowA
            hb = "p (b h) -> p b h"
            re_, rr_, rc_ = rowE.rearrange(hb, h=8), row.rearrange(hb, h=8), rowC.rearrange(hb, h=8)
            hx = rowH.rearrange("p (k h b) -> p k h b", k=3, h=8)
            step(lambda: V.tensor_copy(hx[:, 0], rr_.rearrange("p b h -> p h b")))
            step(lambda: V.memset(hx[:, 0, :, 15:16] if back else hx[:, 0, :, 0:1], NEG))
            step(lambda: V.tensor_copy(hx[:, 1], re_.rearrange("p b h -> p h b")))
            f_ = [rowH[:, k * 128:(k + 1) * 128] for k in range(3)]
            if back:
                f_ = [x[:, ::-1] for x in f_]
            step(lambda: V.tensor_tensor_scan(f_[2], f_[0], f_[1], NEG, ALU.add, ALU.max))
            hv = hx[:, 2].rearrange("p h b -> p b h")
            if back:
                step(lambda: V.tensor_copy(rc_[:, 0:15], hv[:, 1:16]))
                step(lambda: V.memset(rc_[:, 15:16], NEG))
            else:
                step(lambda: V.tensor_copy(rc_[:, 1:16], hv[:, 0:15]))
                step(lambda: V.memset(rc_[:, 0:1], NEG))
            p.wait((v.sem, v.n))
            mp = p.mark(P.matmul(bank[4][:, 256:257], rowC, ones[0:1, 0:1], start=True, stop=True))
            v.wait(mp)
            v.wait(v.mark(V.tensor_copy(ccol, bank[4][:, 256:257])))
            v.wait(v.mark(V.tensor_tensor_scan(dv, st, sp, ccol, ALU.add, ALU.max)))
        return v.mark(V.tensor_tensor(FB, FB, BB, ALU.max))


    def all_done(*qs):
        return [(q.sem, q.n) for q in qs]

    def fence(*qs):
        ms = all_done(v, s, p, g)
        for q in qs:
            q.wait(*[m for m in ms if m[0] is not q.sem or q is not p])

    MS = view(o_sm + 256 + 520, 2 * W)
    RS = view(o_sm + 256 + 580, W)
    EP = view(o_sm + 256 + 610, 1)
    m_ep = v.mark(V.memset(EP, 1e-5))
    ST = view(o_sm + 960, 6 * W)

    def ln_stats(X):
        m = None
        for w in range(W):
            m = v.mark(V.bn_stats(ST[:, 6 * w:6 * w + 6], X[:, w, :]))
        v.wait(m)
        for w in range(W):
            m = v.mark(V.bn_aggr(MS[:, 2 * w:2 * w + 2], ST[:, 6 * w:6 * w + 6]))
        s.wait(m)
        ms = s.mark(S.activation(RS, MS.rearrange("p (w k) -> p w k", k=2)[:, :, 1], ACT.Sqrt, bias=EP))
        v.wait(m, ms)
        m = v.mark(V.reciprocal(RS, RS))
        v.wait(m)
        return m

    def normed(dst, src, w):
        return V.tensor_scalar(dst, src, MS[:, 2 * w:2 * w + 1], RS[:, w:w + 1], ALU.subtract, ALU.mult)

    XN = view(o_ring, 2, 256)
    XT = view(o_ring + 512, 2, 512)
    OUTB = view(o_ring + 1536, 2, 768)

    def transposed(n, get, after, gb=None):
        done = [None] * n
        cp = [None] * n

        def first(w):
            ap, m = get(w)
            p.wait(m, bank_rd[w % 2])
            for k in range(2):
                mm = P.transpose(bank[w % 2][:, k * 128:(k + 1) * 128], ap[:, k * 128:(k + 1) * 128], ident)
            mt = p.mark(mm)
            s.wait(mt)
            if w >= 2:
                s.wait(done[w - 2])
            for k in range(2):
                o = XT[:, w % 2, k * 128:(k + 1) * 128]
                i = bank[w % 2][:, k * 128:(k + 1) * 128]
                if gb is None:
                    cp[w] = s.mark(S.activation(o, i, ACT.Copy))
                else:
                    cp[w] = s.mark(S.activation(o, i, ACT.Identity, scale=gb[0][:, k:k + 1], bias=gb[1][:, k:k + 1]))
            bank_rd[w % 2] = cp[w]
            return mt
        mts = {}
        for w in range(n + 1):
            if w < n:
                mts[w] = first(w)
            if w >= 1:
                done[w - 1] = after(w - 1, XT[:, (w - 1) % 2, :], cp[w - 1])
        return mts, done

    def proj(xt, wt, cols, bk):
        for k in range(2):
            mm = P.matmul(bank[bk][:, 0:cols], xt[:, k * 128:(k + 1) * 128], wt[:, k, :], start=(k == 0), stop=(k == 1))
        return mm

    gs = [Slot(nc, f"gs{i}") for i in range(24)]

    def edge_loop(table, width, idx, loc, ring_o, ngrp, stages, lag, transposed_oh, oh_at=None,
                  between=None):
        ring = view(ring_o, ngrp, 4, width)
        noh = 3 if oh_at is None else 8
        OH = view(o_oh if oh_at is None else oh_at, noh, 512)
        st = [{"rows": ring[:, i % ngrp], "oh": OH[:, i % noh, :], "oht": OHT[:, i % 3, :]} for i in range(G)]
        nst = len(stages)

        def gather(i):
            d = st[i]
            if i >= ngrp:
                g.wait(*st[i - ngrp]["rows_read"])
            d["g"] = []
            for k in range(4):
                sl = (i % ngrp) * 4 + k
                d["g"].append(gs[sl].mark(GP.indirect_dma_start(
                    out=ring[:, i % ngrp, k, :], out_offset=None, in_=table,
                    in_offset=bass.IndirectOffsetOnAxis(ap=idx[:, 4 * i + k:4 * i + k + 1], axis=0))))

        def onehot(i):
            d = st[i]
            if i >= noh:
                v.wait(*st[i - noh]["oh_read"])
            o = (OHB16 if transposed_oh is True else OH)[:, i % noh, :]
            d["moh"] = v.mark(V.tensor_tensor(
                o.rearrange("p (k n) -> p k n", k=4),
                loc[:, 4 * i:4 * i + 4].unsqueeze(2).to_broadcast([128, 4, 128]),
                iota.unsqueeze(1).to_broadcast([128, 4, 128]), ALU.is_equal))

        def transpose(i):
            d = st[i]
            p.wait(d["moh"], bank_rd[i % 2])
            src, idn = (OHB16, ident16) if transposed_oh is True else (OH, ident)
            for k in range(4):
                o_, i_ = bank[i % 2][:, k * 128:(k + 1) * 128], src[:, i % noh, k * 128:(k + 1) * 128]
                mm = P.matmul(o_, i_, idn, start=True, stop=True) if idn is ident16 else P.transpose(o_, i_, idn)
            mt = p.mark(mm)
            d["oh_read"] = [mt]
            s.wait(mt)
            if i >= 3:
                s.wait(*st[i - 3]["oht_read"])
            d["moht"] = bank_rd[i % 2] = s.mark(S.activation(OHT[:, i % 3, :], bank[i % 2][:, :], ACT.Copy))
        for i in range(min(ngrp, G)):
            gather(i)
        if between is not None:
            between()
        nx = 3 if transposed_oh else 1
        for i in range(nx):
            onehot(i)
        if transposed_oh:
            transpose(0)
        for it in range(G + nst - 1):
            if transposed_oh and it + 1 < G:
                transpose(it + 1)
            for k in range(nst):
                if 0 <= it - k < G:
                    stages[k](it - k, st[it - k])
            if it + nx < G:
                onehot(it + nx)
            j = it - lag + ngrp
            if ngrp <= j < G:
                gather(j)

    regs = {}

    def win(q, wi, i):
        k = id(q)
        if k not in regs:
            regs[k] = [q.eng.alloc_register(f"w{j}_{len(regs)}") for j in range(4)]
        q.eng.reg_load(regs[k], wi[0:1, 4 * i:4 * i + 4])
        return [q.eng.snap(r, min_val=0, max_val=W - 1) for r in regs[k]]

    def accumulate(width, wi):
        def add(i, d):
            marks, bks = d["ms"], d["bks"]
            ws = win(v, wi, i)
            res = []
            for k in range(4):
                v.wait(marks[k])
                if add.last:
                    v.wait(add.last)
                d = ACC[:, bass.ds(ws[k], 1), 0:width]
                add.last = v.mark(V.tensor_tensor(d, d, bank[bks[k]][:, 0:width].unsqueeze(1), ALU.add))
                bank_rd[bks[k]] = add.last
        add.last = None
        return add

    KT, VT = dram("KT", [NP, 256]), dram("VT", [NP, 256])
    X1T = dram("X1T", [NP, 72])
    XA = dram("XA", [NP, 256])
    MT = [dram(f"MT{i}", [NP, 260]) for i in range(4)]
    YT = dram("YT", [NP, 512])

    def load_x(dst, q):
        m = v.mark(V.memset(dst[:, 24, :], 0.0))
        q.wait(m)
        xs.mark(q.eng.dma_start(dst[:, 0:24, :], a["x"][0:3072, :].rearrange("(w p) f -> p w f", p=128)))
        return xs.mark(q.eng.dma_start(dst[0:NN - 3072, 24, :], a["x"][3072:NN, :]))

    fence(v, s, p)
    XX = view(o_acc, W, 256)
    m = v.mark(V.memset(XX[:, 24, :], 0.0))
    s.wait(m)
    xs.mark(S.dma_start(XX[:, 6:24, :], a["x"][768:3072, :].rearrange("(w p) f -> p w f", p=128)))
    mx = xs.mark(S.dma_start(XX[0:NN - 3072, 24, :], a["x"][3072:NN, :]))
    p.wait(m_w0)
    v.wait(m_w0)

    def aft(w, xt, m):
        p.wait(m, bank_rd[2 + w % 2])
        mm = p.mark(proj(xt, w_in, 256, 2 + w % 2))
        v.wait(mm)
        bank_rd[2 + w % 2] = v.mark(V.tensor_tensor(H[:, w, :], bank[2 + w % 2][:, 0:256], b_bc, ALU.add))
        return mm
    transposed(W, lambda w: (XE[:, w, :], m_xe) if w < 6 else (XX[:, w, :], mx), aft)

    scale = 1.0 / np.sqrt(32.0)
    Q3 = view(o_q, W, 2, 132).bitcast(BF)
    QL = view(o_acc, W, 132).bitcast(BF)

    tbl = [Slot(nc, "tb0"), Slot(nc, "tb1")]
    st_out = [None, None]

    def load_and_project(l):
        m_w = m_w0
        stq = s
        if l:
            fence(y, v, s, p)
            m_w = load_layer(l)
            stq = y
        else:
            fence(v, s, p)
        ln_stats(H)
        s.wait(m_w)
        p.wait(m_w)
        v.wait(m_w)
        mts = {}

        QWA = view(o_wv, 10, 264)
        v.wait(m_zs, m_sw)
        s.wait(m_zs, m_sw)
        split_done = {}

        def norm(w):
            if w >= 2:
                v.wait(mts[w - 2])
            return v.mark(normed(XN[:, w % 2, :], H[:, w, :], w))

        def split(w0, w1_):
            q_ = QWA[:, w0 % 10:w0 % 10 + 5, :]
            v.wait((v.sem, v.n))
            v.wait(v.mark(V.tensor_copy(Q3[:, w0:w1_, 0, :], q_)))
            v.wait(v.mark(V.tensor_tensor(q_, q_, Q3[:, w0:w1_, 0, :], ALU.subtract)))
            v.wait(v.mark(V.tensor_copy(Q3[:, w0:w1_, 1, :], q_)))
            split_done[w0 // 5] = v.mark(V.tensor_tensor(QL[:, w0:w1_, :], q_, Q3[:, w0:w1_, 1, :], ALU.subtract))

        def project(w, xt, m):
            p.wait(m)
            mms = []
            for k, wt in enumerate((wq, wk, wv)):
                bk = 2 + (3 * w + k) % 6
                p.wait(bank_rd[bk])
                mms.append(p.mark(proj(xt, wt, 256, bk)))
            return mms

        def finish(w, mms):
            o = OUTB[:, w % 2, :]
            v.wait(st_out[w % 2])
            for k, bb in enumerate((bq, bk_, bv)):
                bk = 2 + (3 * w + k) % 6
                v.wait(mms[k])
                bank_rd[bk] = mo_ = v.mark(V.tensor_tensor(o[:, k * 256:(k + 1) * 256], bank[bk][:, 0:256], bb, ALU.add))
                if k == 0:
                    s.wait(mo_, split_done.get(w // 5 - 2))
                    mq = s.mark(S.activation(QWA[:, w % 10, 0:256], o[:, 0:256], ACT.Copy, scale=float(scale)))
            v.wait(mq, mo_)
            v.wait(v.mark(V.tensor_tensor(o[:, 0:256], QWA[:, w % 10, 0:256], o[:, 256:512], ALU.mult)))
            ml = v.mark(V.tensor_reduce(QWA[:, w % 10, 256:264], o[:, 0:256].rearrange("p (h d) -> p h d", d=32), AX, ALU.add))
            if w % 5 == 4:
                split(w - 4, w + 1)
            stq.wait(ml)
            tbs = tbl[w % 2]
            tbs.mark(stq.eng.dma_start(KT[w * 128:(w + 1) * 128, :], o[:, 256:512]))
            st_out[w % 2] = tbs.mark(stq.eng.dma_start(VT[w * 128:(w + 1) * 128, :], o[:, 512:768]))

        done = [None] * W
        cp = [None] * W
        nm = {0: norm(0)}
        for w in range(W + 1):
            if w >= 1:
                mms = project(w - 1, XT[:, (w - 1) % 2, :], cp[w - 1])
                done[w - 1] = mms[2]
            if w < W:
                p.wait(nm[w], bank_rd[w % 2])
                for k in range(2):
                    mm = P.transpose(bank[w % 2][:, k * 128:(k + 1) * 128], XN[:, w % 2, k * 128:(k + 1) * 128], ident)
                mts[w] = p.mark(mm)
                s.wait(mts[w])
                if w >= 2:
                    s.wait(done[w - 2])
                for k in range(2):
                    cp[w] = s.mark(S.activation(XT[:, w % 2, k * 128:(k + 1) * 128],
                                                bank[w % 2][:, k * 128:(k + 1) * 128], ACT.Identity,
                                                scale=gb[:, 0, k:k + 1], bias=gb[:, 1, k:k + 1]))
                bank_rd[w % 2] = cp[w]
            if w + 1 < W:
                nm[w + 1] = norm(w + 1)
            if w >= 1:
                finish(w - 1, mms)

    load_and_project(0)

    rv = v.eng.alloc_register("in_order_dve")
    v.eng.reg_load(rv, flag[0:1, 0:1])
    with v.eng.If_eq(rv, 0):
        for sem, n in m_fetch:
            v.eng.wait_ge(sem, n)
    v.eng.end_ifs()
    wfl = view(o_oht, T)
    ok = view(o_oh, T)
    vl = PA[:, :, 7]
    step(lambda: V.tensor_copy(wfl, wd_i))
    step(lambda: V.scalar_tensor_tensor(locd, wfl, -128.0, PA[:, :, 1], ALU.mult, ALU.add))
    step(lambda: V.scalar_tensor_tensor(ok, locd, 0.0, vl, ALU.is_ge, ALU.mult))
    step(lambda: V.scalar_tensor_tensor(ok, locd, 128.0, ok, ALU.is_lt, ALU.mult))
    step(lambda: V.tensor_tensor(PA[:, :, 0], PA[:, :, 0], ok, ALU.mult))
    v.mark(V.tensor_copy(isrc, PA[:, :, 0]))
    step(lambda: V.tensor_scalar(vl, ok, -PADKEY, PADKEY, ALU.mult, ALU.add))
    step(lambda: V.tensor_tensor(PA[:, :, 1], PA[:, :, 1], vl, ALU.add))
    step(lambda: V.scalar_tensor_tensor(locd, wfl, -128.0, PA[:, :, 1], ALU.mult, ALU.add))

    DS = view(o_S + L, L)
    md = v.mark(V.tensor_copy(D8, blocked(PA[:, :, 1:2].to_broadcast([128, T, 8]))))
    md = to_scan(view(o_S, L), DS, md)
    p.wait(md)
    mp = p.mark(P.matmul(bank[4][:, 0:1], sh_f, DS[:, L - 1:L], start=True, stop=True))
    v.wait(md, mp)
    v.mark(V.tensor_tensor(B[:, 1:L], DS[:, 1:L], DS[:, 0:L - 1], ALU.not_equal))
    v.wait(v.mark(V.tensor_tensor(B[:, 0:1], DS[:, 0:1], bank[4][:, 0:1], ALU.not_equal)))
    v.wait(v.mark(V.tensor_scalar(B[:, 0:L], B[:, 0:L], NEG, None, ALU.mult)))
    mb = v.mark(V.tensor_tensor(B[:, 0:1], B[:, 0:1], g0, ALU.add))
    p.wait(mb)
    mp = p.mark(P.matmul(bank[4][:, 0:1], sh_b, B[:, 0:1], start=True, stop=True))
    v.wait(mb, mp)
    v.wait(v.mark(V.tensor_tensor(B[:, L:L + 1], bank[4][:, 0:1], g1, ALU.add)))
    anyf = view(small + 240, 1)
    anyb = view(small + 241, 1)
    v.mark(V.tensor_reduce(anyf, B[:, 0:L], AX, ALU.min))
    m_any = v.mark(V.tensor_reduce(anyb, B[:, 1:L + 1], AX, ALU.min))
    FL = PA[:, :, 6]

    def put_flag(j, ps, mt):
        v.wait(mt)
        return v.mark(V.tensor_scalar(FL.rearrange("p (b j) -> p j b", j=SB)[:, j],
                                      ps.rearrange("p (b h) -> p b h", h=8)[:, :, 0],
                                      NEG / 2, None, ALU.is_lt))
    from_scan(B, m_any, put_flag)
    v.wait(bank_rd[0], bank_rd[1], bank_rd[2], bank_rd[3])

    p.wait((v.sem, v.n))
    P.transpose(bank[4][0:1, 0:128], anyf, ident)
    mp = p.mark(P.transpose(bank[4][0:1, 128:256], anyb, ident))
    v.wait(mp)
    v.mark(V.tensor_copy(rowA, bank[4][0:1, 0:128]))
    v.wait(v.mark(V.tensor_copy(rowAb, bank[4][0:1, 128:256])))


    for l in range(2):
        if l == 1:
            load_and_project(l)
        fence(v, s, p, g)
        g.wait(st_out[0], st_out[1])

        WV4 = [WV[:, j, :].rearrange("p (k f) -> p k f", k=4) for j in range(2)]

        def expand(i, d):
            ws = win(p, wd_i, i)
            d["ms"] = []
            d["bks"] = [2 + (4 * i + k) % 6 for k in range(4)]
            for k in range(4):
                bk = d["bks"][k]
                p.wait(d["moht"], bank_rd[bk])
                lhs = d["oht"][:, k * 128:(k + 1) * 128]
                P.matmul(bank[bk][:, 0:264], lhs, Q3[:, bass.ds(ws[k], 1), 0, :], start=True, stop=False)
                P.matmul(bank[bk][:, 0:264], lhs, Q3[:, bass.ds(ws[k], 1), 1, :], start=False, stop=False)
                d["ms"].append(p.mark(P.matmul(bank[bk][:, 0:264], lhs, QL[:, bass.ds(ws[k], 1), :],
                                               start=False, stop=True)))
            d["oht_read"] = [d["ms"][3]]

        def scores(i, d):
            tmp = WV4[i % 2]
            for k in range(4):
                bk = d["bks"][k]
                v.wait(d["ms"][k], d["g"][k])
                mv = v.mark(V.tensor_tensor(tmp[:, k, 0:256], d["rows"][:, k, :], bank[bk][:, 0:256], ALU.mult))
                s.wait(d["ms"][k], mv)
                bank_rd[bk] = s.mark(S.activation(SC[:, 4 * i + k, 8:16], bank[bk][:, 256:264], ACT.Copy))
            d["rows_read"] = [mv]
            v.wait(mv)
            v.mark(V.tensor_reduce(SC[:, 4 * i:4 * i + 4, 0:8],
                                   tmp[:, :, 0:256].rearrange("p k (h d) -> p k h d", d=32), AX, ALU.add))

        def both(i, d):
            expand(i, d)
            scores(i, d)
        edge_loop(KT, 256, isrc, locd, o_ring, 4, [both], 0, True)
        def weights():
            SP8 = view(o_q, SB, 16, 8)
            fence(v, s, p)
            mm = v.mark(V.tensor_tensor(SP8, blocked(SC[:, :, 0:8]), blocked(SC[:, :, 8:16]), ALU.max))
            SPs, FB, BB = view(o_acc, L), view(o_acc + L, L), view(o_q, L)
            mm = to_scan(view(o_q, L), SPs, mm)
            v.wait(*all_done(p))
            mm = segment_max(SPs, FB, BB, mm)

            def put_m(j, ps, mt):
                v.wait(mt)
                d = SC.rearrange("p (b j) k -> p j b k", j=SB)[:, j]
                pv = ps.rearrange("p (b h) -> p b h", h=8)
                v.mark(V.tensor_tensor(d[:, :, 0:8], d[:, :, 0:8], pv, ALU.subtract))
                return v.mark(V.tensor_tensor(d[:, :, 8:16], d[:, :, 8:16], pv, ALU.subtract))
            from_scan(FB, mm, put_m)
            s.wait(bank_rd[0], bank_rd[1], bank_rd[2], bank_rd[3])
            me = s.mark(S.activation(SC, SC, ACT.Exp))
            v.wait(me)
            v.mark(V.tensor_tensor(SC[:, :, 8:16], SC[:, :, 8:16], FL.unsqueeze(2).to_broadcast([128, T, 8]), ALU.mult))
            m_acc0 = v.mark(V.memset(ACC, 0.0))
            v.wait(m_acc0)
            fence(p, v, s)
        g.wait(*all_done(v, p))
        add = accumulate(272, wd_i)

        def weigh(i, d):
            j = i % 2
            w_ = WV4[j]
            v.wait(*d["g"], rdwv[j])
            s.wait(rdwv[j])
            mc = s.mark(S.activation(w_[:, :, 256:272], SC[:, 4 * i:4 * i + 4, :], ACT.Copy))
            mw = v.mark(V.tensor_tensor(w_[:, :, 0:256].rearrange("p k (h d) -> p k h d", d=32),
                                        d["rows"].rearrange("p k (h d) -> p k h d", d=32),
                                        SC[:, 4 * i:4 * i + 4, 0:8].unsqueeze(3).to_broadcast([128, 4, 8, 32]), ALU.mult))
            d["rows_read"] = [mw]
            p.wait(mw, mc, d["moh"])
            d["ms"] = []
            d["bks"] = [4 * (i % 2) + k for k in range(4)]
            for k in range(4):
                bk = d["bks"][k]
                p.wait(bank_rd[bk])
                d["ms"].append(p.mark(P.matmul(bank[bk][:, 0:272], d["oh"][:, k * 128:(k + 1) * 128], w_[:, k, :],
                                               start=True, stop=True)))
            rdwv[j] = d["ms"][3]
            d["oh_read"] = [rdwv[j]]
        rdwv = [None, None]
        edge_loop(VT, 256, isrc, locd, o_ring, 4, [weigh, add], 0, False, between=weights)

        g.wait(m_poss, m_zs)
        marks3 = scatter(tg3, R2, lambda c: code[:, c:c + 2], poss, (range(0, 240), range(240, C))[l])

        fence(v, s, p, y)
        VB = view(o_q, 4, 256)
        vb_s = [Slot(nc, f"vb{l}{k}") for k in range(4)]
        AG = XN
        lv = {}

        def ldv(w):
            if w >= 4:
                y.wait(cons[w - 4])
            lv[w] = vb_s[w % 4].mark(SY.dma_start(VB[:, w % 4, :], VT[w * 128:(w + 1) * 128, :]))
        cons = {}
        ldv(0)
        ldv(1)
        ldv(2)
        mts = {}
        cp = [None] * W
        hd = "p (h d) -> p h d"
        RZ = view(o_q + 1024, W, 8)
        v.wait(v.mark(V.tensor_tensor(RZ, ACC[:, :, 256:264], ACC[:, :, 264:272], ALU.add)))
        v.wait(v.mark(V.tensor_scalar(RZ, RZ, 1e-30, None, ALU.max)))
        v.wait(v.mark(V.reciprocal(RZ, RZ)))
        v.wait(v.mark(V.tensor_tensor(H, H, bo.unsqueeze(1).to_broadcast([128, W, 256]), ALU.add)))

        def aggregate(w):
            if w + 3 < W:
                ldv(w + 3)
            v.wait(lv[w])
            if w >= 2:
                v.wait(mts[w - 2])
            ag = AG[:, w % 2, :]
            cons[w] = v.mark(V.tensor_tensor(ag.rearrange(hd, d=32), VB[:, w % 4, :].rearrange(hd, d=32),
                                             ACC[:, w, 264:272].unsqueeze(2).to_broadcast([128, 8, 32]), ALU.mult))
            v.wait(cons[w])
            v.wait(v.mark(V.tensor_tensor(ag, ag, ACC[:, w, 0:256], ALU.add)))
            return v.mark(V.tensor_tensor(ag.rearrange(hd, d=32), ag.rearrange(hd, d=32),
                                          RZ[:, w, :].unsqueeze(2).to_broadcast([128, 8, 32]), ALU.mult))
        am = {0: aggregate(0)}
        done = [None] * W
        for w in range(W + 1):
            if w >= 1:
                u = w - 1
                p.wait(cp[u], bank_rd[2 + u % 2])
                done[u] = p.mark(proj(XT[:, u % 2, :], wo, 256, 2 + u % 2))
            if w < W:
                p.wait(am[w], bank_rd[w % 2])
                for k in range(2):
                    mm = P.transpose(bank[w % 2][:, k * 128:(k + 1) * 128], AG[:, w % 2, k * 128:(k + 1) * 128], ident)
                mts[w] = p.mark(mm)
                s.wait(mts[w])
                if w >= 2:
                    s.wait(done[w - 2])
                cp[w] = bank_rd[w % 2] = s.mark(S.activation(XT[:, w % 2, 0:256], bank[w % 2][:, 0:256], ACT.Copy))
            if w + 1 < W:
                am[w + 1] = aggregate(w + 1)
            if w >= 1:
                v.wait(done[u])
                bank_rd[2 + u % 2] = v.mark(V.tensor_tensor(H[:, u, :], H[:, u, :], bank[2 + u % 2][:, 0:256], ALU.add))
        v.wait((v.sem, v.n))
        fence(y, v, s, p)
        m_w1 = load_w(w1, kview(a["L0_gnn_w1"][l]))
        if l:
            XX = view(o_S, W, 256)
            mx = load_x(XX, y)
        ln_stats(H)
        p.wait(m_w1)
        XT4 = view(o_acc, 2, 2, 512)
        HT = view(o_acc + 2048, 8, 512)
        XN8 = view(o_q, 8, 256)
        ht_rd = None
        xn_rd = {}

        def prepare(gr):
            for w in range(gr * 4, min(gr * 4 + 4, W)):
                if w >= 8:
                    v.wait(xn_rd[w - 8])
                m = v.mark(normed(XN8[:, w % 8, :], H[:, w, :], w))
                bk = w % 2
                p.wait(m, bank_rd[bk])
                for k in range(2):
                    mm = P.transpose(bank[bk][:, k * 128:(k + 1) * 128], XN8[:, w % 8, k * 128:(k + 1) * 128], ident)
                xn_rd[w] = p.mark(mm)
                s.wait(xn_rd[w])
                for k in range(2):
                    mc = s.mark(S.activation(XT4[:, gr % 2, k, (w % 4) * 128:(w % 4) * 128 + 128],
                                             bank[bk][:, k * 128:(k + 1) * 128], ACT.Identity,
                                             scale=gb[:, 2, k:k + 1], bias=gb[:, 3, k:k + 1]))
                bank_rd[bk] = mc
            v.wait(m)
            n_ = min(4, W - gr * 4)
            hb[gr] = v.mark(V.tensor_tensor(H[:, gr * 4:gr * 4 + n_, :], H[:, gr * 4:gr * 4 + n_, :],
                                            b2.unsqueeze(1).to_broadcast([128, n_, 256]), ALU.add))
            return mc
        hb = {}
        ready = prepare(0)
        for gr in range(7):
            ws_ = list(range(gr * 4, min(gr * 4 + 4, W)))
            n = len(ws_) * 128
            p.wait(ready)
            mh = []
            for j in range(8):
                bk = 2 + j % 4
                p.wait(bank_rd[bk])
                for k in range(2):
                    mm = P.matmul(bank[bk][:, 0:n], w1[:, k, j * 128:(j + 1) * 128], XT4[:, gr % 2, k, 0:n],
                                  start=(k == 0), stop=(k == 1))
                s.wait(p.mark(mm), ht_rd)
                mc = s.mark(S.activation(HT[:, j, 0:n], bank[bk][:, 0:n], ACT.Gelu, bias=b1c[:, j:j + 1]))
                bank_rd[bk] = mc
                mh.append(mc)
            if gr < 6:
                ready = prepare(gr + 1)
            for w in ws_:
                bk = 6 + w % 2
                p.wait(bank_rd[bk])
                for j in range(8):
                    p.wait(mh[j])
                    mm = P.matmul(bank[bk][:, 0:256], HT[:, j, (w % 4) * 128:(w % 4) * 128 + 128], w2[:, j, :],
                                  start=(j == 0), stop=(j == 7))
                ht_rd = p.mark(mm)
                v.wait(ht_rd, hb[gr])
                bank_rd[bk] = v.mark(V.tensor_tensor(H[:, w, :], H[:, w, :], bank[bk][:, 0:256], ALU.add))
        v.wait((v.sem, v.n))

    def norm_windows(X, w0, w1_, marks):
        for w in range(w0, w1_):
            m = v.mark(V.bn_stats(ST[:, 6 * w:6 * w + 6], X[:, w, :]))
        yield
        v.wait(m)
        for w in range(w0, w1_):
            m = v.mark(V.bn_aggr(MS[:, 2 * w:2 * w + 2], ST[:, 6 * w:6 * w + 6]))
        s.wait(m)
        ms = s.mark(S.activation(RS[:, w0:w1_], MS.rearrange("p (w k) -> p w k", k=2)[:, w0:w1_, 1], ACT.Sqrt, bias=EP))
        v.wait(m, ms)
        v.wait(v.mark(V.reciprocal(RS[:, w0:w1_], RS[:, w0:w1_])))
        yield
        for w in range(w0, w1_):
            marks[w] = v.mark(normed(X[:, w, :], X[:, w, :], w))

    def ahead(X, make):
        marks = {}
        parts = [make(w0, w0 + 5, marks) for w0 in range(0, W, 5)]

        def get(w):
            if w == 0:
                for _ in parts[0]:
                    pass
            if w // 5 + 1 < len(parts):
                n_ = 99 if w % 5 == 4 else 1
                for _ in range(n_):
                    if next(parts[w // 5 + 1], 1):
                        break
            return X[:, w, :], marks[w]
        return get

    v.wait(mx)

    def end0(w0, w1_, marks):
        v.wait(v.mark(V.tensor_tensor(H[:, w0:w1_], H[:, w0:w1_], XX[:, w0:w1_], ALU.add)))
        yield from norm_windows(H, w0, w1_, marks)
    get0 = ahead(H, end0)

    def dump(ap, m):
        dd = Slot(nc, "dbgx")
        y.wait(*all_done(v, s, p), m)
        y.wait(dd.mark(SY.dma_start(dbg["H"].rearrange("(w p) f -> p w f", p=128), ap)))
    if dbg is not None and stop == 1:
        dump(H, None)
        return

    fence(y, s, p, v)
    T2 = view(o_q + 3328, T, 2)
    reload(tg3, T, 0, 2 * T, T2.rearrange("p c k -> p (c k)"), marks3, o_q)
    wsf = view(o_q + 4200, T)
    ti = view(o_q + 4700, T).bitcast(I)
    tv = view(o_q + 5200, T)
    step(lambda: V.tensor_scalar(tv, T2[:, :, 0], -1.0, 0.0, ALU.add, ALU.max))
    step(lambda: V.tensor_copy(ti, tv))
    step(lambda: V.tensor_scalar(idst, ti, 4095, None, ALU.bitwise_and))
    step(lambda: V.tensor_scalar(ti, ti, 12, None, ALU.logical_shift_right))
    step(lambda: V.tensor_copy(tv, ti))
    step(lambda: V.tensor_scalar(wsf, T2[:, :, 0], 1.0, PADKEY, ALU.is_lt, ALU.mult))
    step(lambda: V.tensor_tensor(PB[:, :, 1], tv, wsf, ALU.add))
    W1_ = WM[:, 0:128].rearrange("p (k n) -> p k n", k=2)
    wlr = WM[:, 128:136]
    b_1 = WM[:, 144:208]
    load_w(W1_, kview(a["L1_gnn_W"]))
    with nc.allow_non_contiguous_dma(reason="small transposed weights"):
        load_w(wlr[0:64, 0:4], a["L1_gnn_Wl"].rearrange("h o -> o h"))
        load_w(wlr[0:64, 4:8], a["L1_gnn_Wr"].rearrange("h o -> o h"))
    m_w = load_w(b_1, rows_bc(a["L1_gnn_b"], 64))
    p.wait(m_w)
    v.wait(m_w)
    EL = view(o_q, W, 4)
    X1 = view(o_q + 128, 4, 72)
    X1c = view(o_q + 512, 4, 128)
    mz = v.mark(V.memset(X1, 0.0))
    st4 = [Slot(nc, f"x1s{k}") for k in range(4)]
    st_m = [None] * 4
    m_h = (v.sem, v.n)
    x1t_rd = {}

    def aft(w, xt, m):
        p.wait(m, bank_rd[2 + w % 2])
        bkk = bank[2 + w % 2]
        proj(xt, W1_, 64, 2 + w % 2)
        for k in range(2):
            mm = P.matmul(bkk[0:64, 128:256], W1_[:, k, :], xt[:, k * 128:(k + 1) * 128], start=(k == 0), stop=(k == 1))
        mm = p.mark(mm)
        s.wait(mm)
        if w >= 4:
            s.wait(x1t_rd[w - 4])
        mc = s.mark(S.activation(X1c[0:64, w % 4, :], bkk[0:64, 128:256], ACT.Copy))
        p.wait(mc, bank_rd[4 + w % 2])
        x1t_rd[w] = p.mark(P.matmul(bank[4 + w % 2][:, 0:8], X1c[0:64, w % 4, :], wlr[0:64, :], start=True, stop=True))
        v.wait(mz, st_m[w % 4], x1t_rd[w])
        bank_rd[2 + w % 2] = v.mark(V.tensor_copy(X1[:, w % 4, 0:64], bkk[:, 0:64]))
        v.mark(V.tensor_copy(X1[:, w % 4, 64:68], bank[4 + w % 2][:, 4:8]))
        bank_rd[4 + w % 2] = v.mark(V.tensor_copy(EL[:, w, :], bank[4 + w % 2][:, 0:4]))
        y.wait(bank_rd[4 + w % 2])
        st_m[w % 4] = st4[w % 4].mark(SY.dma_start(X1T[w * 128:(w + 1) * 128, :], X1[:, w % 4, :]))
        return mm
    transposed(W, get0, aft)
    v.wait(v.mark(V.memset(ACC, 0.0)))
    fence(p, s, v, g)
    g.wait(*st_m)
    locs = PB[:, :, 1]
    E4 = view(o_q + 1100, 3, 16)
    Z4 = view(o_q + 1160, 3, 16)
    EL3 = view(o_q + 1220, W, 6).bitcast(BF).rearrange("p w (c h) -> p w c h", c=3)
    v.wait((v.sem, v.n))
    v.wait(v.mark(V.tensor_copy(EL3[:, :, 0, :], EL)))
    v.wait(v.mark(V.tensor_tensor(EL, EL, EL3[:, :, 0, :], ALU.subtract)))
    v.wait(v.mark(V.tensor_copy(EL3[:, :, 1, :], EL)))
    v.wait(v.mark(V.tensor_tensor(EL3[:, :, 2, :], EL, EL3[:, :, 1, :], ALU.subtract)))
    p.wait((v.sem, v.n))
    add = accumulate(260, ws_i)
    rdwv = [None, None]
    rde = [None, None, None]
    rdc = [None, None, None]

    def logits(i, d):
        j = i % 2
        ws = win(p, ws_i, i)
        p.wait(d["moht"], bank_rd[2 + j])
        for k in range(4):
            mm = P.matmul(bank[2 + j][:, 12 * k:12 * k + 12], d["oht"][:, k * 128:(k + 1) * 128],
                          EL3[:, bass.ds(ws[k], 1), :, :], start=True, stop=True)
        mel = p.mark(mm)
        d["oht_read"] = [mel]

    def logits_edge(i, d):
        j = i % 2
        mel = d["oht_read"][0]
        j3 = i % 3
        v.wait(mel, *d["g"], rde[j3])
        z, e = Z4[:, j3, :], E4[:, j3, :]
        z3 = z.rearrange("p (k h) -> p k h", h=4)
        bank_rd[2 + j] = m = v.mark(V.tensor_reduce(
            z3, bank[2 + j][:, 0:48].rearrange("p (k c h) -> p k h c", k=4, c=3), AX, ALU.add))
        v.wait(m)
        m = v.mark(V.tensor_tensor(z3, z3, d["rows"][:, :, 64:68], ALU.add))
        v.wait(m)
        m = v.mark(V.scalar_tensor_tensor(z, z, 0.2, z, ALU.mult, ALU.max))
        s.wait(m, rde[j3], rdc[j3])
        d["me"] = s.mark(S.activation(e, z, ACT.Exp))

    def weigh1(i, d):
        j = i % 2
        e = E4[:, i % 3, :]
        w_ = WV[:, j, :].rearrange("p (k f) -> p k f", k=4)
        v.wait(d["me"], rdwv[j])
        s.wait(rdwv[j], d["me"])
        mc = s.mark(S.activation(w_[:, :, 256:260], e.rearrange("p (k h) -> p k h", h=4), ACT.Copy))
        for k in range(4):
            mw = v.mark(V.tensor_tensor(w_[:, k, 0:256].rearrange("p (h d) -> p h d", h=4),
                                        d["rows"][:, k, 0:64].unsqueeze(1).to_broadcast([128, 4, 64]),
                                        e[:, 4 * k:4 * k + 4].unsqueeze(2).to_broadcast([128, 4, 64]), ALU.mult))
        d["rows_read"] = [mw]
        rde[i % 3], rdc[i % 3] = mw, mc
        d["mw"] = [mw, mc]

    def gather1(i, d):
        p.wait(*d["mw"], d["moh"])
        d["ms"] = []
        d["bks"] = [4, 5, 6, 7]
        j = i % 2
        w_ = WV[:, j, :].rearrange("p (k f) -> p k f", k=4)
        for k in range(4):
            p.wait(bank_rd[4 + k])
            d["ms"].append(p.mark(P.matmul(bank[4 + k][:, 0:260], d["oh"][:, k * 128:(k + 1) * 128], w_[:, k, 0:260],
                                           start=True, stop=True)))
        rdwv[j] = d["ms"][3]
        d["oh_read"] = [rdwv[j]]

    d1 = {}

    def add_gather(i, d):
        if i:
            add(i - 1, d1[i - 1])
        d1[i] = d
        gather1(i, d)
    edge_loop(X1T, 72, idst, locs, o_ring, 6, [logits, logits_edge, weigh1, add_gather], 2, "both",
              oh_at=o_q + 2048)
    add(G - 1, d1[G - 1])
    fence(v, s)
    RS1 = ACC[:, :, 256:260]
    v.wait(v.mark(V.tensor_scalar(RS1, RS1, 1e-12, None, ALU.max)))
    v.wait(v.mark(V.reciprocal(RS1, RS1)))
    TA = view(o_S, 2, 5, 256)
    b1_1 = view(o_sm + 256, 64)
    v.wait(v.mark(V.tensor_copy(b1_1, b_1)))

    def end1(w0, w1_, marks):
        t = TA[:, (w0 // 5) % 2]
        av = ACC[:, w0:w1_, 0:256]
        for h in range(4):
            m = v.mark(V.tensor_tensor(av[:, :, h * 64:(h + 1) * 64], av[:, :, h * 64:(h + 1) * 64],
                                       RS1[:, w0:w1_, h:h + 1].to_broadcast([128, 5, 64]), ALU.mult))
        v.wait(m)
        for h in range(4):
            m = v.mark(V.tensor_tensor(av[:, :, h * 64:(h + 1) * 64], av[:, :, h * 64:(h + 1) * 64],
                                       b1_1.unsqueeze(1).to_broadcast([128, 5, 64]), ALU.add))
        v.wait(m)
        yield
        m = v.mark(V.tensor_scalar(t, av, 0.0, None, ALU.min))
        s.wait(m)
        me = s.mark(S.activation(t, t, ACT.Exp))
        v.mark(V.scalar_tensor_tensor(H[:, w0:w1_], av, 0.0, H[:, w0:w1_], ALU.max, ALU.add))
        yield
        v.wait(me, (v.sem, v.n))
        v.wait(v.mark(V.scalar_tensor_tensor(H[:, w0:w1_], t, -1.0, H[:, w0:w1_], ALU.add, ALU.add)))
        yield from norm_windows(H, w0, w1_, marks)
    get1 = ahead(H, end1)
    if dbg is not None and stop == 2:
        dump(H, None)
        return

    fence(y, s, p, v)
    WA = WM[:, 0:512].rearrange("p (k n) -> p k n", k=2)
    WB = WM[:, 512:1024].rearrange("p (k n) -> p k n", k=2)
    b1_, b2_ = WM[:, 1024:1280], WM[:, 1280:1536]
    load_w(WA, kview(a["L2_gnn_W1"]))
    load_w(WB, kview(a["L2_gnn_W2"]))
    load_w(b1_, rows_bc(a["L2_gnn_b1"], 256))
    m_w = load_w(b2_, rows_bc(a["L2_gnn_b2"], 256))
    p.wait(m_w)
    v.wait(m_w)
    ST8 = view(o_q, 8, 260)
    sts = [Slot(nc, f"st{k}") for k in range(8)]
    st_m = [None] * 8
    HX = view(o_S, W, 256)

    def to_table(dst, get, wt):
        v.wait(*st_m)
        mst = v.mark(V.memset(ST8, 1.0))
        v.wait(mst)

        def aft(w, xt, m):
            p.wait(m, bank_rd[2 + w % 2])
            mm = p.mark(proj(xt, wt, 256, 2 + w % 2))
            s.wait(mm, mst, st_m[w % 8])
            bank_rd[2 + w % 2] = s.mark(S.activation(ST8[:, w % 8, 0:256], bank[2 + w % 2][:, 0:256], ACT.Copy))
            y.wait(bank_rd[2 + w % 2])
            st_m[w % 8] = sts[w % 8].mark(SY.dma_start(dst[w * 128:(w + 1) * 128, :], ST8[:, w % 8, :]))
            return mm
        transposed(W, get, aft)

    def hop(table, idx, loc, wi, last=False):
        v.wait((v.sem, v.n) if last else v.mark(V.memset(ACC, 0.0)))
        fence(p, s, v, g)
        g.wait(*st_m)
        add = accumulate(257, wi)

        def body(i, d):
            d["ms"] = []
            d["bks"] = [4 * (i % 2) + k for k in range(4)]
            p.wait(d["moh"])
            for k in range(4):
                bk = d["bks"][k]
                p.wait(bank_rd[bk], d["g"][k])
                d["ms"].append(p.mark(P.matmul(bank[bk][:, 0:257], d["oh"][:, k * 128:(k + 1) * 128],
                                               d["rows"][:, k, 0:257], start=True, stop=True)))
            d["rows_read"] = d["oh_read"] = [d["ms"][3]]
        edge_loop(table, 260, idx, loc, o_ring, 4, [body, add], 0, False)
        v.wait((v.sem, v.n))
        v.wait(v.mark(V.tensor_scalar(ACC[:, :, 256:257], ACC[:, :, 256:257], 1.0, None, ALU.max)))
        v.wait(v.mark(V.reciprocal(ACC[:, :, 256:257], ACC[:, :, 256:257])))

    def average(w0, w1_):
        v.wait(v.mark(V.tensor_tensor(ACC[:, w0:w1_, 0:256], ACC[:, w0:w1_, 0:256],
                                      ACC[:, w0:w1_, 256:257].to_broadcast([128, w1_ - w0, 256]), ALU.mult)))

    def prelu(dst, src, tmp):
        v.wait(v.mark(V.tensor_scalar(tmp, src, 0.0, a_bc, ALU.min, ALU.mult)))
        v.wait(v.mark(V.scalar_tensor_tensor(dst, src, 0.0, tmp, ALU.max, ALU.add)))

    gets = [get1, None]
    for r in range(2):
        to_table(MT[2 * r], gets[r], WA if r == 0 else WB)
        hop(MT[2 * r], isrc, locd, wd_i)
        mt = MT[2 * r + 1].rearrange("(w p) f -> p w f", p=128)
        for k in range(5):
            cw = slice(5 * k, 5 * k + 5)
            average(5 * k, 5 * k + 5)
            y.wait(v.mark(V.memset(ACC[:, cw, 256:260], 1.0)))
            st_m[k] = sts[k].mark(SY.dma_start(mt[:, cw, :], ACC[:, cw, 0:260]))
        for k in range(5):
            v.wait(st_m[k])
            v.mark(V.memset(ACC[:, 5 * k:5 * k + 5, :], 0.0))
        hop(MT[2 * r + 1], idst, locs, ws_i, last=True)
        PT = view(o_q + 2080, 2, 5, 256)

        def end2(w0, w1_, marks, r=r):
            hx = HX[:, w0:w1_]
            average(w0, w1_)
            v.wait(v.mark(V.tensor_tensor(hx, ACC[:, w0:w1_, 0:256],
                                          (b1_, b2_)[r].unsqueeze(1).to_broadcast([128, 5, 256]), ALU.add)))
            if r == 1:
                v.wait(v.mark(V.tensor_tensor(hx, hx, H[:, w0:w1_], ALU.add)))
            yield
            prelu(hx, hx, PT[:, (w0 // 5) % 2])
            if r == 0:
                for w in range(w0, w1_):
                    marks[w] = (v.sem, v.n)
            else:
                v.wait(v.mark(V.tensor_tensor(H[:, w0:w1_], H[:, w0:w1_], hx, ALU.add)))
                yield from norm_windows(H, w0, w1_, marks)
        gets[1] = ahead(HX if r == 0 else H, end2)
    get3 = gets[1]
    if dbg is not None and stop == 3:
        dump(H, None)
        return

    fence(y, s, p, v)
    W0 = WM[:, 0:128]
    W1c = WM[:, 128:256]
    load_w(W0[0:64, 0:64], a["L3_gnn_w_00_0"])
    load_w(W0[0:64, 64:128], a["L3_gnn_w_01_1"])
    load_w(W1c[0:64, 0:64], a["L3_gnn_w_10_1"])
    m_w = load_w(W1c[0:64, 64:128], a["L3_gnn_w_11_0"])
    v.wait(m_w)
    mw3 = v.mark(V.tensor_scalar(W1c[0:64, 64:128], W1c[0:64, 64:128], float(1.0 / np.sqrt(3.0)), None, ALU.mult))
    p.wait(m_w, mw3)
    XT3 = view(o_ring, 2, 512)
    YB = view(o_q, 4, 512)
    y_m = [None] * 4
    yss = [Slot(nc, f"ys{k}") for k in range(4)]
    x_rd = {}
    cp = {}
    for w in range(W + 1):
        if w < W:
            p.wait(get3(w)[1], bank_rd[w % 2])
            for k in range(4):
                src = H[:, w, 0:64] if k == 0 else H[:, w, 64:256].rearrange("p (i m) -> p m i", m=3)[:, k - 1]
                mm = P.transpose(bank[w % 2][0:64, k * 128:(k + 1) * 128], src, ident)
            s.wait(p.mark(mm), x_rd.get(w - 2))
            cp[w] = bank_rd[w % 2] = s.mark(S.activation(XT3[0:64, w % 2, :], bank[w % 2][0:64, :], ACT.Copy))
        if w >= 1:
            u = w - 1
            bk = 2 + u % 2
            p.wait(cp[u], bank_rd[bk])
            for k in range(4):
                mm = P.matmul(bank[bk][:, k * 128:(k + 1) * 128], XT3[0:64, u % 2, k * 128:(k + 1) * 128],
                              (W0 if k == 0 else W1c)[0:64, :], start=True, stop=True)
            x_rd[u] = p.mark(mm)
            s.wait(x_rd[u], y_m[u % 4])
            bank_rd[bk] = s.mark(S.activation(YB[:, u % 4, :], bank[bk][:, :], ACT.Copy))
            y.wait(bank_rd[bk])
            y_m[u % 4] = yss[u % 4].mark(SY.dma_start(YT[u * 128:(u + 1) * 128, :], YB[:, u % 4, :]))
    v.wait(v.mark(V.memset(ACC, 0.0)))
    fence(p, s, v, g)
    g.wait(*y_m)
    add = accumulate(256, wd_i)
    MSG = view(o_S, 2, 4, 256)
    T1 = view(o_S + 2048, 2, 4, 192)
    T2 = view(o_S + 3584, 2, 4, 192)
    T3 = view(o_S + 5120, 2, 4, 64)
    rdm = [None, None]

    def tp(i, d):
        j = i % 2
        rows, oh = d["rows"], d["oh"]
        v.wait(*d["g"], rdm[j])
        s.wait(*d["g"], rdm[j])
        r = rows.rearrange("p k (m t o) -> p k m t o", m=4, t=2)
        cc = PA[:, 4 * i:4 * i + 4, 2:6]
        for k in range(4):
            ma = s.mark(S.activation(MSG[:, j, k, :].rearrange("p (m o) -> p m o", m=4), r[:, k, :, 0, :], ACT.Copy,
                                     scale=cc[:, k, 0:1]))
        for k in (2, 3):
            for m_ in range(3):
                ma = s.mark(S.activation(T1[:, j, k, m_ * 64:(m_ + 1) * 64], r[:, k, 0, 1, :], ACT.Copy,
                                         scale=cc[:, k, 1 + m_:2 + m_]))
        m2 = v.mark(V.tensor_tensor(T2[:, j].rearrange("p k (m o) -> p k m o", m=3), r[:, :, 1:4, 1, :],
                                    cc[:, :, 1:4].unsqueeze(3).to_broadcast([128, 4, 3, 64]), ALU.mult))
        mv = v.mark(V.tensor_tensor(T1[:, j, 0:2].rearrange("p k (m o) -> p k m o", m=3),
                                    r[:, 0:2, 0, 1, :].unsqueeze(2).to_broadcast([128, 2, 3, 64]),
                                    cc[:, 0:2, 1:4].unsqueeze(3).to_broadcast([128, 2, 3, 64]), ALU.mult))
        v.wait(m2)
        ms2 = v.mark(V.tensor_reduce(T3[:, j], T2[:, j].rearrange("p k (m o) -> p k o m", m=3), AX, ALU.add))
        p.wait(ma, mv, ms2, d["moh"])
        ms = []
        bks = [4 * (i % 2) + k for k in range(4)]
        for k in range(4):
            p.wait(bank_rd[bks[k]])
            o_ = oh[:, k * 128:(k + 1) * 128]
            P.matmul(bank[bks[k]][:, 0:256], o_, MSG[:, j, k, :], start=True, stop=False, skip_group_check=True)
            P.matmul(bank[bks[k]][:, 64:256], o_, T1[:, j, k, :], start=False, stop=False, skip_group_check=True)
            ms.append(p.mark(P.matmul(bank[bks[k]][:, 0:64], o_, T3[:, j, k, :], start=False, stop=True,
                                      skip_group_check=True)))
        rdm[j] = ms[3]
        d["ms"], d["bks"] = ms, bks
        d["rows_read"], d["oh_read"] = [ma, mv], [ms[3]]
    edge_loop(YT, 512, isrc, locd, o_q, 3, [tp, add], 0, False)
    v.wait((v.sem, v.n))
    fin = Slot(nc, "fin")
    marks = {}
    for w0 in range(0, W, 5):
        w1_ = w0 + 5
        v.mark(V.tensor_tensor(H[:, w0:w1_, 0:64], H[:, w0:w1_, 0:64], ACC[:, w0:w1_, 0:64], ALU.add))
        hv = H[:, w0:w1_, 64:256].rearrange("p w (o m) -> p w o m", m=3)
        v.mark(V.tensor_tensor(hv, hv, ACC[:, w0:w1_, 64:256].rearrange("p w (m o) -> p w o m", m=3), ALU.add))
        v.wait((v.sem, v.n))
        for _ in norm_windows(H, w0, w1_, marks):
            pass
        y.wait(marks[w1_ - 1])
        n_ = min(w1_, 24)
        m = fin.mark(SY.dma_start(out[w0 * 128:n_ * 128, :].rearrange("(w p) f -> p w f", p=128), H[:, w0:n_, :]))
    m = fin.mark(SY.dma_start(out[3072:NN, :], H[0:NN - 3072, 24, :]))
    y.wait(m)


def paired(x):
    x = np.concatenate([x, np.zeros((128 * C - NE, 10), x.dtype)]).reshape(128, C, 10)
    x = np.concatenate([x, np.zeros((128, 1, 10), x.dtype)], 1).reshape(128, (C + 1) // 2, 2, 10)
    return np.ascontiguousarray(x.transpose(2, 3, 1, 0).reshape(20, (C + 1) // 2 * 128))


def kernel(**inputs):
    import concourse.bacc as bacc
    from concourse.bass_utils import run_bass_kernel_spmd

    nc = bacc.Bacc("TRN2", target_bir_lowering=False, num_devices=1)
    arrays, aps = {}, {}
    for name, val in inputs.items():
        x = np.ascontiguousarray(val)
        if name == "edge_attr_10":
            name = "embT"
            x = paired(x)
        arrays["in_" + name] = x
        aps[name] = nc.dram_tensor("in_" + name, x.shape, mybir.dt.from_np(x.dtype), kind="ExternalInput").ap()
    out = nc.dram_tensor("out_0", [NN, 256], F, kind="ExternalOutput").ap()
    program(nc, aps, out)
    r = run_bass_kernel_spmd(nc, [arrays], core_ids=[0])
    return r.results[0]["out_0"]
```
